# Optimizing a Trainium2 kernel written in Bass

```python
import numpy as np
import jax
import jax.numpy as jnp

def _softmax(x, axis=-1):
    return jax.nn.softmax(x, axis=axis)

def _gelu(x):
    return jax.nn.gelu(x, approximate=True)

def _silu(x):
    return jax.nn.silu(x)

def _sigmoid(x):
    return jax.nn.sigmoid(x)

def _layernorm(x, axis=-1, eps=1e-05):
    m = jnp.mean(x, axis=axis, keepdims=True)
    v = jnp.var(x, axis=axis, keepdims=True)
    return (x - m) / jnp.sqrt(v + eps)

def _scatter_add(tgt, idx, src, axis=0):
    return tgt.at[idx].add(src)

def _segment_sum(src, seg, n):
    return jax.ops.segment_sum(src, seg, n)
kernel_name = 'mk_gps_d1_gnn_r32_48c606'

def setup_inputs(seed: int=0):
    np.random.seed(seed)
    _w = jnp.asarray

    def _rec_inputs():
        import jax
        import jax.numpy as jnp
        _gk = jax.random.key(seed)
        x = -0.0003713 + 1 * jax.random.normal(jax.random.fold_in(_gk, 1), (3125, 256), jnp.float32)
        src = jax.random.randint(jax.random.fold_in(_gk, 2), (50000,), 0, 3125, jnp.int32)
        dst = jax.random.randint(jax.random.fold_in(_gk, 3), (50000,), 0, 3125, jnp.int32)
        _o = jnp.argsort(dst, stable=True)
        src = src[_o]
        dst = dst[_o]
        return (x, src, dst)
    x, src, dst = _rec_inputs()

    def _L0_gnn_setup():
        import jax, jax.numpy as jnp
        import numpy as np
        N = 50000
        E = 25000
        F_IN = 256
        K = 8
        F_OUT = 32
        NEG_SLOPE = 0.2
        key = jax.random.key(seed)
        k1, k2, k3, k4, k5, k6 = jax.random.split(key, 6)
        x = jax.random.normal(k1, (N, F_IN), dtype=jnp.float32)
        edge_index = jax.random.randint(k2, (2, E), 0, N, dtype=jnp.int64)
        W = jax.random.normal(k3, (F_IN, K * F_OUT), dtype=jnp.float32) * (2.0 / (F_IN + K * F_OUT)) ** 0.5
        b = jax.random.uniform(k4, (K * F_OUT,), dtype=jnp.float32)
        a_src = jax.random.normal(k5, (1, K, F_OUT), dtype=jnp.float32) * (2.0 / (K * F_OUT + 1)) ** 0.5
        a_trg = jax.random.normal(k6, (1, K, F_OUT), dtype=jnp.float32) * (2.0 / (K * F_OUT + 1)) ** 0.5
        return {'x': x, 'edge_index': edge_index, 'W': W, 'b': b, 'a_src': a_src, 'a_trg': a_trg}
    _L0_gnn_all = _L0_gnn_setup()
    _L0_gnn_in = {k: v for k, v in _L0_gnn_all.items() if k in ('W', 'b', 'a_src', 'a_trg')}
    del _L0_gnn_all

    def _L0_mix_setup():
        import jax, jax.numpy as jnp
        import numpy as np
        C_CURV = 1.0
        MIN_NORM = 1e-15
        BALL_EPS = 1e-05
        ATT_EPS = 1e-15
        DIM = 32

        def _norm(x):
            return jnp.clip(jnp.linalg.norm(x, axis=-1, keepdims=True), MIN_NORM)

        def proj(x, c):
            maxnorm = (1.0 - BALL_EPS) / jnp.sqrt(c)
            n = _norm(x)
            return jnp.where(n > maxnorm, x / n * maxnorm, x)

        def expmap0(u, c):
            sc = jnp.sqrt(c)
            n = _norm(u)
            return jnp.tanh(sc * n) * u / (sc * n)

        def logmap0(p, c):
            sc = jnp.sqrt(c)
            n = _norm(p)
            return jnp.arctanh(jnp.clip(sc * n, -1.0 + 1e-07, 1.0 - 1e-07)) * p / (sc * n)

        def mobius_add(x, y, c):
            x2 = jnp.sum(x * x, -1, keepdims=True)
            y2 = jnp.sum(y * y, -1, keepdims=True)
            xy = jnp.sum(x * y, -1, keepdims=True)
            num = (1 + 2 * c * xy + c * y2) * x + (1 - c * x2) * y
            den = 1 + 2 * c * xy + c * c * x2 * y2
            return num / jnp.clip(den, MIN_NORM)

        def conv1d(x, w, pad, groups=1):
            return jax.lax.conv_general_dilated(x, w, (1,), [(pad, pad)], dimension_numbers=('NCH', 'OIH', 'NCH'), feature_group_count=groups)

        def batchnorm(x, gamma, beta):
            mean = jnp.mean(x, axis=(0, 2), keepdims=True)
            var = jnp.var(x, axis=(0, 2), keepdims=True)
            xn = (x - mean) * jax.lax.rsqrt(var + 1e-05)
            return gamma[None, :, None] * xn + beta[None, :, None]

        def _reference_tuple_inner(x, w_qkv, bn_gamma, bn_beta, w_dw, w_pw, w_res, b_res):
            c = C_CURV
            h = logmap0(proj(x, c), c)
            h = jnp.transpose(h, (1, 2, 0))
            h = conv1d(h, w_qkv, pad=2)
            h = batchnorm(h, bn_gamma, bn_beta)
            h = jax.nn.relu(jnp.transpose(h, (2, 0, 1)))
            qkv = proj(expmap0(h, c), c)
            t = jnp.transpose(logmap0(proj(qkv, c), c), (1, 2, 0))
            s = conv1d(t, w_dw, pad=2, groups=t.shape[1])
            s = conv1d(s, w_pw, pad=0, groups=t.shape[1] // DIM)
            cat = jnp.concatenate([t, s], axis=1)
            ai = proj(expmap0(jnp.transpose(cat, (2, 0, 1)), c), c)
            t2 = logmap0(proj(ai, c), c)
            L, N, C2 = t2.shape
            g = C2 // (3 * DIM)
            qkv3 = jnp.transpose(t2, (1, 2, 0)).reshape(N, g, 3 * DIM, L)
            q, k, v = jnp.split(qkv3, 3, axis=2)
            q = jax.nn.relu(q)
            k = jax.nn.relu(k)
            vk = jnp.einsum('ngdl,ngel->ngde', v, k)
            out = jnp.einsum('ngde,ngdl->ngdl', vk, q)
            out = out / (jnp.sum(v, -1, keepdims=True) + ATT_EPS)
            out = jnp.transpose(out.reshape(N, g * DIM, L), (2, 0, 1))
            fx_h = proj(expmap0(out, c), c)
            ft = jnp.transpose(logmap0(proj(fx_h, c), c), (1, 2, 0))
            ft = conv1d(ft, w_res, pad=0) + b_res[None, :, None]
            fx = proj(expmap0(jnp.transpose(ft, (2, 0, 1)), c), c)
            residual = mobius_add(fx, x, c)
            return (fx, residual)
        key = jax.random.key(seed)
        ks = jax.random.split(key, 6)
        L, N, C, TD = (64, 16, 256, 256)
        x = jax.random.normal(ks[0], (L, N, C), jnp.float32) * 0.05
        w_qkv = jax.random.normal(ks[1], (3 * TD, C, 5), jnp.float32) / np.sqrt(C * 5)
        bn_gamma = jnp.ones((3 * TD,), jnp.float32)
        bn_beta = jnp.zeros((3 * TD,), jnp.float32)
        w_dw = jax.random.normal(ks[2], (3 * TD, 1, 5), jnp.float32) / np.sqrt(5.0)
        w_pw = jax.random.normal(ks[3], (3 * TD, DIM, 1), jnp.float32) / np.sqrt(DIM)
        w_res = jax.random.normal(ks[4], (C, 2 * TD, 1), jnp.float32) / np.sqrt(2 * TD)
        b_res = jnp.zeros((C,), jnp.float32)
        return {'x': x, 'w_qkv': w_qkv, 'bn_gamma': bn_gamma, 'bn_beta': bn_beta, 'w_dw': w_dw, 'w_pw': w_pw, 'w_res': w_res, 'b_res': b_res}
    _L0_mix_all = _L0_mix_setup()
    _L0_mix_in = {k: v for k, v in _L0_mix_all.items() if k in ('w_qkv', 'bn_gamma', 'bn_beta', 'w_dw', 'w_pw', 'w_res', 'b_res')}
    del _L0_mix_all

    def _L0_ffn_setup():
        import jax, jax.numpy as jnp
        import numpy as np
        BN_EPS = 0.001

        def _bn(h, g, b, m, v):
            return g * (h - m) * jax.lax.rsqrt(v + BN_EPS) + b
        key = jax.random.key(seed)
        ks = jax.random.split(key, 8)
        B, F, Df = (256, 64, 256)
        E, H, D = (8, 256, 256)
        s1 = 1.0 / np.sqrt(Df)
        s2 = 1.0 / np.sqrt(H)
        return {'x': jax.random.normal(ks[0], (B, F, Df), jnp.float32), 'Wr': jax.random.normal(ks[1], (Df, E), jnp.float32) * s1, 'br': jnp.zeros((E,), jnp.float32), 'W1': jax.random.normal(ks[2], (E, Df, H), jnp.float32) * s1, 'b1': jnp.zeros((E, H), jnp.float32), 'g1': jnp.ones((E, H), jnp.float32), 'be1': jnp.zeros((E, H), jnp.float32), 'm1': jnp.zeros((E, H), jnp.float32), 'v1': jnp.ones((E, H), jnp.float32), 'W2': jax.random.normal(ks[3], (E, H, H), jnp.float32) * s2, 'b2': jnp.zeros((E, H), jnp.float32), 'g2': jnp.ones((E, H), jnp.float32), 'be2': jnp.zeros((E, H), jnp.float32), 'm2': jnp.zeros((E, H), jnp.float32), 'v2': jnp.ones((E, H), jnp.float32), 'Wo': jax.random.normal(ks[4], (E, H, D), jnp.float32) * s2, 'bo': jnp.zeros((E, D), jnp.float32)}
    _L0_ffn_all = _L0_ffn_setup()
    _L0_ffn_in = {k: v for k, v in _L0_ffn_all.items() if k in ('Wr', 'br', 'W1', 'b1', 'g1', 'be1', 'm1', 'v1', 'W2', 'b2', 'g2', 'be2', 'm2', 'v2', 'Wo', 'bo')}
    del _L0_ffn_all
    return {'x': x, 'src': src, 'dst': dst, 'L0_gnn_W': _L0_gnn_in['W'], 'L0_gnn_b': _L0_gnn_in['b'], 'L0_gnn_a_src': _L0_gnn_in['a_src'], 'L0_gnn_a_trg': _L0_gnn_in['a_trg'], 'L0_mix_w_qkv': _L0_mix_in['w_qkv'], 'L0_mix_bn_gamma': _L0_mix_in['bn_gamma'], 'L0_mix_bn_beta': _L0_mix_in['bn_beta'], 'L0_mix_w_dw': _L0_mix_in['w_dw'], 'L0_mix_w_pw': _L0_mix_in['w_pw'], 'L0_mix_w_res': _L0_mix_in['w_res'], 'L0_mix_b_res': _L0_mix_in['b_res'], 'L0_ffn_Wr': _L0_ffn_in['Wr'], 'L0_ffn_br': _L0_ffn_in['br'], 'L0_ffn_W1': _L0_ffn_in['W1'], 'L0_ffn_b1': _L0_ffn_in['b1'], 'L0_ffn_g1': _L0_ffn_in['g1'], 'L0_ffn_be1': _L0_ffn_in['be1'], 'L0_ffn_m1': _L0_ffn_in['m1'], 'L0_ffn_v1': _L0_ffn_in['v1'], 'L0_ffn_W2': _L0_ffn_in['W2'], 'L0_ffn_b2': _L0_ffn_in['b2'], 'L0_ffn_g2': _L0_ffn_in['g2'], 'L0_ffn_be2': _L0_ffn_in['be2'], 'L0_ffn_m2': _L0_ffn_in['m2'], 'L0_ffn_v2': _L0_ffn_in['v2'], 'L0_ffn_Wo': _L0_ffn_in['Wo'], 'L0_ffn_bo': _L0_ffn_in['bo']}

def reference(x, src, dst, L0_gnn_W, L0_gnn_b, L0_gnn_a_src, L0_gnn_a_trg, L0_mix_w_qkv, L0_mix_bn_gamma, L0_mix_bn_beta, L0_mix_w_dw, L0_mix_w_pw, L0_mix_w_res, L0_mix_b_res, L0_ffn_Wr, L0_ffn_br, L0_ffn_W1, L0_ffn_b1, L0_ffn_g1, L0_ffn_be1, L0_ffn_m1, L0_ffn_v1, L0_ffn_W2, L0_ffn_b2, L0_ffn_g2, L0_ffn_be2, L0_ffn_m2, L0_ffn_v2, L0_ffn_Wo, L0_ffn_bo):
    import jax
    import jax.numpy as jnp

    def _L0_gnn_ref(x, edge_index, W, b, a_src, a_trg):
        import jax, jax.numpy as jnp
        import numpy as np
        N = 50000
        E = 25000
        F_IN = 256
        K = 8
        F_OUT = 32
        NEG_SLOPE = 0.2
        n = x.shape[0]
        loops = jnp.arange(n, dtype=edge_index.dtype)
        src = jnp.concatenate([edge_index[0], loops])
        trg = jnp.concatenate([edge_index[1], loops])
        h_prime = (x @ W + b).reshape(n, K, F_OUT)
        h_src = jnp.sum(h_prime * a_src, axis=2)
        h_trg = jnp.sum(h_prime * a_trg, axis=2)
        e = h_src[src] + h_trg[trg]
        e = jax.nn.leaky_relu(e, negative_slope=NEG_SLOPE)
        e = e - jnp.max(e)
        exp_e = jnp.exp(e)
        denom = jax.ops.segment_sum(exp_e, trg, num_segments=n)
        alpha = exp_e / (denom[trg] + 1e-10)
        msg = h_prime[src] * alpha[:, :, None]
        out = jax.ops.segment_sum(msg, trg, num_segments=n)
        return out.reshape(n, K * F_OUT)

    def _L0_mix_ref(x, w_qkv, bn_gamma, bn_beta, w_dw, w_pw, w_res, b_res):
        import jax, jax.numpy as jnp
        import numpy as np
        C_CURV = 1.0
        MIN_NORM = 1e-15
        BALL_EPS = 1e-05
        ATT_EPS = 1e-15
        DIM = 32

        def _norm(x):
            return jnp.clip(jnp.linalg.norm(x, axis=-1, keepdims=True), MIN_NORM)

        def proj(x, c):
            maxnorm = (1.0 - BALL_EPS) / jnp.sqrt(c)
            n = _norm(x)
            return jnp.where(n > maxnorm, x / n * maxnorm, x)

        def expmap0(u, c):
            sc = jnp.sqrt(c)
            n = _norm(u)
            return jnp.tanh(sc * n) * u / (sc * n)

        def logmap0(p, c):
            sc = jnp.sqrt(c)
            n = _norm(p)
            return jnp.arctanh(jnp.clip(sc * n, -1.0 + 1e-07, 1.0 - 1e-07)) * p / (sc * n)

        def mobius_add(x, y, c):
            x2 = jnp.sum(x * x, -1, keepdims=True)
            y2 = jnp.sum(y * y, -1, keepdims=True)
            xy = jnp.sum(x * y, -1, keepdims=True)
            num = (1 + 2 * c * xy + c * y2) * x + (1 - c * x2) * y
            den = 1 + 2 * c * xy + c * c * x2 * y2
            return num / jnp.clip(den, MIN_NORM)

        def conv1d(x, w, pad, groups=1):
            return jax.lax.conv_general_dilated(x, w, (1,), [(pad, pad)], dimension_numbers=('NCH', 'OIH', 'NCH'), feature_group_count=groups)

        def batchnorm(x, gamma, beta):
            mean = jnp.mean(x, axis=(0, 2), keepdims=True)
            var = jnp.var(x, axis=(0, 2), keepdims=True)
            xn = (x - mean) * jax.lax.rsqrt(var + 1e-05)
            return gamma[None, :, None] * xn + beta[None, :, None]

        def _reference_tuple_inner(x, w_qkv, bn_gamma, bn_beta, w_dw, w_pw, w_res, b_res):
            c = C_CURV
            h = logmap0(proj(x, c), c)
            h = jnp.transpose(h, (1, 2, 0))
            h = conv1d(h, w_qkv, pad=2)
            h = batchnorm(h, bn_gamma, bn_beta)
            h = jax.nn.relu(jnp.transpose(h, (2, 0, 1)))
            qkv = proj(expmap0(h, c), c)
            t = jnp.transpose(logmap0(proj(qkv, c), c), (1, 2, 0))
            s = conv1d(t, w_dw, pad=2, groups=t.shape[1])
            s = conv1d(s, w_pw, pad=0, groups=t.shape[1] // DIM)
            cat = jnp.concatenate([t, s], axis=1)
            ai = proj(expmap0(jnp.transpose(cat, (2, 0, 1)), c), c)
            t2 = logmap0(proj(ai, c), c)
            L, N, C2 = t2.shape
            g = C2 // (3 * DIM)
            qkv3 = jnp.transpose(t2, (1, 2, 0)).reshape(N, g, 3 * DIM, L)
            q, k, v = jnp.split(qkv3, 3, axis=2)
            q = jax.nn.relu(q)
            k = jax.nn.relu(k)
            vk = jnp.einsum('ngdl,ngel->ngde', v, k)
            out = jnp.einsum('ngde,ngdl->ngdl', vk, q)
            out = out / (jnp.sum(v, -1, keepdims=True) + ATT_EPS)
            out = jnp.transpose(out.reshape(N, g * DIM, L), (2, 0, 1))
            fx_h = proj(expmap0(out, c), c)
            ft = jnp.transpose(logmap0(proj(fx_h, c), c), (1, 2, 0))
            ft = conv1d(ft, w_res, pad=0) + b_res[None, :, None]
            fx = proj(expmap0(jnp.transpose(ft, (2, 0, 1)), c), c)
            residual = mobius_add(fx, x, c)
            return (fx, residual)
        return _reference_tuple_inner(x, w_qkv, bn_gamma, bn_beta, w_dw, w_pw, w_res, b_res)[0]

    def _L0_ffn_ref(x, Wr, br, W1, b1, g1, be1, m1, v1, W2, b2, g2, be2, m2, v2, Wo, bo):
        import jax, jax.numpy as jnp
        import numpy as np
        BN_EPS = 0.001

        def _bn(h, g, b, m, v):
            return g * (h - m) * jax.lax.rsqrt(v + BN_EPS) + b
        feat = jnp.mean(x, axis=0)
        w = jax.nn.softmax(feat @ Wr + br, axis=-1)
        h = jnp.einsum('bfd,edh->bfeh', x, W1) + b1
        h = jax.nn.relu(_bn(h, g1, be1, m1, v1))
        h = jnp.einsum('bfeh,ehk->bfek', h, W2) + b2
        h = jax.nn.relu(_bn(h, g2, be2, m2, v2))
        y = jnp.einsum('bfeh,ehd->bfed', h, Wo) + bo
        return jnp.einsum('bfed,fe->bfd', y, w)
    edge_index = jnp.stack([src, dst])
    xn = _layernorm(x, axis=-1)
    x = x + _L0_gnn_ref(xn, edge_index, L0_gnn_W, L0_gnn_b, L0_gnn_a_src, L0_gnn_a_trg) + _L0_mix_ref(xn[None], L0_mix_w_qkv, L0_mix_bn_gamma, L0_mix_bn_beta, L0_mix_w_dw, L0_mix_w_pw, L0_mix_w_res, L0_mix_b_res)[0]
    x = x + _L0_ffn_ref(_layernorm(x, axis=-1)[None], L0_ffn_Wr, L0_ffn_br, L0_ffn_W1, L0_ffn_b1, L0_ffn_g1, L0_ffn_be1, L0_ffn_m1, L0_ffn_v1, L0_ffn_W2, L0_ffn_b2, L0_ffn_g2, L0_ffn_be2, L0_ffn_m2, L0_ffn_v2, L0_ffn_Wo, L0_ffn_bo)[0]
    return x

_drawn_inputs = setup_inputs


def setup_inputs(seed=0):
    import zlib

    import numpy as np

    out = dict(_drawn_inputs(seed))
    spreads = {'L0_mix_bn_gamma': (1.0, 0.6),
     'L0_mix_bn_beta': (0.0, 0.562),
     'L0_mix_b_res': (0.0, 0.43),
     'L0_ffn_br': (0.0, 0.1),
     'L0_ffn_b1': (0.0, 0.381),
     'L0_ffn_g1': (1.0, 0.2),
     'L0_ffn_be1': (0.0, 0.376),
     'L0_ffn_m1': (0.0, 0.364),
     'L0_ffn_v1': (1.0, 0.6),
     'L0_ffn_b2': (0.0, 0.27),
     'L0_ffn_g2': (1.0, 0.2),
     'L0_ffn_be2': (0.0, 0.28),
     'L0_ffn_m2': (0.0, 0.28),
     'L0_ffn_v2': (1.0, 0.6),
     'L0_ffn_bo': (0.0, 0.1)}
    factors = {'L0_mix_w_dw': 8.0, 'L0_mix_w_pw': 8.0}
    for name, (base, spread) in spreads.items():
        noise = np.random.default_rng([zlib.crc32(name.encode()), seed]).standard_normal(out[name].shape)
        drawn = base * np.exp(spread * noise) if base else spread * noise
        out[name] = jnp.asarray(drawn.astype(out[name].dtype))
    for name, factor in factors.items():
        out[name] = (out[name] * factor).astype(out[name].dtype)
    return out
```

```python
import math
from contextlib import ExitStack

import numpy as np

import concourse.bass as bass
from concourse import mybir

F32 = mybir.dt.float32
I32 = mybir.dt.int32
ALU = mybir.AluOpType
ACT = mybir.ActivationFunctionType
AX = mybir.AxisListType

P = 128
N = 3125
E = 50000
F = 256
KC = F // P
H = 8
DH = F // H
NT = -(-N // P)
LASTN = N - (NT - 1) * P
NPAD = NT * P
BLK = 512
NB = N // BLK
TPB = BLK // P
LASTB = N - NB * BLK
HW = F + 2 * H
C2 = 768
MC = C2 // P
OC = 512
NX = 8
LN_EPS, BN_EPS, FBN_EPS, ATT_EPS, GAT_EPS = 1e-5, 1e-5, 1e-3, 1e-15, 1e-10
MIN_NORM = 1e-15
MAXNORM = float(np.float32(1.0 - 1e-5))
ATANH_MAX = math.atanh(MAXNORM)
SLOPE = 0.2

EC = 4
EG = EC * P
NG = -(-E // EG)
LASTE = E - (NG - 1) * EG
WIN = 64
WSHIFT = WIN.bit_length() - 1
PAD_DST = -1000000
SLOTS = 4
GLOOP = (NG - 2) // SLOTS
assert 1 + SLOTS * GLOOP + 1 == NG

CREDIT = 2


def plus(a, b):
    if isinstance(b, int) and b == 0:
        return a
    if isinstance(a, int) and a == 0:
        return b
    return a + b


def at(base, k, size):
    return bass.ds(plus(base * size, k), size) if not isinstance(base, int) else slice(base * size + k, base * size + k + size)


def cut(start, size):
    return slice(start, start + size) if isinstance(start, int) else bass.ds(start, size)


class Chain:

    def __init__(self, eng, sem):
        self.eng, self.sem, self.base, self.n = eng, sem, 0, 0

    def link(self, ins):
        ins.then_inc(self.sem, 1)
        self.n += 1
        self.eng.wait_ge(self.sem, plus(self.base, self.n))

    def enter(self):
        self.first = plus(self.base, self.n)
        return self.first

    def turn(self, i, per):
        self.base, self.n, self.per = plus(i * per, self.first), 0, per

    def leave(self, passes):
        assert self.n == self.per, (self.n, self.per)
        self.base, self.n = self.first + passes * self.per, 0


def program(nc, a, out):
    with ExitStack() as ctx:
        def sb(name, shape, dt=F32):
            return ctx.enter_context(nc.sbuf_tensor(name, shape, dt))

        def sem(name):
            return ctx.enter_context(nc.semaphore(name))

        table = nc.dram_tensor("projected_rows", [NPAD, HW], F32, kind="Internal").ap()
        ranges = nc.dram_tensor("group_ranges", [2 * (NG + 1)], I32, kind="Internal").ap()
        firsts = nc.dram_tensor("group_firsts", [NG], I32, kind="Internal").ap()

        bank = [ctx.enter_context(nc.psum_tensor(f"bank{i}", [P, 512], F32)) for i in range(8)]
        b_q, b_k, b_v, b_o, b_r, b_hte = bank[:6]
        b_seg = bank[6:8]

        Z = sb("Z", [P, MC, NPAD])
        zflat = Z[:, :, :].rearrange("p c n -> p (c n)")
        x_in = zflat[:, 4 * NPAD:4 * NPAD + NT * F].rearrange("p (t f) -> p t f", f=F)
        mixed = Z[:, 0:2, :].rearrange("p c (t n) -> p t c n", n=P)
        ffn_w = zflat[:, 2 * NPAD:2 * NPAD + 3 * NX * KC * F].rearrange("p (m e k f) -> p m e k f", m=3, e=NX, k=KC)
        FR = sb("FR", [P, KC, NPAD])
        DEN = sb("DEN", [H, NPAD])
        hp = [sb(f"hp{i}", [P, HW]) for i in range(2)]
        hst = sb("hst", [P, NT, 2 * H])
        G = [sb(f"G{i}", [P, EC, HW]) for i in range(SLOTS)]
        TT = [sb(f"TT{i}", [P, MC, 2 * P]) for i in range(2)]
        wqkv = TT[0][:, :, :].rearrange("p c n -> p (c n)").rearrange("p (k n) -> p k n", k=KC)
        ip = sb("ip", [P, MC, 2 * P])
        wres = sb("wres", [P, OC // P, F])
        wx = sb("wx", [P, KC, HW])
        acol = sb("acol", [P, 4])
        bcol = sb("bcol", [P, KC])
        hbias = sb("hbias", [P, HW])
        mixvec = sb("mixvec", [P, 3, MC])
        bres = sb("bres", [P, F])
        ident = sb("ident", [P, P])
        ones = sb("ones", [P, P])
        row_i = sb("row_i", [P, WIN], I32)
        row_f = sb("row_f", [P, WIN])
        col_i = sb("col_i", [P, 1], I32)
        col_f = sb("col_f", [P, 1])
        early = [G[i][:, :, :].bitcast(I32).rearrange("p c n -> p (c n)") for i in range(SLOTS)]
        dst_rows = early[3][0:NG, 0:EG]
        src_l = sb("src_l", [P, NG, EC], I32)
        dst_l = early[2][:, 0:NG * EC].rearrange("p (g c) -> p g c", c=EC)
        idx = [sb(f"idx{i}", [P, EC], I32) for i in range(SLOTS)]
        dst_f = sb("dst_f", [P, NG, EC])
        rng_i = sb("rng_i", [NG, 4], I32)
        zero2 = sb("zero2", [1, 2], I32)
        tab = sb("tab", [1, NG + 1, 2], I32)
        first_i = early[1][:, 0:NG]
        first_f = sb("first_f", [P, NG])
        pbase = sb("pbase", [P, NG])
        dcur = sb("dcur", [P, 1])
        pcur = sb("pcur", [WIN, 1])
        dstb = [sb(f"dstb{i}", [WIN, EG], I32) for i in range(SLOTS)]
        htw = [sb(f"htw{i}", [WIN, H]) for i in range(SLOTS)]
        htx = sb("htx", [WIN, H])
        ohT = [sb(f"ohT{i}", [WIN, EG]) for i in range(2)]
        oh = [sb(f"oh{i}", [P, EC, WIN]) for i in range(2)]
        zed = sb("zed", [P, EC, H])
        ex = [sb(f"ex{i}", [P, EC, H]) for i in range(2)]
        mxe = sb("mxe", [P, EC, H])
        exs = sb("exs", [P, NT, H])
        mx2 = sb("mx2", [P, 4])
        mxr = sb("mxr", [2, 1])
        negc = sb("negc", [P, 1])
        guard = sb("guard", [P, 1])
        stats = sb("stats", [P, NT, 6])
        mv = sb("mv", [P, NT, 2])
        bstats = sb("bstats", [P, MC, NB + 1, 6])
        bmv = sb("bmv", [P, MC, 2])
        baff = sb("baff", [P, 2, MC])
        nodes = sb("nodes", [P, 16, NT])
        xs = [sb(f"xs{i}", [P, F]) for i in range(2)]
        fs = [sb(f"fs{i}", [P, KC, P]) for i in range(2)]
        xr = [oh[i][:, :, :].rearrange("p c w -> p (c w)") for i in range(2)]
        U = [sb(f"U{i}", [P, 3, 512]) for i in range(2)]
        oT = sb("oT", [P, 512])
        junk = sb("junk", [P, 512])
        fvec = U[0][:, 0, 0:10 * KC * NX].rearrange("p (v e) -> p v e", v=10)
        ftmp = U[0][:, 0, 160:160 + 2 * KC * NX].rearrange("p (v e) -> p v e", v=2)
        faff = U[0][:, 0, 192:192 + 4 * KC * NX].rearrange("p (v e) -> p v e", v=4)
        gs = [U[0][:, 0, 256 + i * NX:256 + (i + 1) * NX] for i in range(2)]
        gate = U[0][:, 1, 0:NT * NX].rearrange("p (t e) -> p t e", e=NX)
        bo = U[1][0:NX, 0, 0:F]
        gT = [U[1][0:NX, 1, i * P:(i + 1) * P] for i in range(2)]
        dn = [U[1][0:H, 2, i * P:(i + 1) * P] for i in range(2)]
        spill = [junk[:, :].bitcast(mybir.dt.bfloat16)[:, i * F:(i + 1) * F].rearrange("p (h c) -> p h c", h=2) for i in range(4)]
        wT = junk[:, :].rearrange("p (c n) -> p c n", c=KC)
        bcolb = oT[:, 0:256].rearrange("p (c m) -> p c m", c=KC)
        wpw = oT[:, 256:256 + MC * 32].rearrange("p (c o) -> p c o", c=MC)
        ablk = sb("ablk", [P, KC, 2 * H])
        sq6 = [sb(f"sq6{i}", [P, 2, 3]) for i in range(2)]
        tiny = sb("tiny", [P, 12])
        epsr = [sb(f"epsr{i}", [P, 2]) for i in range(2)]
        lneps = sb("lneps", [P, 1])
        ksum = sb("ksum", [P, 16])
        wr = sb("wr", [P, KC, NX])
        brb = sb("brb", [P, NX])
        gred = sb("gred", [P, NT])
        h1T = [TT[i][:, 0:4, :].rearrange("p c n -> p (c n)").rearrange("p (k n) -> p k n", k=KC) for i in range(2)]
        h2T = [G[i][:, :, :].rearrange("p c n -> p (c n)")[:, 0:KC * BLK].rearrange("p (k n) -> p k n", k=KC)
               for i in range(2)]

        names = ("rstd f0 inv_f0 n2 n t0 t1 t2 fsq no2 rs nf2 ff scale").split()
        nd = {k: nodes[:, i, :] for i, k in enumerate(names)}

        s = {k: sem(k) for k in (
            "x_pad x_in weights edge_fill edges idn consts vchain achain gchain rsq_in rsq_out "
            "xs_ready tr_done fs_ready proj_mm hp_ready fr_copied wa_ready wa_mm wx_ready "
            "rng_ready rng_out rng_in ln_in ln_out cm_in cm_tr cm_red cm_mm exs_in exs_out "
            "z_mm z_copied z_stats baff_ready tt_ready u_mm u_evac fsq_ready eps_ready o_ready o_tr oT_ready "
            "r_mm mixed_ready no2_ready fr_clear "
            "ohT_ready hte_ready z_done zl_ready exp_done msg_ready seg_ready acc_done g_free idx_ready win_free "
            "xoT xhtw xhte xz xoh xseg mx_in mx_all "
            "as_ready asm_tr asm_done ft_ready nf2_ready th_in th_out x2_ready xs2_ready tr2_done fs2_ready fr2_copied "
            "lg_mm lg_done sm_in sm_out gates gs_ready gt_tr gt_ready bo_mm x2b "
            "ffn_w ffn_v faff_in faff_out h1_mm h1_act h2_mm h2_act y_mm y_add out_done").split()}
        gath = [sem(f"gath{i}") for i in range(SLOTS)]
        tout = [sem(f"tout{i}") for i in range(2)]
        back_in = [sem(f"back_in{i}") for i in range(2)]
        winl = [sem(f"winl{i}") for i in range(SLOTS)]

        def inside(row):
            return nc.s_assert_within(row, 0, N - 1, skip_runtime_bounds_check_because="a group's last window starts at or before its last target")

        block = ctx.enter_context(nc.Block())

        @block.sync
        def _(sp):
            nc.sync.sem_inc(tout[0], 16)
            nc.sync.sem_inc(tout[1], 16)
            sp.wait_ge(s["x_pad"], 1)
            full = (NT - 1) * P
            sp.dma_start(x_in[:, 0:NT - 1, :], a["x"][0:full, :].rearrange("(t p) f -> p t f", p=P)).then_inc(s["x_in"], 16)
            sp.dma_start(x_in[0:LASTN, NT - 1, :], a["x"][full:N, :]).then_inc(s["x_in"], 16)
            for dst, src in (
                (wx[:, :, 0:F], a["W"].rearrange("(k p) n -> p k n", p=P)),
                (wT, a["WT"].rearrange("(c p) i -> p c i", p=P)),
                (acol[:, :], a["acol"]), (bcol[:, :], a["bcol"]),
                (hbias[:, 0:F], a["b"][None, :].broadcast_to([P, F])),
                (wqkv, a["wqkv"].rearrange("(k p) n -> p k n", p=P)),
                (wpw, a["wpw"]), (mixvec[:, :, :], a["mixvec"]),
                (wres[:, :, :], a["wres"].rearrange("(c p) n -> p c n", p=P)),
                (bres[:, :], a["b_res"][None, :].broadcast_to([P, F])),
            ):
                sp.dma_start(dst, src).then_inc(s["weights"], 16)
            sp.wait_ge(s["edge_fill"], 2)
            whole = (NG - 1) * EG
            sp.dma_start(dst_rows[0:NG - 1, :], a["dst"][0:whole].rearrange("(g e) -> g e", e=EG)).then_inc(s["edges"], 16)
            sp.dma_start(dst_rows[NG - 1:NG, 0:LASTE], a["dst"][whole:E][None, :]).then_inc(s["edges"], 16)
            sp.dma_start(dst_rows[NG - 1:NG, LASTE:EG], a["dst"][whole:whole + EG - LASTE][None, :]).then_inc(s["edges"], 16)
            rest, part = divmod(LASTE, P)
            for buf, lay, raw in ((src_l, "src_l", "src"), (dst_l, "dst_l", "dst")):
                sp.dma_start(buf[:, 0:NG - 1, :], a[lay]).then_inc(s["edges"], 16)
                sp.dma_start(buf[:, NG - 1, 0:rest], a[raw + "_t"]).then_inc(s["edges"], 16)
                sp.dma_start(buf[0:part, NG - 1, rest:rest + 1], a[raw][whole + rest * P:E][:, None]).then_inc(s["edges"], 16)
            sp.wait_ge(s["rng_ready"], 1)
            sp.dma_start(ranges[None, 0:2], zero2[:, :]).then_inc(s["rng_out"], 16)
            sp.dma_start(ranges[2:2 * (NG + 1)].rearrange("(g c) -> g c", c=2), rng_i[:, 0:2]).then_inc(s["rng_out"], 16)
            sp.dma_start(firsts[:, None], rng_i[:, 0:1]).then_inc(s["rng_out"], 16)
            sp.wait_ge(s["rng_out"], 48)
            sp.dma_start(tab[:, :, :], ranges.rearrange("(a g c) -> a g c", a=1, c=2)).then_inc(s["rng_in"], 16)
            sp.dma_start(first_i, firsts[None, :].broadcast_to([P, NG])).then_inc(s["rng_in"], 16)
            def table_rows(t, slot):
                sp.wait_ge(s["hp_ready"], plus(t, 2))
                sp.dma_start(table[cut(t * P, P), :], hp[slot][:, :]).then_inc(tout[slot], 16)
            with sp.Fori(0, NT // 2) as i:
                for j in range(2):
                    table_rows(plus(i * 2, j), j)
            table_rows(NT - 1, 0)

            def window(g, slot, edges):
                sp.wait_ge(s["win_free"], plus(g, 1))
                d0 = sp.value_load(tab[0:1, cut(plus(g, 1), 1), 0], min_val=0, max_val=N - 1)
                sp.dma_start(dstb[slot][:, 0:edges], a["dst"][cut(g * EG, edges)][None, :].broadcast_to([WIN, edges])).then_inc(winl[slot], 16)
                sp.dma_start(htw[slot][:, :], table[bass.ds(d0, WIN), F + H:HW]).then_inc(winl[slot], 16)

            turns = sp.alloc_register("sp_extra")
            sp.reg_mov(turns, 0)

            def more_windows(g):
                entry = cut(plus(g, 1), 1)
                more = sp.value_load(tab[0:1, entry, 1], min_val=0, max_val=NPAD // WIN)
                with sp.If(more > 0):
                    d0 = sp.value_load(tab[0:1, entry, 0], min_val=0, max_val=N - 1)
                    with sp.Fori(1, more + 1) as w:
                        done = sp.snap(turns)
                        sp.wait_ge(s["xz"], done + 1)
                        row = inside(sp.snap(d0 + w * WIN))
                        sp.dma_start(htx[:, :], table[bass.ds(row, WIN), F + H:HW]).then_inc(s["xhtw"], 16)
                        sp.reg_add(turns, turns, 1)

            sp.wait_ge(tout[0], 16 * (1 + NT - NT // 2))
            sp.wait_ge(tout[1], 16 * (1 + NT // 2))
            sp.wait_ge(s["rng_in"], 32)
            for g in range(SLOTS):
                window(g, g, EG)
            more_windows(0)

            def step(g, j):
                if j is not None:
                    window(plus(g, 3), (j + 1 + 3) % SLOTS, EG)
                more_windows(g)

            with sp.Fori(0, GLOOP - 1) as i:
                for j in range(SLOTS):
                    step(i * SLOTS + (1 + j), j)
            g0 = 1 + (GLOOP - 1) * SLOTS
            for g in range(g0, NG):
                if g + 3 < NG:
                    window(g + 3, (g + 3) % SLOTS, EG if g + 3 < NG - 1 else LASTE)
                more_windows(g)

            sp.wait_ge(s["tt_ready"], NB * 2 + 1)
            for m, w in enumerate(("W1", "W2", "Wo")):
                sp.dma_start(ffn_w[:, m], a[w].rearrange("e (k p) f -> p e k f", p=P)).then_inc(s["ffn_w"], 16)
            for dst, src in ((fvec[:, :, :], a["fvec"]), (wr[:, :, :], a["Wr"].rearrange("(k p) e -> p k e", p=P)),
                             (brb[:, :], a["br"][None, :].broadcast_to([P, NX])), (bo[:, :], a["bo"])):
                sp.dma_start(dst, src).then_inc(s["ffn_v"], 16)
            def residual_rows(t, slot, rows):
                sp.wait_ge(s["asm_done"], plus(t, 1))
                sp.dma_start(xr[slot][0:rows, :], a["x"][cut(t * P, rows), :]).then_inc(back_in[slot], 16)
                sp.dma_start(hp[slot][:, :], table[cut(t * P, P), :]).then_inc(back_in[slot], 16)
            sp.wait_ge(s["seg_ready"], 1 + NG)
            with sp.Fori(0, NT // 2) as i:
                for j in range(2):
                    residual_rows(plus(i * 2, j), j, P)
            residual_rows(NT - 1, 0, LASTN)

            def store(t, k, rows, need):
                sp.wait_ge(s["y_add"], plus(need, 1))
                sp.dma_start(out[cut(t * P, rows), :].rearrange("n (c f) -> n c f", c=KC), mixed_rows(t, rows)).then_inc(s["out_done"], 16)

            def mixed_rows(t, rows):
                return mixed[0:rows, t] if isinstance(t, int) else mixed[0:rows, bass.ds(t, 1)].rearrange("p a c n -> p (a c) n")

            with sp.Fori(0, NB) as b:
                for j in range(TPB):
                    store(b * TPB + j, None, P, plus(b * (TPB * NX), (NX - 1) * TPB + j + 1))
            store(NT - 1, None, LASTN, NB * TPB * NX + NX)
            sp.wait_ge(s["out_done"], 16 * NT)

        @block.gpsimd
        def _(pool):
            g = nc.gpsimd
            chain = Chain(pool, s["gchain"])
            g.memset(x_in[:, NT - 1, :], 0.0).then_inc(s["x_pad"], 1)
            g.memset(src_l[:, NG - 1, :], 0).then_inc(s["edge_fill"], 1)
            g.memset(dst_l[:, NG - 1, :], PAD_DST).then_inc(s["edge_fill"], 1)
            chain.link(g.memset(ident[:, :], 0.0))
            g.memset(ones[:, :], 1.0).then_inc(s["consts"], 1)
            g.memset(ablk[:, :, :], 0.0).then_inc(s["consts"], 1)
            g.memset(ip[:, :, :], 0.0).then_inc(s["consts"], 1)
            g.memset(zero2[:, :], 0).then_inc(s["consts"], 1)
            g.iota(row_i[:, :], pattern=[[1, WIN]], base=0, channel_multiplier=0).then_inc(s["consts"], 1)
            g.iota(col_i[:, :], pattern=[[0, 1]], base=0, channel_multiplier=1).then_inc(s["consts"], 1)
            g.affine_select(out=ident[:, :], in_=ident[:, :], compare_op=ALU.not_equal, fill=1.0, base=0,
                            pattern=[[-1, P]], channel_multiplier=1).then_inc(s["idn"], 1)

            def keep(t, k, slot):
                pool.wait_ge(s["fs_ready"], plus(k, 1))
                g.tensor_copy(FR[:, :, cut(t * P, P)], fs[slot][:, :, :]).then_inc(s["fr_copied"], 1)
            g.sem_inc(s["fr_copied"], CREDIT)
            with pool.Fori(0, NT // 2) as i:
                for j in range(2):
                    keep(i * 2 + j, i * 2 + j, j)
            keep(NT - 1, NT - 1, 0)

            def sources(grp, slot, uses):
                if not isinstance(uses, int) or uses:
                    pool.wait_ge(gath[slot], uses)
                g.tensor_copy(idx[slot][:, :], src_l[:, cut(grp, 1), :].rearrange("p a c -> p (a c)")).then_inc(s["idx_ready"], 1)

            def gather(grp, slot, nxt):
                pool.wait_ge(s["idx_ready"], plus(grp, 1))
                pool.wait_ge(s["g_free"], plus(grp, 1))
                if nxt is not None:
                    sources(*nxt)
                for c in range(EC):
                    g.indirect_dma_start(
                        out=G[slot][:, c, :], out_offset=None, in_=table[:, :],
                        in_offset=bass.IndirectOffsetOnAxis(ap=idx[slot][:, c:c + 1], axis=0),
                    ).then_inc(gath[slot], 16)
            pool.wait_ge(s["edges"], 16 * 9)
            pool.wait_ge(tout[0], 16 * (1 + NT - NT // 2))
            pool.wait_ge(tout[1], 16 * (1 + NT // 2))
            pool.wait_ge(s["exs_in"], 1)
            sources(0, 0, 0)
            for grp in range(SLOTS + 1):
                gather(grp, grp % SLOTS, (grp + 1, (grp + 1) % SLOTS, (grp + 1) // SLOTS * (16 * EC)))
            with pool.Fori(1, GLOOP) as i:
                for j in range(SLOTS):
                    gather(i * SLOTS + (1 + j), (1 + j) % SLOTS, (i * SLOTS + (2 + j), (2 + j) % SLOTS, (i + (2 + j) // SLOTS) * (16 * EC)))
            gather(NG - 1, (NG - 1) % SLOTS, None)

            pool.wait_ge(s["mx_in"], 1)
            g.partition_all_reduce(mx2[:, 1:2], mx2[:, 0:1], P, bass.bass_isa.ReduceOp.max).then_inc(s["mx_all"], 1)

            def take(t, k, slot):
                pool.wait_ge(s["asm_tr"], plus(k, 1))
                g.tensor_copy(fs[slot][:, :, :], FR[:, :, cut(t * P, P)]).then_inc(s["as_ready"], 1)
                g.tensor_copy(dn[slot][:, :], DEN[:, cut(t * P, P)]).then_inc(s["as_ready"], 1)
            pool.wait_ge(s["g_free"], SLOTS + NG)
            with pool.Fori(0, NT // 2) as i:
                for j in range(2):
                    take(i * 2 + j, i * 2 + j, j)
            take(NT - 1, NT - 1, 0)

            def keep2(t, k, slot):
                pool.wait_ge(s["fs2_ready"], plus(k, 1))
                g.tensor_copy(FR[:, :, cut(t * P, P)], fs[slot][:, :, :]).then_inc(s["fr2_copied"], 1)
            g.sem_inc(s["fr2_copied"], CREDIT)
            with pool.Fori(0, NT // 2) as i:
                for j in range(2):
                    keep2(i * 2 + j, i * 2 + j, j)
            keep2(NT - 1, NT - 1, 0)

            pool.wait_ge(s["gates"], 1)

            def gates(t, k, slot):
                pool.wait_ge(s["gt_tr"], plus(k, 1))
                g.tensor_copy(gs[slot][:, :], gate[:, cut(t, 1), :].rearrange("p a e -> p (a e)")).then_inc(s["gs_ready"], 1)
            with pool.Fori(0, NT // 2) as i:
                for j in range(2):
                    gates(i * 2 + j, i * 2 + j, j)
            gates(NT - 1, NT - 1, 0)

        @block.scalar
        def _(act):
            A = nc.scalar
            A.sem_inc(s["z_copied"], 3)
            A.sem_inc(s["oT_ready"], 1)
            A.sem_inc(s["mixed_ready"], 1)
            A.sem_inc(s["nf2_ready"], 1)
            A.sem_inc(s["h1_act"], 1)
            A.sem_inc(s["h2_act"], 1)
            A.sem_inc(s["u_evac"], 3)
            A.sem_inc(s["no2_ready"], CREDIT)
            act.wait_ge(s["rsq_in"], 1)
            A.activation(nd["t0"], nd["t1"], ACT.Sqrt).then_inc(s["rsq_out"], 1)
            act.wait_ge(s["rsq_in"], 2)
            A.activation(nd["n"], nd["n2"], ACT.Sqrt).then_inc(s["rsq_out"], 1)
            act.wait_ge(s["ln_in"], 1)
            A.activation(nd["t1"], nd["t0"], ACT.Ln).then_inc(s["ln_out"], 1)

            act.wait_ge(s["wa_mm"], 1)
            A.copy(wx[:, :, F:HW], b_r[:, 0:KC * 2 * H].rearrange("p (k h) -> p k h", k=KC)).then_inc(s["wx_ready"], 1)
            A.copy(hbias[:, F:HW], b_r[:, 64:64 + 2 * H]).then_inc(s["wx_ready"], 1)

            def features(t, k, slot):
                act.wait_ge(s["tr_done"], plus(k, 1 + CREDIT))
                act.wait_ge(s["proj_mm"], plus(k, 1))
                act.wait_ge(s["fr_copied"], plus(k, 1))
                A.copy(fs[slot][:, :, :], bank[slot][:, 0:F].rearrange("p (k n) -> p k n", k=KC)).then_inc(s["fs_ready"], 1)
            with act.Fori(0, NT // 2) as i:
                for j in range(2):
                    features(i * 2 + j, i * 2 + j, j)
            features(NT - 1, NT - 1, 0)

            act.wait_ge(s["exs_in"], 1)
            A.activation(exs[:, :, :], exs[:, :, :], ACT.Exp, bias=negc[:, 0:1]).then_inc(s["exs_out"], 1)

            def z_copy(b, n):
                for c in range(MC):
                    act.wait_ge(s["z_mm"], plus(b * MC, c + 1))
                    A.copy(Z[:, c, cut(b * BLK, n)], bank[c % 3][:, 0:n]).then_inc(s["z_copied"], 1)
            with act.Fori(0, NB) as b:
                z_copy(b, BLK)
            z_copy(NB, P)
            act.wait_ge(s["rsq_in"], 3)
            A.activation(baff[:, 0, :], baff[:, 1, :], ACT.Sqrt).then_inc(s["rsq_out"], 1)

            act.wait_ge(s["baff_ready"], 1)

            def batch_norm(b, half, k, n, free):
                act.wait_ge(s["u_mm"], plus(free, 1))
                for c in range(MC):
                    ins = A.activation(TT[half][:, c, 0:n], Z[:, c, cut(plus(b * BLK, half * 2 * P), n)], ACT.Relu,
                                       bias=baff[:, 1, c:c + 1], scale=baff[:, 0, c:c + 1])
                ins.then_inc(s["tt_ready"], 1)

            def squares(t, slot):
                act.wait_ge(s["o_tr"], plus(t, 1))
                act.wait_ge(s["no2_ready"], plus(t, 1))
                for m in range(3):
                    act.wait_ge(s["u_mm"], plus(t * 3, m + 2))
                    act.wait_ge(s["u_evac"], plus(t * 3, m + 2))
                    src = bank[m][:, :].rearrange("p (h s c) -> p h s c", h=2, s=2)
                    A.activation(U[slot][:, m, :], bank[m][:, :], ACT.Copy if m == 2 else ACT.Relu)
                    for part in range(2):
                        ins = A.activation(spill[((slot * 3 + m) % 2) * 2 + part], src[:, :, part, :], ACT.Square,
                                           accum_out=sq6[slot][:, part, m:m + 1])
                    ins.then_inc(s["u_evac"], 1)

            def epsilon(t, slot):
                act.wait_ge(s["fsq_ready"], plus(t, 1))
                A.activation(epsr[slot][:, 0:1], nd["fsq"][:, cut(t, 1)], ACT.Ln).then_inc(s["achain"], 1)
                act.wait_ge(s["achain"], plus(t, 1))
                A.activation(epsr[slot][:, 1:2], epsr[slot][:, 0:1], ACT.Exp, scale=-0.5, bias=lneps[:, 0:1]).then_inc(s["eps_ready"], 1)

            def rows_out(t, slot):
                act.wait_ge(s["o_ready"], plus(t, 1))
                A.activation(U[slot][:, 1, :], U[slot][:, 0, :], ACT.Square, accum_out=nd["no2"][:, cut(t, 1)]).then_inc(s["no2_ready"], 1)
                act.wait_ge(s["o_tr"], plus(t, 1 + CREDIT))
                act.wait_ge(s["r_mm"], plus(t, 1))
                A.copy(oT[:, :], b_o[:, :]).then_inc(s["oT_ready"], 1)
                act.wait_ge(s["r_mm"], plus(t, 2))
                A.copy(mixed[:, cut(t, 1)].rearrange("p a c n -> p (a c) n"),
                       b_r[:, 0:F].rearrange("p (c n) -> p c n", c=KC)).then_inc(s["mixed_ready"], 1)

            def mix(b, tiles):
                t0 = b * TPB
                batch_norm(b, 0, None, min(2, tiles) * P, t0 * 3)
                if tiles > 2:
                    batch_norm(b, 1, None, 2 * P, t0 * 3)
                for j in range(tiles):
                    t = plus(t0, j)
                    squares(t, j % 2)
                    epsilon(t, j % 2)
                    if j:
                        rows_out(plus(t0, j - 1), (j - 1) % 2)
                rows_out(plus(t0, tiles - 1), (tiles - 1) % 2)

            with act.Fori(0, NB) as b:
                mix(b, TPB)
            mix(NB, 1)

            act.wait_ge(s["rsq_in"], 4)
            A.activation(nd["t1"], nd["t0"], ACT.Sqrt).then_inc(s["rsq_out"], 1)

            def norms(t, k):
                act.wait_ge(s["ft_ready"], plus(k, 1))
                act.wait_ge(s["nf2_ready"], plus(k, 1))
                A.activation(junk[:, 0:F].rearrange("p (c n) -> p c n", c=KC), mixed[:, cut(t, 1)].rearrange("p a c n -> p (a c) n"),
                             ACT.Square, accum_out=nd["nf2"][:, cut(t, 1)]).then_inc(s["nf2_ready"], 1)
            with act.Fori(0, NT) as i:
                norms(i, i)
            act.wait_ge(s["th_in"], 1)
            A.activation(nd["n"], nd["t0"], ACT.Sqrt).then_inc(s["achain"], 1)
            act.wait_ge(s["achain"], NT + 1)
            A.activation(nd["t1"], nd["n"], ACT.Tanh).then_inc(s["th_out"], 1)
            def step(grp, par):
                act.wait_ge(s["zl_ready"], plus(grp, 1))
                if not (isinstance(grp, int) and grp == 0):
                    act.wait_ge(s["seg_ready"], grp)
                A.activation(ex[par][:, :, :], zed[:, :, :], ACT.Exp, bias=negc[:, 0:1]).then_inc(s["exp_done"], 1)
            step(0, 0)
            with act.Fori(0, GLOOP) as i:
                for j in range(SLOTS):
                    step(i * SLOTS + (1 + j), (1 + j) % 2)
            step(NG - 1, (NG - 1) % 2)

            act.wait_ge(s["rsq_in"], 5)
            A.activation(nd["t0"], nd["t1"], ACT.Sqrt).then_inc(s["rsq_out"], 1)
            act.wait_ge(s["faff_in"], 1)
            A.activation(ftmp[:, :, :], ftmp[:, :, :], ACT.Sqrt).then_inc(s["faff_out"], 1)

            def features2(t, k, slot):
                act.wait_ge(s["tr2_done"], plus(k, 1 + CREDIT))
                act.wait_ge(s["lg_mm"], plus(k, 1))
                act.wait_ge(s["fr2_copied"], plus(k, 1))
                A.copy(fs[slot][:, :, :], bank[slot][:, 0:F].rearrange("p (k n) -> p k n", k=KC)).then_inc(s["fs2_ready"], 1)
            with act.Fori(0, NT // 2) as i:
                for j in range(2):
                    features2(i * 2 + j, i * 2 + j, j)
            features2(NT - 1, NT - 1, 0)
            act.wait_ge(s["sm_in"], 1)
            A.activation(gate[:, :, :], gate[:, :, :], ACT.Exp).then_inc(s["sm_out"], 1)

            def gates(t, k, slot):
                act.wait_ge(s["gt_tr"], plus(k, 1 + CREDIT))
                act.wait_ge(s["bo_mm"], plus(k, 1))
                A.copy(gT[slot][:, :], bank[slot][0:NX, 0:P]).then_inc(s["gt_ready"], 1)
            with act.Fori(0, NT // 2) as i:
                for j in range(2):
                    gates(i * 2 + j, i * 2 + j, j)
            gates(NT - 1, NT - 1, 0)

            def first(b, e, n):
                for m in range(KC):
                    act.wait_ge(s["h1_mm"], plus(b * (NX * KC), e * KC + m + 1))
                    if m == 0:
                        act.wait_ge(s["h2_mm"], plus(b * NX, e + 1))
                    A.activation(h1T[e % 2][:, m, 0:n], bank[m][:, 0:n], ACT.Relu, bias=faff[:, 1, e * KC + m:e * KC + m + 1],
                                 scale=faff[:, 0, e * KC + m:e * KC + m + 1]).then_inc(s["h1_act"], 1)

            def second(b, e, n):
                for m in range(KC):
                    act.wait_ge(s["h2_mm"], plus(b * NX, e + 1 + CREDIT))
                    if m == 0:
                        act.wait_ge(s["y_mm"], plus(b * NX, e + 1))
                    A.activation(h2T[e % 2][:, m, 0:n], bank[2 + m][:, 0:n], ACT.Relu, bias=faff[:, 3, e * KC + m:e * KC + m + 1],
                                 scale=faff[:, 2, e * KC + m:e * KC + m + 1]).then_inc(s["h2_act"], 1)

            def experts(b, n):
                first(b, 0, n)
                for e in range(NX):
                    if e + 1 < NX:
                        first(b, e + 1, n)
                    second(b, e, n)
            act.wait_ge(s["faff_out"], 2)
            with act.Fori(0, NB) as b:
                experts(b, BLK)
            experts(NB, P)

        @block.tensor
        def _(pe):
            T = nc.tensor
            T.sem_inc(s["tr_done"], CREDIT)
            T.sem_inc(s["seg_ready"], 1)
            T.sem_inc(s["r_mm"], 1)
            T.sem_inc(s["u_mm"], 1)
            T.sem_inc(s["proj_mm"], CREDIT)
            T.sem_inc(s["o_tr"], CREDIT)
            T.sem_inc(s["asm_tr"], CREDIT)
            T.sem_inc(s["tr2_done"], CREDIT)
            T.sem_inc(s["lg_mm"], CREDIT)
            T.sem_inc(s["gt_tr"], CREDIT)
            T.sem_inc(s["bo_mm"], CREDIT)
            T.sem_inc(s["h2_mm"], CREDIT)
            T.sem_inc(s["y_mm"], CREDIT)

            pe.wait_ge(s["wa_ready"], 2)
            for k in range(KC):
                for c in range(KC):
                    T.matmul(b_r[:, k * 2 * H:(k + 1) * 2 * H], wT[:, c, k * P:(k + 1) * P], ablk[:, c, :], start=(c == 0), stop=(c == KC - 1))
            for c in range(KC):
                ins = T.matmul(b_r[:, 64:64 + 2 * H], bcolb[:, c, :], ablk[:, c, :], start=(c == 0), stop=(c == KC - 1))
            ins.then_inc(s["wa_mm"], 1)
            pe.wait_ge(s["idn"], 1)

            def turn(t, k, slot, ready, free, done):
                pe.wait_ge(s[ready], plus(k, 1))
                if free is not None:
                    pe.wait_ge(s[free], k)
                for c in range(KC):
                    ins = T.transpose(bank[slot][:, c * P:(c + 1) * P], xs[slot][:, c * P:(c + 1) * P], ident[:, :])
                ins.then_inc(s[done], 1)

            def project(k, slot):
                pe.wait_ge(s["fs_ready"], plus(k, 1))
                pe.wait_ge(s["hp_ready"], plus(k, 1))
                for c in range(KC):
                    ins = T.matmul(bank[2 + slot][:, 0:HW], fs[slot][:, c, :], wx[:, c, :], start=(c == 0), stop=(c == KC - 1))
                ins.then_inc(s["proj_mm"], 1)

            pe.wait_ge(s["wx_ready"], 2)
            with pe.Fori(0, NT // 2) as i:
                for j in range(2):
                    turn(None, i * 2 + j, j, "xs_ready", None, "tr_done")
                for j in range(2):
                    pe.wait_ge(s["fs_ready"], i * 2 + (j + 1))
                    if j == 0:
                        pe.wait_ge(s["hp_ready"], i * 2 + 1)
                    for c in range(KC):
                        ins = T.matmul(bank[2 + j][:, 0:HW], fs[j][:, c, :], wx[:, c, :], start=(c == 0), stop=(c == KC - 1))
                    ins.then_inc(s["proj_mm"], 1)
            turn(None, NT - 1, 0, "xs_ready", None, "tr_done")
            project(NT - 1, 0)

            pe.wait_ge(s["cm_in"], 1)
            T.transpose(b_hte[0:2, 0:P], mx2[:, 0:2], ident[:, :]).then_inc(s["cm_tr"], 1)
            pe.wait_ge(s["cm_red"], 1)
            T.matmul(b_hte[:, 256:257], ones[0:2, :], mxr[:, :], start=True, stop=True).then_inc(s["cm_mm"], 1)

            pe.wait_ge(s["fr_copied"], NT + CREDIT)
            pe.wait_ge(s["hp_ready"], 1 + NT)

            def channels(b, n):
                for c in range(MC):
                    pe.wait_ge(s["z_copied"], plus(b * MC, c + 1))
                    for k in range(KC):
                        ins = T.matmul(bank[c % 3][:, 0:n], wqkv[:, k, c * P:(c + 1) * P], FR[:, k, cut(b * BLK, n)],
                                       start=(k == 0), stop=(k == KC - 1))
                    ins.then_inc(s["z_mm"], 1)
            with pe.Fori(0, NB) as b:
                channels(b, BLK)
            channels(NB, P)

            pe.wait_ge(s["z_copied"], 3 + (NB + 1) * MC)

            def u_rows(t, j):
                half, col = j // 2, (j % 2) * P
                if j % 2 == 0:
                    pass
                for m in range(3):
                    pe.wait_ge(s["u_evac"], plus(t * 3, m + 1))
                    for h in range(2):
                        c = 2 * m + h
                        ins = T.matmul(bank[m][:, h * 256:(h + 1) * 256], TT[half][:, c, col:col + P], ip[:, c, :], start=True, stop=True)
                    ins.then_inc(s["u_mm"], 1)

            def out_rows(t, slot):
                pe.wait_ge(s["o_ready"], plus(t, 1))
                pe.wait_ge(s["oT_ready"], plus(t, 1))
                for c in range(4):
                    ins = T.transpose(b_o[:, c * P:(c + 1) * P], U[slot][:, 0, c * P:(c + 1) * P], ident[:, :])
                ins.then_inc(s["o_tr"], 1)
                pe.wait_ge(s["oT_ready"], plus(t, 2))
                pe.wait_ge(s["mixed_ready"], plus(t, 1))
                for c in range(4):
                    half, src = divmod(c, 2)
                    ins = T.matmul(b_r[:, 0:F], oT[:, c * P:(c + 1) * P], wres[:, 2 * src + half, :], start=(c == 0), stop=(c == 3))
                ins.then_inc(s["r_mm"], 1)

            def mix(b, tiles, tts):
                t0 = b * TPB
                for j in range(tiles):
                    if j % 2 == 0:
                        pe.wait_ge(s["tt_ready"], plus(b * 2, j // 2 + 1))
                    u_rows(plus(t0, j), j)
                    if j:
                        out_rows(plus(t0, j - 1), (j - 1) % 2)
                out_rows(plus(t0, tiles - 1), (tiles - 1) % 2)

            with pe.Fori(0, NB) as b:
                mix(b, TPB, 2)
            mix(NB, 1, 1)

            def targets(grp, slot, par, edges=EG):
                pe.wait_ge(s["ohT_ready"], plus(grp, 1))
                pe.wait_ge(winl[slot], plus(use(grp, slot) * 32, 32))
                if not (isinstance(grp, int) and grp == 0):
                    pe.wait_ge(s["z_done"], grp)
                for c in range(EC):
                    ins = T.matmul(b_hte[:, c * H:(c + 1) * H], ohT[par][:, c * P:(c + 1) * P], htw[slot][:, :], start=True, stop=True)
                ins.then_inc(s["hte_ready"], 1)

            def use(grp, slot):
                if isinstance(grp, int):
                    return grp // SLOTS
                raise ValueError

            turns_a = pe.alloc_register("pe_extra_a")
            turns_b = pe.alloc_register("pe_extra_b")
            pe.reg_mov(turns_a, 0)
            pe.reg_mov(turns_b, 0)

            def more_targets(grp):
                more = pe.value_load(tab[0:1, cut(plus(grp, 1), 1), 1], min_val=0, max_val=NPAD // WIN)
                with pe.If(more > 0):
                    with pe.Fori(0, more) as w:
                        done = pe.snap(turns_a)
                        pe.wait_ge(s["xoT"], done + 1)
                        pe.wait_ge(s["xhtw"], done * 16 + 16)
                        for c in range(EC):
                            ins = T.matmul(b_hte[:, 256 + c * H:256 + (c + 1) * H], ohT[0][:, c * P:(c + 1) * P] if False else xohT[:, c * P:(c + 1) * P], htx[:, :], start=True, stop=True)
                        ins.then_inc(s["xhte"], 1)
                        pe.reg_add(turns_a, turns_a, 1)

            xohT = junk[0:WIN, :]

            def sums_of(slot, par, onehot, seg):
                for m in range(KC):
                    for c in range(EC):
                        T.matmul(seg[:, m * WIN:(m + 1) * WIN], G[slot][:, c, m * P:(m + 1) * P], onehot[:, c, :], start=(c == 0), stop=(c == EC - 1))
                for c in range(EC):
                    ins = T.matmul(seg[0:H, KC * WIN:(KC + 1) * WIN], ex[par][:, c, :], onehot[:, c, :], start=(c == 0), stop=(c == EC - 1))
                return ins

            xoh = junk[:, 0:EC * WIN].rearrange("p (c w) -> p c w", c=EC)

            def more_sums(grp, slot, par):
                more = pe.value_load(tab[0:1, cut(plus(grp, 1), 1), 1], min_val=0, max_val=NPAD // WIN)
                with pe.If(more > 0):
                    with pe.Fori(0, more) as w:
                        done = pe.snap(turns_b)
                        pe.wait_ge(s["xoh"], done + 1)
                        sums_of(slot, par, xoh, b_seg[par]).then_inc(s["xseg"], 1)
                        pe.reg_add(turns_b, turns_b, 1)

            def sums(grp, slot, par):
                pe.wait_ge(s["msg_ready"], plus(grp, 1))
                pe.wait_ge(s["acc_done"], plus(grp, 1))
                sums_of(slot, par, oh[par], b_seg[par]).then_inc(s["seg_ready"], 1)

            def load_wait(slot, uses):
                pe.wait_ge(winl[slot], uses)

            def targets_at(grp, slot, par, uses):
                pe.wait_ge(s["ohT_ready"], plus(grp, 1))
                pe.wait_ge(winl[slot], uses)
                pe.wait_ge(s["z_done"], grp)
                for c in range(EC):
                    ins = T.matmul(b_hte[:, c * H:(c + 1) * H], ohT[par][:, c * P:(c + 1) * P], htw[slot][:, :], start=True, stop=True)
                ins.then_inc(s["hte_ready"], 1)

            def targets_first():
                pe.wait_ge(s["ohT_ready"], 1)
                pe.wait_ge(winl[0], 32)
                for c in range(EC):
                    ins = T.matmul(b_hte[:, c * H:(c + 1) * H], ohT[0][:, c * P:(c + 1) * P], htw[0][:, :], start=True, stop=True)
                ins.then_inc(s["hte_ready"], 1)

            targets_first()
            targets_at(1, 1, 1, 32)
            more_targets(0)
            sums(0, 0, 0)
            with pe.Fori(0, GLOOP - 1) as i:
                for j in range(SLOTS):
                    grp = i * SLOTS + (1 + j)
                    nxt = 2 + j
                    targets_at(grp + 1, nxt % SLOTS, nxt % 2, (i + nxt // SLOTS) * 32 + 32)
                    more_targets(grp)
                    more_sums(grp - 1 if j == 0 else i * SLOTS + j, j % SLOTS, j % 2)
                    sums(grp, (1 + j) % SLOTS, (1 + j) % 2)
            for grp in range(1 + (GLOOP - 1) * SLOTS, NG):
                if grp + 1 < NG:
                    targets_at(grp + 1, (grp + 1) % SLOTS, (grp + 1) % 2, ((grp + 1) // SLOTS + 1) * 32)
                more_targets(grp)
                more_sums(grp - 1, (grp - 1) % SLOTS, (grp - 1) % 2)
                sums(grp, grp % SLOTS, grp % 2)
            more_sums(NG - 1, (NG - 1) % SLOTS, (NG - 1) % 2)

            def back(t, k, slot, first):
                pe.wait_ge(s["as_ready"], plus(k * 2, 2))
                if not first:
                    pe.wait_ge(s["asm_done"], plus(k, 1))
                for c in range(KC):
                    T.transpose(bank[slot][:, c * P:(c + 1) * P], fs[slot][:, c, :], ident[:, :])
                T.transpose(bank[slot][:, F:F + H], dn[slot][:, :], ident[0:H, 0:H]).then_inc(s["asm_tr"], 1)
            with pe.Fori(0, NT // 2) as i:
                for j in range(2):
                    back(None, i * 2 + j, j, False)
            back(None, NT - 1, 0, False)

            pe.wait_ge(s["ffn_v"], 64)

            def scores(k, slot):
                pe.wait_ge(s["fs2_ready"], plus(k, 1))
                pe.wait_ge(s["lg_done"], plus(k, 1))
                for c in range(KC):
                    ins = T.matmul(bank[2 + slot][:, 0:NX], fs[slot][:, c, :], wr[:, c, :], start=(c == 0), stop=(c == KC - 1))
                ins.then_inc(s["lg_mm"], 1)
            pe.wait_ge(s["asm_done"], CREDIT + NT)
            with pe.Fori(0, NT // 2) as i:
                for j in range(2):
                    turn(None, i * 2 + j, j, "xs2_ready", None, "tr2_done")
                for j in range(2):
                    scores(i * 2 + j, j)
            turn(None, NT - 1, 0, "xs2_ready", None, "tr2_done")
            scores(NT - 1, 0)

            pe.wait_ge(s["lg_done"], CREDIT + NT)

            def biases(k, slot):
                pe.wait_ge(s["gs_ready"], plus(k, 1))
                T.transpose(bank[slot][0:NX, 0:P], gs[slot][:, :], ident[:, :]).then_inc(s["gt_tr"], 1)
                pe.wait_ge(s["gt_ready"], plus(k, 1))
                pe.wait_ge(s["x2b"], plus(k, 1))
                T.matmul(bank[2 + slot][:, 0:F], gT[slot][:, :], bo[:, :], start=True, stop=True).then_inc(s["bo_mm"], 1)
            with pe.Fori(0, NT // 2) as i:
                for j in range(2):
                    biases(i * 2 + j, j)
            biases(NT - 1, 0)

            pe.wait_ge(s["x2b"], CREDIT + NT)
            pe.wait_ge(s["fr2_copied"], CREDIT + NT)
            pe.wait_ge(s["ffn_w"], 48)

            def first(b, e, n):
                for m in range(KC):
                    pe.wait_ge(s["h1_act"], plus(b * (NX * KC), (e - 1) * KC + m + 2 if e else 1))
                    for k in range(KC):
                        ins = T.matmul(bank[m][:, 0:n], ffn_w[:, 0, e, k, m * P:(m + 1) * P], FR[:, k, cut(b * BLK, n)],
                                       start=(k == 0), stop=(k == KC - 1))
                    ins.then_inc(s["h1_mm"], 1)

            def second(b, e, n):
                pe.wait_ge(s["h1_act"], plus(b * (NX * KC), e * KC + KC + 1))
                pe.wait_ge(s["h2_act"], plus(b * (NX * KC), e * KC + 1))
                for m in range(KC):
                    for k in range(KC):
                        ins = T.matmul(bank[2 + m][:, 0:n], ffn_w[:, 1, e, k, m * P:(m + 1) * P], h1T[e % 2][:, k, 0:n],
                                       start=(k == 0), stop=(k == KC - 1))
                ins.then_inc(s["h2_mm"], 1)

            def third(b, e, tiles):
                pe.wait_ge(s["h2_act"], plus(b * (NX * KC), e * KC + KC + 1))
                pe.wait_ge(s["y_add"], plus(b * (NX * TPB), max(e - 1, 0) * tiles + 1))
                for j in range(tiles):
                    y = bank[4 + 2 * (e % 2) + j // 2][:, (j % 2) * F:(j % 2 + 1) * F]
                    for k in range(KC):
                        ins = T.matmul(y, h2T[e % 2][:, k, j * P:(j + 1) * P], ffn_w[:, 2, e, k, :], start=(k == 0), stop=(k == KC - 1))
                ins.then_inc(s["y_mm"], 1)

            def experts(b, n, tiles):
                first(b, 0, n)
                for e in range(NX):
                    if e + 1 < NX:
                        first(b, e + 1, n)
                    second(b, e, n)
                    if e:
                        third(b, e - 1, tiles)
                third(b, NX - 1, tiles)
            with pe.Fori(0, NB) as b:
                experts(b, BLK, TPB)
            experts(NB, P, 1)

        @block.vector
        def _(dve):
            V = nc.vector
            ch = Chain(dve, s["vchain"])
            link = ch.link
            V.sem_inc(s["g_free"], SLOTS)
            V.sem_inc(s["hp_ready"], 1)
            V.sem_inc(s["y_add"], 1)
            V.sem_inc(s["win_free"], SLOTS)
            V.sem_inc(s["acc_done"], CREDIT)
            V.sem_inc(s["asm_done"], CREDIT)
            V.sem_inc(s["lg_done"], CREDIT)
            V.sem_inc(s["x2b"], CREDIT)

            def rsqrt(y, v, root, count):
                dve.wait_ge(s["rsq_out"], count)
                link(V.reciprocal(y, root))
                newton(y, v, root)

            def newton(y, v, tmp):
                link(V.tensor_tensor(tmp, y, y, ALU.mult))
                link(V.tensor_tensor(tmp, tmp, v, ALU.mult))
                link(V.tensor_scalar(tmp, tmp, -0.5, 1.5, ALU.mult, ALU.add))
                link(V.tensor_tensor(y, y, tmp, ALU.mult))

            dve.wait_ge(s["x_in"], 32)
            first = ch.enter()
            with dve.Fori(0, NT) as t:
                V.bn_stats(stats[:, cut(t, 1), :].rearrange("p a s -> p (a s)"), x_in[:, cut(t, 1), :].rearrange("p a f -> p (a f)")).then_inc(s["vchain"], 1)
            ch.n += NT
            dve.wait_ge(s["vchain"], NT)
            for t in range(NT):
                V.bn_aggr(mv[:, t, :], stats[:, t, :]).then_inc(s["vchain"], 1)
            ch.n += NT
            dve.wait_ge(s["vchain"], 2 * NT)
            var = mv[:, :, 1]
            V.tensor_scalar(nd["t1"], var, LN_EPS, None, ALU.add).then_inc(s["rsq_in"], 1)
            rsqrt(nd["rstd"], nd["t1"], nd["t0"], 1)
            link(V.tensor_tensor(nd["t0"], nd["rstd"], nd["rstd"], ALU.mult))
            link(V.tensor_tensor(nd["t0"], nd["t0"], var, ALU.mult))
            link(V.tensor_scalar(nd["n2"], nd["t0"], float(F), MIN_NORM ** 2, ALU.mult, ALU.max))
            V.tensor_copy(nd["t2"], nd["n2"]).then_inc(s["rsq_in"], 1)
            dve.wait_ge(s["rsq_out"], 2)
            link(V.tensor_scalar(nd["t0"], nd["n"], MAXNORM, None, ALU.min))
            link(V.tensor_scalar(nd["t1"], nd["t0"], -1.0, 1.0, ALU.mult, ALU.add))
            link(V.tensor_scalar(nd["t0"], nd["t0"], 1.0, None, ALU.add))
            link(V.reciprocal(nd["scale"], nd["t1"]))
            V.tensor_tensor(nd["t0"], nd["t0"], nd["scale"], ALU.mult).then_inc(s["ln_in"], 1)
            dve.wait_ge(s["ln_out"], 1)
            link(V.reciprocal(nd["scale"], nd["n"]))
            link(V.tensor_scalar(nd["t1"], nd["t1"], 0.5, None, ALU.mult))
            link(V.tensor_tensor(nd["f0"], nd["t1"], nd["scale"], ALU.mult))
            link(V.tensor_scalar(nd["t2"], nd["n2"], 0.01, None, ALU.min))
            link(V.tensor_scalar(nd["t1"], nd["t2"], 1.0 / 9, 1.0 / 7, ALU.mult, ALU.add))
            for c in (1.0 / 5, 1.0 / 3, 1.0):
                link(V.tensor_tensor(nd["t1"], nd["t1"], nd["t2"], ALU.mult))
                link(V.tensor_scalar(nd["t1"], nd["t1"], c, None, ALU.add))
            link(V.tensor_scalar(nd["t0"], nd["n2"], 0.01, None, ALU.is_lt))
            link(V.tensor_tensor(nd["t1"], nd["t1"], nd["f0"], ALU.subtract))
            link(V.tensor_tensor(nd["t1"], nd["t1"], nd["t0"], ALU.mult))
            link(V.tensor_tensor(nd["f0"], nd["f0"], nd["t1"], ALU.add))
            link(V.reciprocal(nd["inv_f0"], nd["f0"]))
            link(V.tensor_tensor(nd["scale"], nd["rstd"], nd["f0"], ALU.mult))

            dve.wait_ge(s["weights"], 160)
            dve.wait_ge(s["consts"], 6)
            per_chunk = P // DH
            for c in range(KC):
                for q in range(per_chunk):
                    h = c * per_chunk + q
                    rows = slice(q * DH, (q + 1) * DH)
                    ins = V.tensor_copy(ablk[rows, c, h:h + H + 1:H], acol[rows, c:c + 3:2])
            link(ins)
            for c in range(KC):
                ins = V.tensor_scalar(bcolb[:, c, :], ones[:, :], bcol[:, c:c + 1], None, ALU.mult)
            ins.then_inc(s["wa_ready"], 2)
            for q in range(P // 32):
                rows = slice(q * 32, (q + 1) * 32)
                V.tensor_tensor(ip[rows, :, P + q * 32:P + (q + 1) * 32], wpw[rows],
                                mixvec[rows, 2, :][:, :, None].broadcast_to([32, MC, 32]), ALU.mult)
            dve.wait_ge(s["idn"], 1)
            V.tensor_copy(ip[:, :, 0:P], ident[:, None, :].broadcast_to([P, MC, P]))
            V.tensor_copy(row_f[:, :], row_i[:, :])
            link(V.tensor_copy(col_f[:, :], col_i[:, :]))
            V.memset(lneps[:, :], math.log(ATT_EPS))

            dve.wait_ge(s["edges"], 16 * 9)
            V.tensor_copy(dst_f[:, :, :], dst_l[:, :, :])
            V.tensor_reduce(rng_i[:, 0:1], dst_rows, AX.X, ALU.min)
            link(V.tensor_reduce(rng_i[:, 2:3], dst_rows, AX.X, ALU.max))
            link(V.tensor_tensor(rng_i[:, 3:4], rng_i[:, 2:3], rng_i[:, 0:1], ALU.subtract))
            V.tensor_scalar(rng_i[:, 1:2], rng_i[:, 3:4], WSHIFT, None, ALU.arith_shift_right).then_inc(s["rng_ready"], 1)

            def normed(t, k, slot, ready, done, data, mean, scale):
                dve.wait_ge(s[done], plus(k, 1))
                V.tensor_scalar(xs[slot][:, :], data, mean, scale, ALU.subtract, ALU.mult).then_inc(s[ready], 1)

            def norm1(t, slot):
                normed(t, t, slot, "xs_ready", "tr_done", x_in[:, cut(t, 1), :].rearrange("p a f -> p (a f)"),
                       mv[:, cut(t, 1), 0], nd["scale"][:, cut(t, 1)])

            def project(t, slot, use):
                dve.wait_ge(s["proj_mm"], plus(t, 1 + CREDIT))
                dve.wait_ge(tout[slot], plus(use * 16, 16))
                V.scalar_tensor_tensor(out=hst[:, cut(t, 1), :].rearrange("p a f -> p (a f)"), in0=bank[2 + slot][:, F:HW],
                                       scalar=nd["inv_f0"][:, cut(t, 1)], in1=hbias[:, F:HW], op0=ALU.mult, op1=ALU.add)
                V.scalar_tensor_tensor(out=hp[slot][:, :], in0=bank[2 + slot][:, 0:HW],
                                       scalar=nd["inv_f0"][:, cut(t, 1)], in1=hbias[:, :], op0=ALU.mult, op1=ALU.add).then_inc(s["hp_ready"], 1)
            dve.wait_ge(s["wx_ready"], 2)
            with dve.Fori(0, NT // 2) as i:
                for j in range(2):
                    norm1(i * 2 + j, j)
                for j in range(2):
                    project(i * 2 + j, j, i)
            norm1(NT - 1, 0)
            project(NT - 1, 0, NT // 2)
            dve.wait_ge(s["hp_ready"], 1 + NT)

            V.tensor_reduce(mx2[:, 0:1], hst[:, :, 0:H], AX.XY, ALU.max)
            link(V.tensor_reduce(mx2[:, 2:3], hst[:, :, H:2 * H], AX.XY, ALU.max))
            V.tensor_scalar(mx2[:, 1:2], mx2[:, 2:3], 0.0, None, ALU.max).then_inc(s["cm_in"], 1)
            dve.wait_ge(s["cm_tr"], 1)
            V.tensor_reduce(mxr[:, :], b_hte[0:2, 0:P], AX.X, ALU.max).then_inc(s["cm_red"], 1)
            dve.wait_ge(s["cm_mm"], 1)
            link(V.tensor_scalar(tiny[:, 0:1], b_hte[:, 256:257], SLOPE, None, ALU.mult))
            link(V.tensor_tensor(tiny[:, 1:2], tiny[:, 0:1], b_hte[:, 256:257], ALU.max))
            link(V.tensor_scalar(negc[:, :], tiny[:, 1:2], -1.0, None, ALU.mult))
            dve.wait_ge(s["rng_in"], 32)
            link(V.tensor_copy(first_f[:, :], first_i))
            link(V.tensor_scalar(pbase[:, :], first_f[:, :], col_f[:, 0:1], None, ALU.add))
            link(V.tensor_tensor(exs[:, :, :], hst[:, :, 0:H], hst[:, :, H:2 * H], ALU.add))
            V.scalar_tensor_tensor(out=exs[:, :, :], in0=exs[:, :, :], scalar=SLOPE, in1=exs[:, :, :], op0=ALU.mult, op1=ALU.max).then_inc(s["exs_in"], 1)
            link(V.memset(mxe[:, :, :], 0.0))

            def z_stats(b, n):
                for c in range(MC):
                    dve.wait_ge(s["z_copied"], plus(b * MC, c + 1 + 3))
                    V.bn_stats(bstats[:, c, cut(b, 1), :].rearrange("p a s -> p (a s)"), Z[:, c, cut(b * BLK, n)]).then_inc(s["z_stats"], 1)
            with dve.Fori(0, NB) as b:
                z_stats(b, BLK)
            z_stats(NB, LASTB)
            dve.wait_ge(s["z_stats"], (NB + 1) * MC)
            for c in range(MC):
                ins = V.bn_aggr(bmv[:, c, :], bstats[:, c, :, :].rearrange("p b s -> p (b s)"))
            link(ins)
            V.tensor_scalar(baff[:, 1, :], bmv[:, :, 1], BN_EPS, None, ALU.add).then_inc(s["rsq_in"], 1)
            rsqrt(tiny[:, 0:MC], baff[:, 1, :], baff[:, 0, :], 3)
            link(V.tensor_tensor(baff[:, 0, :], tiny[:, 0:MC], mixvec[:, 0, :], ALU.mult))
            link(V.tensor_tensor(tiny[:, 0:MC], baff[:, 0, :], bmv[:, :, 0], ALU.mult))
            V.tensor_tensor(baff[:, 1, :], mixvec[:, 1, :], tiny[:, 0:MC], ALU.subtract).then_inc(s["baff_ready"], 1)

            dve.wait_ge(s["z_mm"], (NB + 1) * MC)
            link(V.memset(FR[:, :, :], 0.0))
            link(V.memset(DEN[:, :], 0.0))

            A2 = ATANH_MAX ** 2

            def mix(t, slot):
                u = U[slot]
                dve.wait_ge(s["u_evac"], plus(t * 3, 3 + 3))
                s1, st, f1, c2, f2 = (tiny[:, i:i + 1] for i in range(5))
                V.tensor_reduce(st, sq6[slot][:, :, :], AX.XY, ALU.add)
                link(V.tensor_reduce(s1, sq6[slot][:, 0, :], AX.X, ALU.add))
                link(V.tensor_scalar(s1, s1, MIN_NORM ** 2, None, ALU.max))
                link(V.reciprocal(f1, s1))
                link(V.tensor_scalar(f1, f1, A2, 1.0, ALU.mult, ALU.min))
                link(V.tensor_scalar(c2, st, f1, MIN_NORM ** 2, ALU.mult, ALU.max))
                link(V.reciprocal(f2, c2))
                link(V.tensor_scalar(f2, f2, A2, 1.0, ALU.mult, ALU.min))
                V.tensor_tensor(nd["fsq"][:, cut(t, 1)], f1, f2, ALU.mult).then_inc(s["fsq_ready"], 1)
                k3 = u[:, 1, :].rearrange("p (g d) -> p g d", d=32)
                q3 = u[:, 0, :].rearrange("p (g d) -> p g d", d=32)
                link(V.tensor_reduce(ksum[:, :], k3, AX.X, ALU.add))
                link(V.tensor_tensor(q3, q3, ksum[:, :, None].broadcast_to([P, 16, 32]), ALU.mult))
                dve.wait_ge(s["eps_ready"], plus(t, 1))
                link(V.tensor_scalar(u[:, 1, :], u[:, 2, :], epsr[slot][:, 1:2], None, ALU.add))
                link(V.reciprocal(u[:, 1, :], u[:, 1, :]))
                link(V.tensor_tensor(u[:, 1, :], u[:, 1, :], u[:, 2, :], ALU.mult))
                V.tensor_tensor(u[:, 0, :], u[:, 0, :], u[:, 1, :], ALU.mult).then_inc(s["o_ready"], 1)

            per = 12 * TPB
            ch.enter()
            with dve.Fori(0, NB) as b:
                ch.turn(b, per)
                for j in range(TPB):
                    mix(plus(b * TPB, j), j % 2)
            ch.leave(NB)
            mix(NT - 1, 0)

            def tile2(buf, t):
                return buf[:, cut(t, 1)].rearrange("p a c n -> p (a c) n")

            dve.wait_ge(s["no2_ready"], CREDIT + NT)
            V.tensor_scalar(nd["t0"], nd["no2"], MIN_NORM ** 2, None, ALU.max).then_inc(s["rsq_in"], 1)
            rsqrt(nd["rs"], nd["t0"], nd["t1"], 4)
            link(V.tensor_scalar(nd["rs"], nd["rs"], ATANH_MAX, None, ALU.mult))
            link(V.tensor_tensor(nd["rs"], nd["rs"], nd["fsq"], ALU.min))
            dve.wait_ge(s["mixed_ready"], 1 + NT)
            with dve.Fori(0, NT) as t:
                m = tile2(mixed, t)
                V.scalar_tensor_tensor(out=m, in0=m, scalar=nd["rs"][:, cut(t, 1)], in1=bres[:, :].rearrange("p (c n) -> p c n", c=KC),
                                       op0=ALU.mult, op1=ALU.add).then_inc(s["ft_ready"], 1)
            dve.wait_ge(s["nf2_ready"], 1 + NT)
            V.tensor_scalar(nd["t0"], nd["nf2"], MIN_NORM ** 2, None, ALU.max).then_inc(s["th_in"], 1)
            dve.wait_ge(s["th_out"], 1)
            link(V.reciprocal(nd["ff"], nd["n"]))
            link(V.tensor_scalar(nd["t1"], nd["t1"], MAXNORM, None, ALU.min))
            link(V.tensor_tensor(nd["ff"], nd["ff"], nd["t1"], ALU.mult))

            turns_a = dve.alloc_register("dve_extra_a")
            turns_b = dve.alloc_register("dve_extra_b")
            dve.reg_mov(turns_a, 0)
            dve.reg_mov(turns_b, 0)
            xohT = junk[0:WIN, :]
            xoh = junk[:, 0:EC * WIN].rearrange("p (c w) -> p c w", c=EC)
            row3 = row_f[:, None, :].broadcast_to([P, EC, WIN])

            def window(grp, slot, par, uses, edges):
                dve.wait_ge(winl[slot], uses)
                V.tensor_scalar(ohT[par][:, 0:edges], dstb[slot][:, 0:edges], pbase[0:WIN, cut(grp, 1)], None, ALU.is_equal).then_inc(s["ohT_ready"], 1)

            def scores(grp, slot, par, uses):
                dve.wait_ge(gath[slot], uses)
                dve.wait_ge(s["hte_ready"], plus(grp, 1))
                V.tensor_tensor(zed[:, :, :], G[slot][:, :, F:F + H], b_hte[:, 0:EC * H].rearrange("p (c h) -> p c h", c=EC), ALU.add).then_inc(s["z_done"], 1)

            def onehot(dst, base, out_):
                return V.scalar_tensor_tensor(out=out_, in0=dst.broadcast_to([P, EC, WIN]), scalar=base, in1=row3, op0=ALU.subtract, op1=ALU.is_equal)

            def targets_of(grp):
                return dst_f[:, cut(grp, 1), :].rearrange("p a c -> p (a c)")[:, :, None]

            def more_scores(grp, slot):
                more = dve.value_load(tab[0:1, cut(plus(grp, 1), 1), 1], min_val=0, max_val=NPAD // WIN)
                with dve.If(more > 0):
                    V.tensor_copy(pcur[:, :], pbase[0:WIN, cut(grp, 1)])
                    with dve.Fori(0, more) as w:
                        done = dve.snap(turns_a)
                        dve.drain()
                        V.tensor_scalar(pcur[:, :], pcur[:, :], float(WIN), None, ALU.add)
                        dve.drain()
                        V.tensor_scalar(xohT, dstb[slot][:, :], pcur[:, 0:1], None, ALU.is_equal).then_inc(s["xoT"], 1)
                        dve.wait_ge(s["xhte"], done + 1)
                        V.tensor_tensor(zed[:, :, :], zed[:, :, :], b_hte[:, 256:256 + EC * H].rearrange("p (c h) -> p c h", c=EC), ALU.add).then_inc(s["xz"], 1)
                        dve.drain()
                        dve.reg_add(turns_a, turns_a, 1)

            def accumulate(seg, base):
                rows = FR[:, :, bass.ds(base, WIN)]
                V.tensor_tensor(rows, rows, seg[:, 0:KC * WIN].rearrange("p (k w) -> p k w", k=KC), ALU.add)
                rows = DEN[:, bass.ds(base, WIN)]
                return V.tensor_tensor(rows, rows, seg[0:H, KC * WIN:(KC + 1) * WIN], ALU.add)

            def collect(grp, slot, par):
                entry = cut(plus(grp, 1), 1)
                d0 = dve.value_load(tab[0:1, entry, 0], min_val=0, max_val=N - 1)
                more = dve.value_load(tab[0:1, entry, 1], min_val=0, max_val=NPAD // WIN)
                dve.wait_ge(s["acc_done"], plus(grp, CREDIT))
                dve.wait_ge(s["seg_ready"], plus(grp, 2))
                accumulate(b_seg[par], d0).then_inc(s["acc_done"], 1)
                with dve.If(more > 0):
                    V.tensor_copy(dcur[:, :], first_f[:, cut(grp, 1)])
                    with dve.Fori(1, more + 1) as w:
                        done = dve.snap(turns_b)
                        base = inside(dve.snap(d0 + w * WIN))
                        dve.drain()
                        V.tensor_scalar(dcur[:, :], dcur[:, :], float(WIN), None, ALU.add)
                        dve.drain()
                        onehot(targets_of(grp), dcur[:, 0:1], xoh).then_inc(s["xoh"], 1)
                        dve.wait_ge(s["xseg"], done + 1)
                        accumulate(b_seg[par], base)
                        dve.drain()
                        dve.reg_add(turns_b, turns_b, 1)
                V.tensor_copy(tiny[:, 11:12], ones[:, 0:1]).then_inc(s["g_free"], 1)

            def maxima(par, parts):
                for rows, cs in parts:
                    ins = V.tensor_tensor(mxe[0:rows, cs, :], mxe[0:rows, cs, :], ex[par][0:rows, cs, :], ALU.max)
                return ins

            def step(grp, slot, par, uses, nxt, before, parts):
                if nxt is not None:
                    window(*nxt)
                scores(grp, slot, par, uses)
                dve.wait_ge(s["z_done"], plus(grp, 1))
                more_scores(grp, slot)
                V.scalar_tensor_tensor(out=zed[:, :, :], in0=zed[:, :, :], scalar=SLOPE, in1=zed[:, :, :], op0=ALU.mult, op1=ALU.max).then_inc(s["zl_ready"], 1)
                onehot(targets_of(grp), first_f[:, cut(grp, 1)], oh[par][:, :, :]).then_inc(s["win_free"], 1)
                if before is not None:
                    collect(*before)
                dve.wait_ge(s["exp_done"], plus(grp, 1))
                maxima(par, parts)
                m3 = G[slot][:, :, 0:F].rearrange("p c (h d) -> p c h d", h=H)
                V.tensor_tensor(m3, m3, ex[par][:, :, :, None].broadcast_to([P, EC, H, DH]), ALU.mult).then_inc(s["msg_ready"], 1)

            whole = [(P, slice(0, EC))]
            rest, part = divmod(LASTE, P)
            V.sem_inc(s["xz"], 1)
            window(0, 0, 0, 32, EG)
            step(0, 0, 0, 64, (1, 1, 1, 32, EG), None, whole)
            with dve.Fori(0, GLOOP - 1) as i:
                for j in range(SLOTS):
                    grp = i * SLOTS + (1 + j)
                    k, nx = 1 + j, 2 + j
                    step(grp, k % SLOTS, k % 2, (i + k // SLOTS) * 64 + 64,
                         (grp + 1, nx % SLOTS, nx % 2, (i + nx // SLOTS) * 32 + 32, EG),
                         (plus(i * SLOTS, j), j % SLOTS, j % 2), whole)
            for grp in range(1 + (GLOOP - 1) * SLOTS, NG):
                nx = grp + 1
                step(grp, grp % SLOTS, grp % 2, (grp // SLOTS + 1) * 64,
                     (nx, nx % SLOTS, nx % 2, (nx // SLOTS + 1) * 32, EG if nx < NG - 1 else LASTE) if nx < NG else None,
                     (grp - 1, (grp - 1) % SLOTS, (grp - 1) % 2),
                     whole if grp < NG - 1 else [(P, slice(0, rest)), (part, slice(rest, rest + 1))])
            collect(NG - 1, (NG - 1) % SLOTS, (NG - 1) % 2)

            dve.wait_ge(s["exs_out"], 1)
            dve.drain()
            V.tensor_reduce(tiny[:, 0:1], mxe[:, :, :], AX.XY, ALU.max)
            V.tensor_reduce(tiny[:, 1:2], exs[:, 0:NT - 1, :], AX.XY, ALU.max)
            link(V.memset(tiny[:, 2:3], 0.0))
            link(V.tensor_reduce(tiny[0:LASTN, 2:3], exs[0:LASTN, NT - 1, :], AX.X, ALU.max))
            V.tensor_reduce(mx2[:, 0:1], tiny[:, 0:3], AX.X, ALU.max).then_inc(s["mx_in"], 1)
            dve.wait_ge(s["mx_all"], 1)
            link(V.tensor_scalar(guard[:, :], mx2[:, 1:2], GAT_EPS, 1e-37, ALU.mult, ALU.max))

            def assemble(t, slot, rows, use):
                y = xs[slot][:, :].rearrange("p (h d) -> p h d", h=H)
                e = exs[:, cut(t, 1), :].rearrange("p a h -> p (a h)")
                dve.wait_ge(s["asm_tr"], plus(t, 1 + CREDIT))
                dve.wait_ge(back_in[slot], plus(use * 32, 32))
                link(V.tensor_tensor(y, hp[slot][:, 0:F].rearrange("p (h d) -> p h d", h=H), e[:, :, None].broadcast_to([P, H, DH]), ALU.mult))
                link(V.scalar_tensor_tensor(out=tiny[:, 0:H], in0=bank[slot][:, F:F + H], scalar=guard[:, 0:1], in1=e, op0=ALU.add, op1=ALU.add))
                link(V.reciprocal(tiny[:, 0:H], tiny[:, 0:H]))
                link(V.tensor_tensor(y, y, bank[slot][:, 0:F].rearrange("p (h d) -> p h d", h=H), ALU.add))
                link(V.tensor_tensor(y, y, tiny[:, 0:H, None].broadcast_to([P, H, DH]), ALU.mult))
                m = tile2(mixed, t)
                link(V.scalar_tensor_tensor(out=m, in0=m, scalar=nd["ff"][:, cut(t, 1)], in1=xs[slot][:, :].rearrange("p (c n) -> p c n", c=KC),
                                            op0=ALU.mult, op1=ALU.add))
                m = m[0:rows]
                V.tensor_tensor(m, m, xr[slot][0:rows, :].rearrange("p (c n) -> p c n", c=KC), ALU.add).then_inc(s["asm_done"], 1)
            ch.enter()
            with dve.Fori(0, NT // 2) as i:
                ch.turn(i, 12)
                for j in range(2):
                    assemble(i * 2 + j, j, P, i)
            ch.leave(NT // 2)
            assemble(NT - 1, 0, LASTN, NT // 2)

            def residual(t):
                V.bn_stats(stats[:, cut(t, 1), :].rearrange("p a s -> p (a s)"), tile2(mixed, t)).then_inc(s["x2_ready"], 1)
            dve.wait_ge(s["asm_done"], CREDIT + NT)
            with dve.Fori(0, NT) as t:
                residual(t)
            dve.wait_ge(s["x2_ready"], NT)
            for t in range(NT):
                V.bn_aggr(mv[:, t, :], stats[:, t, :]).then_inc(s["x2_ready"], 1)
            dve.wait_ge(s["x2_ready"], 2 * NT)
            V.tensor_scalar(nd["t1"], mv[:, :, 1], LN_EPS, None, ALU.add).then_inc(s["rsq_in"], 1)
            rsqrt(nd["rstd"], nd["t1"], nd["t0"], 5)
            dve.wait_ge(s["ffn_v"], 64)
            v_ = fvec[:, 4:10:5, :]
            V.tensor_scalar(ftmp[:, :, :], v_, FBN_EPS, None, ALU.add).then_inc(s["faff_in"], 1)
            link(V.tensor_scalar(fvec[:, 4:10:5, :], v_, FBN_EPS, None, ALU.add))
            dve.wait_ge(s["faff_out"], 1)
            scale_, bias_ = faff[:, 0:4:2, :], faff[:, 1:4:2, :]
            link(V.reciprocal(scale_, ftmp[:, :, :]))
            newton(scale_, v_, ftmp[:, :, :])
            link(V.tensor_tensor(scale_, scale_, fvec[:, 1:10:5, :], ALU.mult))
            link(V.tensor_tensor(bias_, fvec[:, 0:10:5, :], fvec[:, 3:10:5, :], ALU.subtract))
            link(V.tensor_tensor(bias_, bias_, scale_, ALU.mult))
            V.tensor_tensor(bias_, bias_, fvec[:, 2:10:5, :], ALU.add).then_inc(s["faff_out"], 1)

            def norm2(t, slot):
                dve.wait_ge(s["tr2_done"], plus(t, 1))
                V.tensor_scalar(xs[slot][:, :].rearrange("p (c n) -> p c n", c=KC), tile2(mixed, t), mv[:, cut(t, 1), 0],
                                nd["rstd"][:, cut(t, 1)], ALU.subtract, ALU.mult).then_inc(s["xs2_ready"], 1)

            def gate_rows(t, slot):
                dve.wait_ge(s["lg_mm"], plus(t, 1 + CREDIT))
                V.tensor_tensor(gate[:, cut(t, 1), :].rearrange("p a e -> p (a e)"), bank[2 + slot][:, 0:NX], brb[:, :], ALU.add).then_inc(s["lg_done"], 1)
            with dve.Fori(0, NT // 2) as i:
                for j in range(2):
                    norm2(i * 2 + j, j)
                for j in range(2):
                    gate_rows(i * 2 + j, j)
            norm2(NT - 1, 0)
            gate_rows(NT - 1, 0)
            dve.wait_ge(s["lg_done"], CREDIT + NT)
            g3 = gred[:, :, None].broadcast_to([P, NT, NX])
            link(V.tensor_reduce(gred[:, :], gate[:, :, :], AX.X, ALU.max))
            V.tensor_tensor(gate[:, :, :], gate[:, :, :], g3, ALU.subtract).then_inc(s["sm_in"], 1)
            dve.wait_ge(s["sm_out"], 1)
            link(V.tensor_reduce(gred[:, :], gate[:, :, :], AX.X, ALU.add))
            link(V.reciprocal(gred[:, :], gred[:, :]))
            V.tensor_tensor(gate[:, :, :], gate[:, :, :], g3, ALU.mult).then_inc(s["gates"], 1)

            def bias_rows(t, slot):
                dve.wait_ge(s["bo_mm"], plus(t, 1 + CREDIT))
                m = tile2(mixed, t)
                V.tensor_tensor(m, m, bank[2 + slot][:, 0:F].rearrange("p (c n) -> p c n", c=KC), ALU.add).then_inc(s["x2b"], 1)
            with dve.Fori(0, NT // 2) as i:
                for j in range(2):
                    bias_rows(i * 2 + j, j)
            bias_rows(NT - 1, 0)
            dve.wait_ge(s["x2b"], CREDIT + NT)
            dve.wait_ge(s["gates"], 1)

            def experts(b, tiles):
                for e in range(NX):
                    dve.wait_ge(s["y_mm"], plus(b * NX, e + 1 + CREDIT))
                    for j in range(tiles):
                        t = plus(b * TPB, j)
                        if e:
                            dve.wait_ge(s["y_add"], plus(b * (NX * TPB), (e - 1) * tiles + j + 2))
                        m = tile2(mixed, t)
                        y = bank[4 + 2 * (e % 2) + j // 2][:, (j % 2) * F:(j % 2 + 1) * F].rearrange("p (c n) -> p c n", c=KC)
                        V.scalar_tensor_tensor(out=m, in0=y, scalar=gate[:, cut(t, 1), e], in1=m, op0=ALU.mult, op1=ALU.add).then_inc(s["y_add"], 1)
            with dve.Fori(0, NB) as b:
                experts(b, TPB)
            experts(NB, 1)


def _layout(i):
    def g(name):
        return np.asarray(i[name])

    def cols(v):
        return v.reshape(NX, KC, P).transpose(2, 0, 1).reshape(P, NX * KC)

    def chunked(v):
        return v.reshape((2, 4, 3, 32) + v.shape[1:]).swapaxes(1, 2).swapaxes(0, 1)

    def per_partition(v):
        return chunked(v).reshape(MC, P).T

    whole = (NG - 1) * EG
    tail = {k + "_t": g(k)[whole:whole + LASTE // P * P].reshape(LASTE // P, P).T for k in ("src", "dst")}
    arrays = {
        **tail,
        "x": g("x"), "src": g("src"), "dst": g("dst"),
        "src_l": g("src")[:whole].reshape(NG - 1, EC, P).transpose(2, 0, 1),
        "dst_l": g("dst")[:whole].reshape(NG - 1, EC, P).transpose(2, 0, 1),
        "W": g("L0_gnn_W"), "WT": g("L0_gnn_W").T, "b": g("L0_gnn_b"), "bcol": g("L0_gnn_b").reshape(KC, P).T,
        "acol": np.concatenate([g("L0_gnn_a_src").reshape(KC, P).T, g("L0_gnn_a_trg").reshape(KC, P).T], axis=1),
        "wqkv": chunked(g("L0_mix_w_qkv")[:, :, 2]).reshape(C2, F).T,
        "wpw": g("L0_mix_w_pw")[:, :, 0].reshape(2, 4, 3, 32, 32).transpose(1, 4, 2, 0, 3).reshape(P, MC, 32),
        "mixvec": np.stack([per_partition(g("L0_mix_bn_gamma")), per_partition(g("L0_mix_bn_beta")),
                            per_partition(g("L0_mix_w_dw")[:, 0, 2])], axis=1),
        "wres": g("L0_mix_w_res")[:, :, 0].T, "b_res": g("L0_mix_b_res"),
        "fvec": np.stack([cols(g("L0_ffn_" + n)) for n in ("b1", "g1", "be1", "m1", "v1", "b2", "g2", "be2", "m2", "v2")], axis=1),
        "W1": g("L0_ffn_W1"), "W2": g("L0_ffn_W2"), "Wo": g("L0_ffn_Wo"),
        "Wr": g("L0_ffn_Wr"), "br": g("L0_ffn_br"), "bo": g("L0_ffn_bo"),
    }
    return {k: np.ascontiguousarray(v) for k, v in arrays.items()}


def kernel(**inputs):
    import concourse.bacc as bacc
    from concourse.bass_utils import run_bass_kernel_spmd

    nc = bacc.Bacc("TRN2", target_bir_lowering=False, num_devices=1)
    arrays = _layout(inputs)
    args = {k: nc.dram_tensor(f"in_{k}", v.shape, mybir.dt.from_np(v.dtype), kind="ExternalInput").ap() for k, v in arrays.items()}
    out = nc.dram_tensor("out", (N, F), F32, kind="ExternalOutput").ap()
    program(nc, args, out)
    r = run_bass_kernel_spmd(nc, [{f"in_{k}": v for k, v in arrays.items()}], core_ids=[0])
    return r.results[0]["out"]
```

```python
import math
from contextlib import ExitStack

import numpy as np

import concourse.bass as bass
from concourse import mybir

F32 = mybir.dt.float32
I32 = mybir.dt.int32
ALU = mybir.AluOpType
ACT = mybir.ActivationFunctionType
AX = mybir.AxisListType

P = 128
N = 3125
E = 50000
F = 256
KC = F // P
H = 8
DH = F // H
NT = -(-N // P)
LASTN = N - (NT - 1) * P
NPAD = NT * P
BLK = 512
NB = N // BLK
TPB = BLK // P
LASTB = N - NB * BLK
HW = F + 2 * H
C2 = 768
MC = C2 // P
OC = 512
NX = 8
LN_EPS, BN_EPS, FBN_EPS, ATT_EPS, GAT_EPS = 1e-5, 1e-5, 1e-3, 1e-15, 1e-10
MIN_NORM = 1e-15
MAXNORM = float(np.float32(1.0 - 1e-5))
ATANH_MAX = math.atanh(MAXNORM)
SLOPE = 0.2

EC = 8
EG = EC * P
NG = -(-E // EG)
LASTE = E - (NG - 1) * EG
ACOLS = F + H
TSHIFT = P.bit_length() - 1
PAD_DST = -1000000
SLOTS = 4
GPT = 2
UNITS = 2
PASSES = (NT - 1) // UNITS
assert GPT * (NT - 1) == NG - 1 and PASSES * UNITS == NT - 1 and SLOTS == GPT * UNITS

CREDIT = 2


def plus(a, b):
    if isinstance(b, int) and b == 0:
        return a
    if isinstance(a, int) and a == 0:
        return b
    return a + b


def at(base, k, size):
    return bass.ds(plus(base * size, k), size) if not isinstance(base, int) else slice(base * size + k, base * size + k + size)


def cut(start, size):
    return slice(start, start + size) if isinstance(start, int) else bass.ds(start, size)


class Chain:

    def __init__(self, eng, sem):
        self.eng, self.sem, self.base, self.n = eng, sem, 0, 0

    def link(self, ins):
        ins.then_inc(self.sem, 1)
        self.n += 1
        self.eng.wait_ge(self.sem, plus(self.base, self.n))

    def enter(self):
        self.first = plus(self.base, self.n)
        return self.first

    def turn(self, i, per, start=0):
        self.base, self.n, self.per = plus(i * per, self.first - start * per), 0, per

    def leave(self, passes):
        assert self.n == self.per, (self.n, self.per)
        self.base, self.n = self.first + passes * self.per, 0


def program(nc, a, out):
    with ExitStack() as ctx:
        def sb(name, shape, dt=F32):
            return ctx.enter_context(nc.sbuf_tensor(name, shape, dt))

        def sem(name):
            return ctx.enter_context(nc.semaphore(name))

        table = nc.dram_tensor("projected_rows", [NPAD, HW], F32, kind="Internal").ap()
        ranges = nc.dram_tensor("group_ranges", [2 * NG], I32, kind="Internal").ap()
        firsts = nc.dram_tensor("group_firsts", [2 * NG], I32, kind="Internal").ap()

        bank = [ctx.enter_context(nc.psum_tensor(f"bank{i}", [P, 512], F32)) for i in range(8)]
        b_q, b_k, b_v, b_o, b_r, b_hte = bank[:6]
        b_seg = bank[6:8]

        Z = sb("Z", [P, MC, NPAD])
        zflat = Z[:, :, :].rearrange("p c n -> p (c n)")
        x_in = zflat[:, 4 * NPAD:4 * NPAD + NT * F].rearrange("p (t f) -> p t f", f=F)
        mixed = Z[:, 0:2, :].rearrange("p c (t n) -> p t c n", n=P)
        ffn_w = zflat[:, 2 * NPAD:2 * NPAD + 3 * NX * KC * F].rearrange("p (m e k f) -> p m e k f", m=3, e=NX, k=KC)
        frows = sb("frows", [P, (NT + 1) * ACOLS])
        FR = frows[:, 0:KC * NPAD].rearrange("p (k n) -> p k n", k=KC)
        ACC = frows[:, :].rearrange("p (t f) -> p t f", f=ACOLS)
        hst = sb("hst", [P, NT + 1, 2 * H])
        G = [sb(f"G{i}", [P, EC, HW]) for i in range(SLOTS)]
        tt_all = sb("TT", [P, 2 * MC * P])
        TT = [tt_all[:, i * MC * P:(i + 1) * MC * P].rearrange("p (c n) -> p c n", c=MC) for i in range(2)]
        wqkv = tt_all[:, :].rearrange("p (k n) -> p k n", k=KC)
        ip = sb("ip", [P, MC + 1, P])
        ident = ip[:, 0, :]
        wres = sb("wres", [P, OC // P, F])
        acol = sb("acol", [P, 4])
        bcol = sb("bcol", [P, KC])
        mixvec = sb("mixvec", [P, 3, MC])
        bres = sb("bres", [P, F])
        ones = sb("ones", [P, P])
        row_f = sb("row_f", [P, P])
        col_i = sb("col_i", [P, 1], I32)
        col_f = sb("col_f", [P, 1])
        early = [G[i][:, :, :].bitcast(I32).rearrange("p c n -> p (c n)") for i in range(SLOTS)]
        dst_rows = early[3][0:NG, 0:EG]
        dst_l = early[2][:, 0:NG * EC].rearrange("p (g c) -> p g c", c=EC)
        mod_l = early[2][:, NG * EC:2 * NG * EC].rearrange("p (g c) -> p g c", c=EC)
        src_l = sb("src_l", [P, NG, EC], I32)
        idx = [sb(f"idx{i}", [P, EC], I32) for i in range(SLOTS)]
        dst_f = sb("dst_f", [P, NG, EC])
        mod_f = sb("mod_f", [P, NG, EC])
        key = sb("key", [P, NG, EC])
        rng_i = sb("rng_i", [NG, 6], I32)
        tab = sb("tab", [1, NG, 2], I32)
        first_i = early[1][:, 0:NG]
        firstm_i = early[1][:, NG:2 * NG]
        row_i = early[1][:, 128:256]
        first_f = sb("first_f", [P, NG])
        firstm = sb("firstm", [P, NG])
        below = sb("below", [P, NG])
        above = sb("above", [P, NG])
        target = sb("target", [P, NG])
        dcur = sb("dcur", [P, 2])
        xkey = sb("xkey", [P, EC])
        xtmp = sb("xtmp", [P, EC])
        dstb = [sb(f"dstb{i}", [P, EG], I32) for i in range(2)]
        hsel = [sb(f"hsel{i}", [P, H]) for i in range(2)]
        htmp = sb("htmp", [P, H])
        ohT = [sb(f"ohT{i}", [P, EG]) for i in range(2)]
        oh = [sb(f"oh{i}", [P, EC, P]) for i in range(2)]
        hp = [oh[i][:, :, :].rearrange("p c w -> p (c w)")[:, F:F + HW] for i in range(2)]
        wx = ohT[0][:, 0:KC * HW].rearrange("p (k n) -> p k n", k=KC)
        hbias = ohT[0][:, KC * HW:(KC + 1) * HW]
        fs = [ohT[1][:, i * F:(i + 1) * F].rearrange("p (k n) -> p k n", k=KC) for i in range(2)]
        xs = [ohT[1][:, (2 + i) * F:(3 + i) * F] for i in range(2)]
        zed = [sb(f"zed{i}", [P, EC, H]) for i in range(2)]
        mxe = sb("mxe", [P, EC, H])
        exs = sb("exs", [P, NT, H])
        mx2 = sb("mx2", [P, 4])
        mxr = sb("mxr", [2, 1])
        negc = sb("negc", [P, 1])
        guard = sb("guard", [P, 1])
        stats = sb("stats", [P, NT, 6])
        mv = sb("mv", [P, NT, 2])
        bmv = sb("bmv", [P, MC, 2])
        baff = sb("baff", [P, 2, MC])
        nodes = sb("nodes", [P, 16, NT])
        xr = [oh[i][:, :, :].rearrange("p c w -> p (c w)")[:, 0:F] for i in range(2)]
        U = [sb(f"U{i}", [P, 3, 512]) for i in range(2)]
        bstats = U[0][:, 0, 0:MC * (NB + 1) * 6].rearrange("p (c b s) -> p c b s", c=MC, s=6)
        oT = sb("oT", [P, 512])
        junk = sb("junk", [P, 512])
        fvec = U[0][:, 0, 0:10 * KC * NX].rearrange("p (v e) -> p v e", v=10)
        ftmp = U[0][:, 0, 160:160 + 2 * KC * NX].rearrange("p (v e) -> p v e", v=2)
        faff = U[0][:, 0, 192:192 + 4 * KC * NX].rearrange("p (v e) -> p v e", v=4)
        gs = [U[0][:, 0, 256 + i * NX:256 + (i + 1) * NX] for i in range(2)]
        gate = U[0][:, 1, 0:NT * NX].rearrange("p (t e) -> p t e", e=NX)
        bo = U[1][0:NX, 0, 0:F]
        gT = [U[1][0:NX, 1, i * P:(i + 1) * P] for i in range(2)]
        spill = [junk[:, :].bitcast(mybir.dt.bfloat16)[:, i * F:(i + 1) * F].rearrange("p (h c) -> p h c", h=2) for i in range(4)]
        wT = junk[:, :].rearrange("p (c n) -> p c n", c=KC)
        bcolb = oT[:, 0:256].rearrange("p (c m) -> p c m", c=KC)
        wpw = oT[:, 256:256 + MC * 32].rearrange("p (c o) -> p c o", c=MC)
        ablk = sb("ablk", [P, KC, 2 * H])
        sq6 = [sb(f"sq6{i}", [P, 2, 3]) for i in range(2)]
        tiny = sb("tiny", [P, 12])
        epsr = [sb(f"epsr{i}", [P, 2]) for i in range(2)]
        lneps = sb("lneps", [P, 1])
        ksum = sb("ksum", [P, 16])
        wr = sb("wr", [P, KC, NX])
        brb = sb("brb", [P, NX])
        gred = sb("gred", [P, NT])
        h1T, h2T = ([G[i + j][:, :, :].rearrange("p c n -> p (c n)")[:, 0:KC * BLK].rearrange("p (k n) -> p k n", k=KC)
                     for i in range(2)] for j in (0, 2))

        names = ("rstd f0 inv_f0 n2 n t0 t1 t2 fsq no2 rs nf2 ff scale").split()
        nd = {k: nodes[:, i, :] for i, k in enumerate(names)}

        s = {k: sem(k) for k in (
            "x_pad x_in weights edge_fill edges idn consts vchain achain gchain rsq_in rsq_out "
            "xs_ready tr_done fs_ready proj_mm hp_ready fr_copied wa_ready wa_mm wx_ready "
            "rng_ready rng_out rng_in ln_in ln_out cm_in cm_tr cm_red cm_mm exs_in exs_out "
            "z_mm z_copied z_stats baff_ready tt_ready u_mm u_evac fsq_ready eps_ready o_ready o_tr oT_ready "
            "r_mm mixed_ready no2_ready fr_clear "
            "ohT_ready hte_ready z_done zl_ready exp_done msg_ready seg_ready acc_done g_free idx_ready dstb_free hsel_tmp "
            "xoT xhte xoh xseg oh_order mx_in mx_all "
            "asm_done ft_ready nf2_ready th_in th_out x2_ready xs2_ready tr2_done fs2_ready fr2_copied "
            "lg_mm lg_done sm_in sm_out gates gs_ready gt_tr gt_ready bo_mm x2b "
            "ffn_w ffn_v faff_in faff_out h1_mm h1_act h2_mm h2_act y_mm y_add out_done").split()}
        gath = [sem(f"gath{i}") for i in range(SLOTS)]
        tout = [sem(f"tout{i}") for i in range(2)]
        back_in = [sem(f"back_in{i}") for i in range(2)]
        dstl = [sem(f"dstl{i}") for i in range(2)]

        block = ctx.enter_context(nc.Block())

        @block.sync
        def _(sp):
            nc.sync.sem_inc(tout[0], 16)
            nc.sync.sem_inc(tout[1], 16)
            sp.wait_ge(s["x_pad"], 1)
            full = (NT - 1) * P
            sp.dma_start(x_in[:, 0:NT - 1, :], a["x"][0:full, :].rearrange("(t p) f -> p t f", p=P)).then_inc(s["x_in"], 16)
            sp.dma_start(x_in[0:LASTN, NT - 1, :], a["x"][full:N, :]).then_inc(s["x_in"], 16)
            for dst, src in (
                (wx[:, :, 0:F], a["W"].rearrange("(k p) n -> p k n", p=P)),
                (wT, a["WT"].rearrange("(c p) i -> p c i", p=P)),
                (acol[:, :], a["acol"]), (bcol[:, :], a["bcol"]),
                (hbias[:, 0:F], a["b"][None, :].broadcast_to([P, F])),
                (wqkv, a["wqkv"].rearrange("(k p) n -> p k n", p=P)),
                (wpw, a["wpw"]), (mixvec[:, :, :], a["mixvec"]),
                (wres[:, :, :], a["wres"].rearrange("(c p) n -> p c n", p=P)),
                (bres[:, :], a["b_res"][None, :].broadcast_to([P, F])),
            ):
                sp.dma_start(dst, src).then_inc(s["weights"], 16)
            sp.wait_ge(s["edge_fill"], 2)
            whole = (NG - 1) * EG
            sp.dma_start(dst_rows[0:NG - 1, :], a["dst"][0:whole].rearrange("(g e) -> g e", e=EG)).then_inc(s["edges"], 16)
            sp.dma_start(dst_rows[NG - 1:NG, 0:LASTE], a["dst"][whole:E][None, :]).then_inc(s["edges"], 16)
            sp.dma_start(dst_rows[NG - 1:NG, LASTE:EG], a["dst"][whole:whole + EG - LASTE][None, :]).then_inc(s["edges"], 16)
            rest, part = divmod(LASTE, P)
            for buf, lay, raw in ((src_l, "src_l", "src"), (dst_l, "dst_l", "dst")):
                sp.dma_start(buf[:, 0:NG - 1, :], a[lay]).then_inc(s["edges"], 16)
                sp.dma_start(buf[:, NG - 1, 0:rest], a[raw + "_t"]).then_inc(s["edges"], 16)
                sp.dma_start(buf[0:part, NG - 1, rest:rest + 1], a[raw][whole + rest * P:E][:, None]).then_inc(s["edges"], 16)
            sp.wait_ge(s["rng_ready"], 1)
            sp.dma_start(ranges.rearrange("(g c) -> g c", c=2), rng_i[:, 0:2]).then_inc(s["rng_out"], 16)
            for c in range(2):
                sp.dma_start(firsts[c * NG:(c + 1) * NG][:, None], rng_i[:, 2 + c:3 + c]).then_inc(s["rng_out"], 16)
            sp.wait_ge(s["rng_out"], 48)
            sp.dma_start(tab[:, :, :], ranges.rearrange("(a g c) -> a g c", a=1, c=2)).then_inc(s["rng_in"], 16)
            sp.dma_start(first_i, firsts[None, 0:NG].broadcast_to([P, NG])).then_inc(s["rng_in"], 16)
            sp.dma_start(firstm_i, firsts[None, NG:2 * NG].broadcast_to([P, NG])).then_inc(s["rng_in"], 16)
            def table_rows(t, slot):
                sp.wait_ge(s["hp_ready"], plus(t, 2))
                sp.dma_start(table[cut(t * P, P), :], hp[slot][:, :]).then_inc(tout[slot], 16)
            with sp.Fori(0, NT // 2) as i:
                for j in range(2):
                    table_rows(plus(i * 2, j), j)
            table_rows(NT - 1, 0)

            def targets(g, slot, edges):
                sp.wait_ge(s["dstb_free"], plus(g, 1))
                sp.dma_start(dstb[slot][:, 0:edges], a["dst"][cut(g * EG, edges)][None, :].broadcast_to([P, edges])).then_inc(dstl[slot], 16)
            with sp.Fori(0, (NG - 1) // 2) as i:
                for j in range(2):
                    targets(i * 2 + j, j, EG)
            targets(NG - 1, 0, LASTE)

            sp.wait_ge(s["tt_ready"], NT)
            for m, w in enumerate(("W1", "W2", "Wo")):
                sp.dma_start(ffn_w[:, m], a[w].rearrange("e (k p) f -> p e k f", p=P)).then_inc(s["ffn_w"], 16)
            sp.wait_ge(s["no2_ready"], CREDIT + NT)
            sp.wait_ge(s["o_tr"], CREDIT + NT)
            for dst, src in ((fvec[:, :, :], a["fvec"]), (wr[:, :, :], a["Wr"].rearrange("(k p) e -> p k e", p=P)),
                             (brb[:, :], a["br"][None, :].broadcast_to([P, NX])), (bo[:, :], a["bo"])):
                sp.dma_start(dst, src).then_inc(s["ffn_v"], 16)
            def residual_rows(t, slot, rows):
                sp.wait_ge(s["asm_done"], plus(t, 1))
                sp.dma_start(xr[slot][0:rows, :], a["x"][cut(t * P, rows), :]).then_inc(back_in[slot], 16)
                sp.dma_start(hp[slot][:, :], table[cut(t * P, P), :]).then_inc(back_in[slot], 16)
            sp.wait_ge(s["seg_ready"], 1 + NG)
            with sp.Fori(0, NT // 2) as i:
                for j in range(2):
                    residual_rows(plus(i * 2, j), j, P)
            residual_rows(NT - 1, 0, LASTN)

            def store(t, k, rows, need):
                sp.wait_ge(s["y_add"], plus(need, 1))
                sp.dma_start(out[cut(t * P, rows), :].rearrange("n (c f) -> n c f", c=KC), mixed_rows(t, rows)).then_inc(s["out_done"], 16)

            def mixed_rows(t, rows):
                return mixed[0:rows, t] if isinstance(t, int) else mixed[0:rows, bass.ds(t, 1)].rearrange("p a c n -> p (a c) n")

            with sp.Fori(0, NB) as b:
                for j in range(TPB):
                    store(b * TPB + j, None, P, plus(b * (TPB * NX), (NX - 1) * TPB + j + 1))
            store(NT - 1, None, LASTN, NB * TPB * NX + NX)
            sp.wait_ge(s["out_done"], 16 * NT)

        @block.gpsimd
        def _(pool):
            g = nc.gpsimd
            chain = Chain(pool, s["gchain"])
            g.memset(x_in[:, NT - 1, :], 0.0).then_inc(s["x_pad"], 1)
            g.memset(src_l[:, NG - 1, :], 0).then_inc(s["edge_fill"], 1)
            g.memset(dst_l[:, NG - 1, :], PAD_DST).then_inc(s["edge_fill"], 1)
            g.memset(ones[:, :], 1.0).then_inc(s["consts"], 1)
            g.memset(ablk[:, :, :], 0.0).then_inc(s["consts"], 1)
            g.memset(ip[:, 1:MC + 1, :], 0.0).then_inc(s["consts"], 1)
            chain.link(g.memset(ident[:, :], 0.0))
            g.iota(row_i, pattern=[[1, P]], base=0, channel_multiplier=0).then_inc(s["consts"], 1)
            g.iota(col_i[:, :], pattern=[[0, 1]], base=0, channel_multiplier=1).then_inc(s["consts"], 1)
            g.affine_select(out=ident[:, :], in_=ident[:, :], compare_op=ALU.not_equal, fill=1.0, base=0,
                            pattern=[[-1, P]], channel_multiplier=1).then_inc(s["idn"], 1)

            def keep(t, k, slot):
                pool.wait_ge(s["fs_ready"], plus(k, 1))
                g.tensor_copy(FR[:, :, cut(t * P, P)], fs[slot][:, :, :]).then_inc(s["fr_copied"], 1)
            g.sem_inc(s["fr_copied"], CREDIT)
            with pool.Fori(0, NT // 2) as i:
                for j in range(2):
                    keep(i * 2 + j, i * 2 + j, j)
            keep(NT - 1, NT - 1, 0)

            def sources(grp, slot, uses):
                if not isinstance(uses, int) or uses:
                    pool.wait_ge(gath[slot], uses)
                g.tensor_copy(idx[slot][:, :], src_l[:, cut(grp, 1), :].rearrange("p a c -> p (a c)")).then_inc(s["idx_ready"], 1)

            def gather(grp, slot, nxt):
                pool.wait_ge(s["idx_ready"], plus(grp, 1))
                pool.wait_ge(s["g_free"], plus(grp, 1))
                if nxt is not None:
                    sources(*nxt)
                for c in range(EC):
                    g.indirect_dma_start(
                        out=G[slot][:, c, :], out_offset=None, in_=table[:, :],
                        in_offset=bass.IndirectOffsetOnAxis(ap=idx[slot][:, c:c + 1], axis=0),
                    ).then_inc(gath[slot], 16)
            pool.wait_ge(s["edges"], 16 * 9)
            pool.wait_ge(tout[0], 16 * (1 + NT - NT // 2))
            pool.wait_ge(tout[1], 16 * (1 + NT // 2))
            pool.wait_ge(s["exs_in"], 1)
            sources(0, 0, 0)
            def with_next(grp, static, i, j):
                gather(grp, static % SLOTS, (plus(grp, 1), (static + 1) % SLOTS, plus(i * (16 * EC), (j + 1) // SLOTS * (16 * EC))))
            for g_ in range(SLOTS):
                with_next(g_, g_, 0, g_)
            with pool.Fori(1, PASSES - 1) as i:
                for j in range(SLOTS):
                    with_next(plus(i * SLOTS, j), j, i, j)
            for g_ in range((PASSES - 1) * SLOTS, NG - 1):
                with_next(g_, g_, g_ // SLOTS, g_ % SLOTS)
            gather(NG - 1, (NG - 1) % SLOTS, None)

            pool.wait_ge(s["mx_in"], 1)
            g.partition_all_reduce(mx2[:, 1:2], mx2[:, 0:1], P, bass.bass_isa.ReduceOp.max).then_inc(s["mx_all"], 1)

            def keep2(t, k, slot):
                pool.wait_ge(s["fs2_ready"], plus(k, 1))
                g.tensor_copy(FR[:, :, cut(t * P, P)], fs[slot][:, :, :]).then_inc(s["fr2_copied"], 1)
            g.sem_inc(s["fr2_copied"], CREDIT)
            with pool.Fori(0, NT // 2) as i:
                for j in range(2):
                    keep2(i * 2 + j, i * 2 + j, j)
            keep2(NT - 1, NT - 1, 0)

            pool.wait_ge(s["gates"], 1)

            def gates(t, k, slot):
                pool.wait_ge(s["gt_tr"], plus(k, 1))
                g.tensor_copy(gs[slot][:, :], gate[:, cut(t, 1), :].rearrange("p a e -> p (a e)")).then_inc(s["gs_ready"], 1)
            with pool.Fori(0, NT // 2) as i:
                for j in range(2):
                    gates(i * 2 + j, i * 2 + j, j)
            gates(NT - 1, NT - 1, 0)

        @block.scalar
        def _(act):
            A = nc.scalar
            A.sem_inc(s["z_copied"], 3)
            A.sem_inc(s["oT_ready"], 1)
            A.sem_inc(s["mixed_ready"], 1)
            A.sem_inc(s["nf2_ready"], 1)
            A.sem_inc(s["h1_act"], 1)
            A.sem_inc(s["h2_act"], 1)
            A.sem_inc(s["u_evac"], 3)
            A.sem_inc(s["no2_ready"], CREDIT)
            act.wait_ge(s["rsq_in"], 1)
            A.activation(nd["t0"], nd["t1"], ACT.Sqrt).then_inc(s["rsq_out"], 1)
            act.wait_ge(s["rsq_in"], 2)
            A.activation(nd["n"], nd["n2"], ACT.Sqrt).then_inc(s["rsq_out"], 1)
            act.wait_ge(s["ln_in"], 1)
            A.activation(nd["t1"], nd["t0"], ACT.Ln).then_inc(s["ln_out"], 1)

            act.wait_ge(s["wa_mm"], 1)
            A.copy(wx[:, :, F:HW], b_r[:, 0:KC * 2 * H].rearrange("p (k h) -> p k h", k=KC)).then_inc(s["wx_ready"], 1)
            A.copy(hbias[:, F:HW], b_r[:, 64:64 + 2 * H]).then_inc(s["wx_ready"], 1)

            def features(t, k, slot):
                act.wait_ge(s["tr_done"], plus(k, 1 + CREDIT))
                act.wait_ge(s["proj_mm"], plus(k, 1))
                act.wait_ge(s["fr_copied"], plus(k, 1))
                A.copy(fs[slot][:, :, :], bank[slot][:, 0:F].rearrange("p (k n) -> p k n", k=KC)).then_inc(s["fs_ready"], 1)
            with act.Fori(0, NT // 2) as i:
                for j in range(2):
                    features(i * 2 + j, i * 2 + j, j)
            features(NT - 1, NT - 1, 0)

            act.wait_ge(s["exs_in"], 1)
            A.activation(exs[:, :, :], exs[:, :, :], ACT.Exp, bias=negc[:, 0:1]).then_inc(s["exs_out"], 1)

            def z_copy(b, n):
                for c in range(MC):
                    act.wait_ge(s["z_mm"], plus(b * MC, c + 1))
                    A.copy(Z[:, c, cut(b * BLK, n)], bank[c % 3][:, 0:n]).then_inc(s["z_copied"], 1)
            with act.Fori(0, NB) as b:
                z_copy(b, BLK)
            z_copy(NB, P)
            act.wait_ge(s["rsq_in"], 3)
            A.activation(baff[:, 0, :], baff[:, 1, :], ACT.Sqrt).then_inc(s["rsq_out"], 1)

            act.wait_ge(s["baff_ready"], 1)

            def batch_norm(t, slot, free):
                if free is not None:
                    act.wait_ge(s["u_mm"], free)
                for c in range(MC):
                    ins = A.activation(TT[slot][:, c, :], Z[:, c, cut(t * P, P)], ACT.Relu,
                                       bias=baff[:, 1, c:c + 1], scale=baff[:, 0, c:c + 1])
                ins.then_inc(s["tt_ready"], 1)

            def squares(t, slot):
                act.wait_ge(s["o_tr"], plus(t, 1))
                act.wait_ge(s["no2_ready"], plus(t, 1))
                for m in range(3):
                    act.wait_ge(s["u_mm"], plus(t * 3, m + 2))
                    act.wait_ge(s["u_evac"], plus(t * 3, m + 2))
                    src = bank[m][:, :].rearrange("p (h s c) -> p h s c", h=2, s=2)
                    A.activation(U[slot][:, m, :], bank[m][:, :], ACT.Copy if m == 2 else ACT.Relu)
                    for part in range(2):
                        ins = A.activation(spill[((slot * 3 + m) % 2) * 2 + part], src[:, :, part, :], ACT.Square,
                                           accum_out=sq6[slot][:, part, m:m + 1])
                    ins.then_inc(s["u_evac"], 1)

            def epsilon(t, slot):
                act.wait_ge(s["fsq_ready"], plus(t, 1))
                A.activation(epsr[slot][:, 0:1], nd["fsq"][:, cut(t, 1)], ACT.Ln).then_inc(s["achain"], 1)
                act.wait_ge(s["achain"], plus(t, 1))
                A.activation(epsr[slot][:, 1:2], epsr[slot][:, 0:1], ACT.Exp, scale=-0.5, bias=lneps[:, 0:1]).then_inc(s["eps_ready"], 1)

            def out_features(t, slot):
                act.wait_ge(s["o_ready"], plus(t, 1))
                A.activation(U[slot][:, 1, :], U[slot][:, 0, :], ACT.Square, accum_out=nd["no2"][:, cut(t, 1)]).then_inc(s["no2_ready"], 1)
                act.wait_ge(s["o_tr"], plus(t, 1 + CREDIT))
                act.wait_ge(s["r_mm"], plus(t, 1))
                A.copy(oT[:, :], b_o[:, :]).then_inc(s["oT_ready"], 1)

            def mixed_out(t):
                act.wait_ge(s["r_mm"], plus(t, 2))
                A.copy(mixed[:, cut(t, 1)].rearrange("p a c n -> p (a c) n"),
                       b_r[:, 0:F].rearrange("p (c n) -> p c n", c=KC)).then_inc(s["mixed_ready"], 1)

            def exponentials(g, slot, par):
                act.wait_ge(s["zl_ready"], plus(g, 1))
                A.activation(G[slot][:, :, F:F + H], zed[par][:, :, :], ACT.Exp, bias=negc[:, 0:1]).then_inc(s["exp_done"], 1)

            def unit(t, v, before=2, groups=GPT, last=False):
                g = t * GPT
                if groups:
                    if not last:
                        exponentials(plus(g, 1), (GPT * v + 1) % SLOTS, 1)
                if before >= 1:
                    epsilon(plus(t, -1), 1 - v)
                if groups:
                    squares(t, v)
                if groups and not last:
                    exponentials(plus(g, 2), (GPT * v + 2) % SLOTS, 0)
                    batch_norm(plus(t, 1), 1 - v, plus(t * 3, 1) if not isinstance(t, int) or t else None)
                if before >= 1:
                    out_features(plus(t, -1), 1 - v)
                if before >= 2:
                    mixed_out(plus(t, -2))

            batch_norm(0, 0, None)
            exponentials(0, 0, 0)
            for v in range(UNITS):
                unit(v, v, before=v)
            with act.Fori(1, PASSES) as i:
                for v in range(UNITS):
                    unit(plus(i * UNITS, v), v)
            unit(NT - 1, 0, last=True)
            unit(NT, 1, groups=0)
            mixed_out(NT - 1)

            act.wait_ge(s["rsq_in"], 4)
            A.activation(nd["t1"], nd["t0"], ACT.Sqrt).then_inc(s["rsq_out"], 1)

            def norms(t, k):
                act.wait_ge(s["ft_ready"], plus(k, 1))
                act.wait_ge(s["nf2_ready"], plus(k, 1))
                A.activation(junk[:, 0:F].rearrange("p (c n) -> p c n", c=KC), mixed[:, cut(t, 1)].rearrange("p a c n -> p (a c) n"),
                             ACT.Square, accum_out=nd["nf2"][:, cut(t, 1)]).then_inc(s["nf2_ready"], 1)
            with act.Fori(0, NT) as i:
                norms(i, i)
            act.wait_ge(s["th_in"], 1)
            A.activation(nd["n"], nd["t0"], ACT.Sqrt).then_inc(s["achain"], 1)
            act.wait_ge(s["achain"], NT + 1)
            A.activation(nd["t1"], nd["n"], ACT.Tanh).then_inc(s["th_out"], 1)
            act.wait_ge(s["rsq_in"], 5)
            A.activation(nd["t0"], nd["t1"], ACT.Sqrt).then_inc(s["rsq_out"], 1)
            act.wait_ge(s["faff_in"], 1)
            A.activation(ftmp[:, :, :], ftmp[:, :, :], ACT.Sqrt).then_inc(s["faff_out"], 1)

            def features2(t, k, slot):
                act.wait_ge(s["tr2_done"], plus(k, 1 + CREDIT))
                act.wait_ge(s["lg_mm"], plus(k, 1))
                act.wait_ge(s["fr2_copied"], plus(k, 1))
                A.copy(fs[slot][:, :, :], bank[slot][:, 0:F].rearrange("p (k n) -> p k n", k=KC)).then_inc(s["fs2_ready"], 1)
            with act.Fori(0, NT // 2) as i:
                for j in range(2):
                    features2(i * 2 + j, i * 2 + j, j)
            features2(NT - 1, NT - 1, 0)
            act.wait_ge(s["sm_in"], 1)
            A.activation(gate[:, :, :], gate[:, :, :], ACT.Exp).then_inc(s["sm_out"], 1)

            def gates(t, k, slot):
                act.wait_ge(s["gt_tr"], plus(k, 1 + CREDIT))
                act.wait_ge(s["bo_mm"], plus(k, 1))
                A.copy(gT[slot][:, :], bank[slot][0:NX, 0:P]).then_inc(s["gt_ready"], 1)
            with act.Fori(0, NT // 2) as i:
                for j in range(2):
                    gates(i * 2 + j, i * 2 + j, j)
            gates(NT - 1, NT - 1, 0)

            def first(b, e, n):
                for m in range(KC):
                    act.wait_ge(s["h1_mm"], plus(b * (NX * KC), e * KC + m + 1))
                    if m == 0:
                        act.wait_ge(s["h2_mm"], plus(b * NX, e + 1))
                    A.activation(h1T[e % 2][:, m, 0:n], bank[m][:, 0:n], ACT.Relu, bias=faff[:, 1, e * KC + m:e * KC + m + 1],
                                 scale=faff[:, 0, e * KC + m:e * KC + m + 1]).then_inc(s["h1_act"], 1)

            def second(b, e, n):
                for m in range(KC):
                    act.wait_ge(s["h2_mm"], plus(b * NX, e + 1 + CREDIT))
                    if m == 0:
                        act.wait_ge(s["y_mm"], plus(b * NX, e + 1))
                    A.activation(h2T[e % 2][:, m, 0:n], bank[2 + m][:, 0:n], ACT.Relu, bias=faff[:, 3, e * KC + m:e * KC + m + 1],
                                 scale=faff[:, 2, e * KC + m:e * KC + m + 1]).then_inc(s["h2_act"], 1)

            def experts(b, n):
                first(b, 0, n)
                for e in range(NX):
                    if e + 1 < NX:
                        first(b, e + 1, n)
                    second(b, e, n)
            act.wait_ge(s["faff_out"], 2)
            with act.Fori(0, NB) as b:
                experts(b, BLK)
            experts(NB, P)

        @block.tensor
        def _(pe):
            T = nc.tensor
            T.sem_inc(s["tr_done"], CREDIT)
            T.sem_inc(s["seg_ready"], 1)
            T.sem_inc(s["r_mm"], 1)
            T.sem_inc(s["u_mm"], 1)
            T.sem_inc(s["proj_mm"], CREDIT)
            T.sem_inc(s["o_tr"], CREDIT)
            T.sem_inc(s["tr2_done"], CREDIT)
            T.sem_inc(s["lg_mm"], CREDIT)
            T.sem_inc(s["gt_tr"], CREDIT)
            T.sem_inc(s["bo_mm"], CREDIT)
            T.sem_inc(s["h2_mm"], CREDIT)
            T.sem_inc(s["y_mm"], CREDIT)

            pe.wait_ge(s["wa_ready"], 2)
            for k in range(KC):
                for c in range(KC):
                    T.matmul(b_r[:, k * 2 * H:(k + 1) * 2 * H], wT[:, c, k * P:(k + 1) * P], ablk[:, c, :], start=(c == 0), stop=(c == KC - 1))
            for c in range(KC):
                ins = T.matmul(b_r[:, 64:64 + 2 * H], bcolb[:, c, :], ablk[:, c, :], start=(c == 0), stop=(c == KC - 1))
            ins.then_inc(s["wa_mm"], 1)
            pe.wait_ge(s["idn"], 1)

            def turn(t, k, slot, ready, free, done):
                pe.wait_ge(s[ready], plus(k, 1))
                if free is not None:
                    pe.wait_ge(s[free], k)
                for c in range(KC):
                    ins = T.transpose(bank[slot][:, c * P:(c + 1) * P], xs[slot][:, c * P:(c + 1) * P], ident[:, :])
                ins.then_inc(s[done], 1)

            def project(k, slot):
                pe.wait_ge(s["fs_ready"], plus(k, 1))
                pe.wait_ge(s["hp_ready"], plus(k, 1))
                for c in range(KC):
                    ins = T.matmul(bank[2 + slot][:, 0:HW], fs[slot][:, c, :], wx[:, c, :], start=(c == 0), stop=(c == KC - 1))
                ins.then_inc(s["proj_mm"], 1)

            pe.wait_ge(s["wx_ready"], 2)
            with pe.Fori(0, NT // 2) as i:
                for j in range(2):
                    turn(None, i * 2 + j, j, "xs_ready", None, "tr_done")
                for j in range(2):
                    pe.wait_ge(s["fs_ready"], i * 2 + (j + 1))
                    if j == 0:
                        pe.wait_ge(s["hp_ready"], i * 2 + 1)
                    for c in range(KC):
                        ins = T.matmul(bank[2 + j][:, 0:HW], fs[j][:, c, :], wx[:, c, :], start=(c == 0), stop=(c == KC - 1))
                    ins.then_inc(s["proj_mm"], 1)
            turn(None, NT - 1, 0, "xs_ready", None, "tr_done")
            project(NT - 1, 0)

            pe.wait_ge(s["cm_in"], 1)
            T.transpose(b_hte[0:2, 0:P], mx2[:, 0:2], ident[:, :]).then_inc(s["cm_tr"], 1)
            pe.wait_ge(s["cm_red"], 1)
            T.matmul(b_hte[:, 256:257], ones[0:2, :], mxr[:, :], start=True, stop=True).then_inc(s["cm_mm"], 1)

            pe.wait_ge(s["fr_copied"], NT + CREDIT)
            pe.wait_ge(s["hp_ready"], 1 + NT)

            def channels(b, n):
                for c in range(MC):
                    pe.wait_ge(s["z_copied"], plus(b * MC, c + 1))
                    for k in range(KC):
                        ins = T.matmul(bank[c % 3][:, 0:n], wqkv[:, k, c * P:(c + 1) * P], FR[:, k, cut(b * BLK, n)],
                                       start=(k == 0), stop=(k == KC - 1))
                    ins.then_inc(s["z_mm"], 1)
            with pe.Fori(0, NB) as b:
                channels(b, BLK)
            channels(NB, P)

            pe.wait_ge(s["z_copied"], 3 + (NB + 1) * MC)

            def u_rows(t, slot):
                pe.wait_ge(s["tt_ready"], plus(t, 1))
                for m in range(3):
                    pe.wait_ge(s["u_evac"], plus(t * 3, m + 1))
                    for h in range(2):
                        c = 2 * m + h
                        ins = T.matmul(bank[m][:, h * 256:(h + 1) * 256], TT[slot][:, c, :], ip[:, 0:c + 2:c + 1, :], start=True, stop=True)
                    ins.then_inc(s["u_mm"], 1)

            def out_features(t, slot):
                pe.wait_ge(s["o_ready"], plus(t, 1))
                pe.wait_ge(s["oT_ready"], plus(t, 1))
                for c in range(4):
                    ins = T.transpose(b_o[:, c * P:(c + 1) * P], U[slot][:, 0, c * P:(c + 1) * P], ident[:, :])
                ins.then_inc(s["o_tr"], 1)

            def mixed_out(t):
                pe.wait_ge(s["oT_ready"], plus(t, 2))
                pe.wait_ge(s["mixed_ready"], plus(t, 1))
                for c in range(4):
                    half, src = divmod(c, 2)
                    ins = T.matmul(b_r[:, 0:F], oT[:, c * P:(c + 1) * P], wres[:, 2 * src + half, :], start=(c == 0), stop=(c == 3))
                ins.then_inc(s["r_mm"], 1)

            turns_a = pe.alloc_register("pe_extra_a")
            turns_b = pe.alloc_register("pe_extra_b")
            pe.reg_mov(turns_a, 0)
            pe.reg_mov(turns_b, 0)

            def per_edge(par, first_col):
                for c in range(EC):
                    ins = T.matmul(b_hte[:, first_col + c * H:first_col + (c + 1) * H], ohT[par][:, c * P:(c + 1) * P], hsel[par][:, :],
                                   start=True, stop=True)
                return ins

            def targets(g, par):
                pe.wait_ge(s["ohT_ready"], plus(g, 1))
                if not (isinstance(g, int) and g == 0):
                    pe.wait_ge(s["zl_ready"], g)
                per_edge(par, 0).then_inc(s["hte_ready"], 1)

            def sums_of(slot, par):
                for c in range(EC):
                    ins = T.matmul(b_seg[par][:, 0:ACOLS], oh[par][:, c, :], G[slot][:, c, 0:ACOLS], start=(c == 0), stop=(c == EC - 1))
                return ins

            def more_targets(g, par):
                more = pe.value_load(tab[0:1, cut(g, 1), 1], min_val=0, max_val=NPAD // P)
                with pe.If(more > 0):
                    with pe.Fori(0, more) as w:
                        done = pe.snap(turns_a)
                        pe.wait_ge(s["xoT"], done + 1)
                        per_edge(par, 256).then_inc(s["xhte"], 1)
                        pe.reg_add(turns_a, turns_a, 1)

            def more_sums(g, slot, par):
                more = pe.value_load(tab[0:1, cut(g, 1), 1], min_val=0, max_val=NPAD // P)
                with pe.If(more > 0):
                    with pe.Fori(0, more) as w:
                        done = pe.snap(turns_b)
                        pe.wait_ge(s["xoh"], done + 1)
                        sums_of(slot, par).then_inc(s["xseg"], 1)
                        pe.reg_add(turns_b, turns_b, 1)

            def step(g, k, first=False, left=3):
                par = k % 2
                if left >= 1:
                    more_targets(plus(g, 1), 1 - par)
                if left >= 2:
                    targets(plus(g, 2), par)
                if not first:
                    more_sums(plus(g, -1), (k - 1) % SLOTS, 1 - par)
                pe.wait_ge(s["msg_ready"], plus(g, 1))
                pe.wait_ge(s["acc_done"], plus(g, 1))
                sums_of(k % SLOTS, par).then_inc(s["seg_ready"], 1)

            def unit(t, v, before=2, lefts=(3, 3)):
                g = t * GPT
                if before >= 2:
                    mixed_out(plus(t, -2))
                if lefts:
                    u_rows(t, v)
                    step(g, GPT * v, first=isinstance(t, int) and t == 0, left=lefts[0])
                if before >= 1:
                    out_features(plus(t, -1), 1 - v)
                if len(lefts) > 1:
                    step(plus(g, 1), GPT * v + 1, left=lefts[1])

            targets(0, 0)
            more_targets(0, 0)
            targets(1, 1)
            for v in range(UNITS):
                unit(v, v, before=v)
            with pe.Fori(1, PASSES - 1) as i:
                for v in range(UNITS):
                    unit(plus(i * UNITS, v), v)
            for t in range(NT - 1 - UNITS, NT - 1):
                unit(t, t % UNITS, lefts=(3, 3) if t < NT - 2 else (2, 1))
            unit(NT - 1, 0, lefts=(0,))
            more_sums(NG - 1, (NG - 1) % SLOTS, 0)
            unit(NT, 1, lefts=())
            mixed_out(NT - 1)

            pe.wait_ge(s["ffn_v"], 64)

            def scores(k, slot):
                pe.wait_ge(s["fs2_ready"], plus(k, 1))
                pe.wait_ge(s["lg_done"], plus(k, 1))
                for c in range(KC):
                    ins = T.matmul(bank[2 + slot][:, 0:NX], fs[slot][:, c, :], wr[:, c, :], start=(c == 0), stop=(c == KC - 1))
                ins.then_inc(s["lg_mm"], 1)
            pe.wait_ge(s["asm_done"], CREDIT + NT)
            with pe.Fori(0, NT // 2) as i:
                for j in range(2):
                    turn(None, i * 2 + j, j, "xs2_ready", None, "tr2_done")
                for j in range(2):
                    scores(i * 2 + j, j)
            turn(None, NT - 1, 0, "xs2_ready", None, "tr2_done")
            scores(NT - 1, 0)

            pe.wait_ge(s["lg_done"], CREDIT + NT)

            def biases(k, slot):
                pe.wait_ge(s["gs_ready"], plus(k, 1))
                T.transpose(bank[slot][0:NX, 0:P], gs[slot][:, :], ident[:, :]).then_inc(s["gt_tr"], 1)
                pe.wait_ge(s["gt_ready"], plus(k, 1))
                pe.wait_ge(s["x2b"], plus(k, 1))
                T.matmul(bank[2 + slot][:, 0:F], gT[slot][:, :], bo[:, :], start=True, stop=True).then_inc(s["bo_mm"], 1)
            with pe.Fori(0, NT // 2) as i:
                for j in range(2):
                    biases(i * 2 + j, j)
            biases(NT - 1, 0)

            pe.wait_ge(s["x2b"], CREDIT + NT)
            pe.wait_ge(s["fr2_copied"], CREDIT + NT)
            pe.wait_ge(s["ffn_w"], 48)

            def first(b, e, n):
                for m in range(KC):
                    pe.wait_ge(s["h1_act"], plus(b * (NX * KC), (e - 1) * KC + m + 2 if e else 1))
                    for k in range(KC):
                        ins = T.matmul(bank[m][:, 0:n], ffn_w[:, 0, e, k, m * P:(m + 1) * P], FR[:, k, cut(b * BLK, n)],
                                       start=(k == 0), stop=(k == KC - 1))
                    ins.then_inc(s["h1_mm"], 1)

            def second(b, e, n):
                pe.wait_ge(s["h1_act"], plus(b * (NX * KC), e * KC + KC + 1))
                pe.wait_ge(s["h2_act"], plus(b * (NX * KC), e * KC + 1))
                for m in range(KC):
                    for k in range(KC):
                        ins = T.matmul(bank[2 + m][:, 0:n], ffn_w[:, 1, e, k, m * P:(m + 1) * P], h1T[e % 2][:, k, 0:n],
                                       start=(k == 0), stop=(k == KC - 1))
                ins.then_inc(s["h2_mm"], 1)

            def third(b, e, tiles):
                pe.wait_ge(s["h2_act"], plus(b * (NX * KC), e * KC + KC + 1))
                pe.wait_ge(s["y_add"], plus(b * (NX * TPB), max(e - 1, 0) * tiles + 1))
                for j in range(tiles):
                    y = bank[4 + 2 * (e % 2) + j // 2][:, (j % 2) * F:(j % 2 + 1) * F]
                    for k in range(KC):
                        ins = T.matmul(y, h2T[e % 2][:, k, j * P:(j + 1) * P], ffn_w[:, 2, e, k, :], start=(k == 0), stop=(k == KC - 1))
                ins.then_inc(s["y_mm"], 1)

            def experts(b, n, tiles):
                first(b, 0, n)
                for e in range(NX):
                    if e + 1 < NX:
                        first(b, e + 1, n)
                    second(b, e, n)
                    if e:
                        third(b, e - 1, tiles)
                third(b, NX - 1, tiles)
            with pe.Fori(0, NB) as b:
                experts(b, BLK, TPB)
            experts(NB, P, 1)

        @block.vector
        def _(dve):
            V = nc.vector
            ch = Chain(dve, s["vchain"])
            link = ch.link
            V.sem_inc(s["g_free"], SLOTS)
            V.sem_inc(s["hp_ready"], 1)
            V.sem_inc(s["y_add"], 1)
            V.sem_inc(s["dstb_free"], 2)
            V.sem_inc(s["acc_done"], CREDIT)
            V.sem_inc(s["asm_done"], CREDIT)
            V.sem_inc(s["lg_done"], CREDIT)
            V.sem_inc(s["x2b"], CREDIT)

            def rsqrt(y, v, root, count):
                dve.wait_ge(s["rsq_out"], count)
                link(V.reciprocal(y, root))
                newton(y, v, root)

            def newton(y, v, tmp):
                link(V.tensor_tensor(tmp, y, y, ALU.mult))
                link(V.tensor_tensor(tmp, tmp, v, ALU.mult))
                link(V.tensor_scalar(tmp, tmp, -0.5, 1.5, ALU.mult, ALU.add))
                link(V.tensor_tensor(y, y, tmp, ALU.mult))

            dve.wait_ge(s["x_in"], 32)
            first = ch.enter()
            with dve.Fori(0, NT) as t:
                V.bn_stats(stats[:, cut(t, 1), :].rearrange("p a s -> p (a s)"), x_in[:, cut(t, 1), :].rearrange("p a f -> p (a f)")).then_inc(s["vchain"], 1)
            ch.n += NT
            dve.wait_ge(s["vchain"], NT)
            for t in range(NT):
                V.bn_aggr(mv[:, t, :], stats[:, t, :]).then_inc(s["vchain"], 1)
            ch.n += NT
            dve.wait_ge(s["vchain"], 2 * NT)
            var = mv[:, :, 1]
            V.tensor_scalar(nd["t1"], var, LN_EPS, None, ALU.add).then_inc(s["rsq_in"], 1)
            rsqrt(nd["rstd"], nd["t1"], nd["t0"], 1)
            link(V.tensor_tensor(nd["t0"], nd["rstd"], nd["rstd"], ALU.mult))
            link(V.tensor_tensor(nd["t0"], nd["t0"], var, ALU.mult))
            link(V.tensor_scalar(nd["n2"], nd["t0"], float(F), MIN_NORM ** 2, ALU.mult, ALU.max))
            V.tensor_copy(nd["t2"], nd["n2"]).then_inc(s["rsq_in"], 1)
            dve.wait_ge(s["rsq_out"], 2)
            link(V.tensor_scalar(nd["t0"], nd["n"], MAXNORM, None, ALU.min))
            link(V.tensor_scalar(nd["t1"], nd["t0"], -1.0, 1.0, ALU.mult, ALU.add))
            link(V.tensor_scalar(nd["t0"], nd["t0"], 1.0, None, ALU.add))
            link(V.reciprocal(nd["scale"], nd["t1"]))
            V.tensor_tensor(nd["t0"], nd["t0"], nd["scale"], ALU.mult).then_inc(s["ln_in"], 1)
            dve.wait_ge(s["ln_out"], 1)
            link(V.reciprocal(nd["scale"], nd["n"]))
            link(V.tensor_scalar(nd["t1"], nd["t1"], 0.5, None, ALU.mult))
            link(V.tensor_tensor(nd["f0"], nd["t1"], nd["scale"], ALU.mult))
            link(V.tensor_scalar(nd["t2"], nd["n2"], 0.01, None, ALU.min))
            link(V.tensor_scalar(nd["t1"], nd["t2"], 1.0 / 9, 1.0 / 7, ALU.mult, ALU.add))
            for c in (1.0 / 5, 1.0 / 3, 1.0):
                link(V.tensor_tensor(nd["t1"], nd["t1"], nd["t2"], ALU.mult))
                link(V.tensor_scalar(nd["t1"], nd["t1"], c, None, ALU.add))
            link(V.tensor_scalar(nd["t0"], nd["n2"], 0.01, None, ALU.is_lt))
            link(V.tensor_tensor(nd["t1"], nd["t1"], nd["f0"], ALU.subtract))
            link(V.tensor_tensor(nd["t1"], nd["t1"], nd["t0"], ALU.mult))
            link(V.tensor_tensor(nd["f0"], nd["f0"], nd["t1"], ALU.add))
            link(V.reciprocal(nd["inv_f0"], nd["f0"]))
            link(V.tensor_tensor(nd["scale"], nd["rstd"], nd["f0"], ALU.mult))

            dve.wait_ge(s["weights"], 160)
            dve.wait_ge(s["consts"], 5)
            per_chunk = P // DH
            for c in range(KC):
                for q in range(per_chunk):
                    h = c * per_chunk + q
                    rows = slice(q * DH, (q + 1) * DH)
                    ins = V.tensor_copy(ablk[rows, c, h:h + H + 1:H], acol[rows, c:c + 3:2])
            link(ins)
            for c in range(KC):
                ins = V.tensor_scalar(bcolb[:, c, :], ones[:, :], bcol[:, c:c + 1], None, ALU.mult)
            ins.then_inc(s["wa_ready"], 2)
            for q in range(P // 32):
                rows = slice(q * 32, (q + 1) * 32)
                V.tensor_tensor(ip[rows, 1:MC + 1, q * 32:(q + 1) * 32], wpw[rows],
                                mixvec[rows, 2, :][:, :, None].broadcast_to([32, MC, 32]), ALU.mult)
            dve.wait_ge(s["idn"], 1)
            V.tensor_copy(row_f[:, :], row_i)
            link(V.tensor_copy(col_f[:, :], col_i[:, :]))
            V.memset(lneps[:, :], math.log(ATT_EPS))

            dve.wait_ge(s["edges"], 16 * 9)
            V.tensor_copy(dst_f[:, :, :], dst_l[:, :, :])
            V.tensor_scalar(mod_l, dst_l, P - 1, None, ALU.bitwise_and)
            link(V.tensor_reduce(rng_i[:, 4:5], dst_rows, AX.X, ALU.max))
            link(V.tensor_reduce(rng_i[:, 2:3], dst_rows, AX.X, ALU.min))
            V.tensor_copy(mod_f[:, :, :], mod_l)
            V.tensor_scalar(rng_i[:, 3:4], rng_i[:, 2:3], P - 1, None, ALU.bitwise_and)
            V.tensor_scalar(rng_i[:, 0:1], rng_i[:, 2:3], TSHIFT, None, ALU.arith_shift_right)
            link(V.tensor_tensor(rng_i[:, 5:6], rng_i[:, 4:5], rng_i[:, 2:3], ALU.subtract))
            V.tensor_scalar(rng_i[:, 1:2], rng_i[:, 5:6], TSHIFT, None, ALU.arith_shift_right).then_inc(s["rng_ready"], 1)

            def window_key(out_, offset, column, order):
                order(V.scalar_tensor_tensor(out=out_, in0=offset, scalar=0.0, in1=column, op0=ALU.is_ge, op1=ALU.mult))
                order(V.scalar_tensor_tensor(out=out_, in0=offset, scalar=float(P), in1=out_, op0=ALU.is_lt, op1=ALU.mult))
                order(V.tensor_scalar(out_, out_, -1.0, None, ALU.add))

            def normed(t, k, slot, ready, done, data, mean, scale):
                dve.wait_ge(s[done], plus(k, 1))
                V.tensor_scalar(xs[slot][:, :], data, mean, scale, ALU.subtract, ALU.mult).then_inc(s[ready], 1)

            def norm1(t, slot):
                normed(t, t, slot, "xs_ready", "tr_done", x_in[:, cut(t, 1), :].rearrange("p a f -> p (a f)"),
                       mv[:, cut(t, 1), 0], nd["scale"][:, cut(t, 1)])

            def project(t, slot, use):
                dve.wait_ge(s["proj_mm"], plus(t, 1 + CREDIT))
                dve.wait_ge(tout[slot], plus(use * 16, 16))
                V.scalar_tensor_tensor(out=hst[:, cut(t, 1), :].rearrange("p a f -> p (a f)"), in0=bank[2 + slot][:, F:HW],
                                       scalar=nd["inv_f0"][:, cut(t, 1)], in1=hbias[:, F:HW], op0=ALU.mult, op1=ALU.add)
                V.scalar_tensor_tensor(out=hp[slot][:, :], in0=bank[2 + slot][:, 0:HW],
                                       scalar=nd["inv_f0"][:, cut(t, 1)], in1=hbias[:, :], op0=ALU.mult, op1=ALU.add).then_inc(s["hp_ready"], 1)
            dve.wait_ge(s["wx_ready"], 2)
            with dve.Fori(0, NT // 2) as i:
                for j in range(2):
                    norm1(i * 2 + j, j)
                for j in range(2):
                    project(i * 2 + j, j, i)
            norm1(NT - 1, 0)
            project(NT - 1, 0, NT // 2)
            dve.wait_ge(s["hp_ready"], 1 + NT)

            V.tensor_reduce(mx2[:, 0:1], hst[:, 0:NT, 0:H], AX.XY, ALU.max)
            link(V.tensor_reduce(mx2[:, 2:3], hst[:, 0:NT, H:2 * H], AX.XY, ALU.max))
            V.tensor_scalar(mx2[:, 1:2], mx2[:, 2:3], 0.0, None, ALU.max).then_inc(s["cm_in"], 1)
            dve.wait_ge(s["cm_tr"], 1)
            V.tensor_reduce(mxr[:, :], b_hte[0:2, 0:P], AX.X, ALU.max).then_inc(s["cm_red"], 1)
            dve.wait_ge(s["cm_mm"], 1)
            link(V.tensor_scalar(tiny[:, 0:1], b_hte[:, 256:257], SLOPE, None, ALU.mult))
            link(V.tensor_tensor(tiny[:, 1:2], tiny[:, 0:1], b_hte[:, 256:257], ALU.max))
            link(V.tensor_scalar(negc[:, :], tiny[:, 1:2], -1.0, None, ALU.mult))
            dve.wait_ge(s["rng_in"], 48)
            V.tensor_copy(firstm[:, :], firstm_i)
            link(V.tensor_copy(first_f[:, :], first_i))
            link(V.tensor_scalar(below[:, :], firstm[:, :], col_f[:, 0:1], None, ALU.is_gt))
            V.tensor_scalar(above[:, :], below[:, :], -1.0, 1.0, ALU.mult, ALU.add)
            link(V.tensor_tensor(target[:, :], first_f[:, :], firstm[:, :], ALU.subtract))
            link(V.tensor_scalar(target[:, :], target[:, :], col_f[:, 0:1], None, ALU.add))
            link(V.scalar_tensor_tensor(out=target[:, :], in0=below[:, :], scalar=float(P), in1=target[:, :], op0=ALU.mult, op1=ALU.add))
            link(V.tensor_tensor(dst_f[:, :, :], dst_f[:, :, :], first_f[:, :, None].broadcast_to([P, NG, EC]), ALU.subtract))
            link(V.tensor_scalar(mod_f[:, :, :], mod_f[:, :, :], 1.0, None, ALU.add))
            window_key(key[:, :, :], dst_f[:, :, :], mod_f[:, :, :], link)
            link(V.tensor_tensor(exs[:, :, :], hst[:, 0:NT, 0:H], hst[:, 0:NT, H:2 * H], ALU.add))
            V.scalar_tensor_tensor(out=exs[:, :, :], in0=exs[:, :, :], scalar=SLOPE, in1=exs[:, :, :], op0=ALU.mult, op1=ALU.max).then_inc(s["exs_in"], 1)
            link(V.memset(mxe[:, :, :], 0.0))
            link(V.memset(hst[:, NT, :], 0.0))

            def z_stats(b, n):
                for c in range(MC):
                    dve.wait_ge(s["z_copied"], plus(b * MC, c + 1 + 3))
                    V.bn_stats(bstats[:, c, cut(b, 1), :].rearrange("p a s -> p (a s)"), Z[:, c, cut(b * BLK, n)]).then_inc(s["z_stats"], 1)
            with dve.Fori(0, NB) as b:
                z_stats(b, BLK)
            z_stats(NB, LASTB)
            dve.wait_ge(s["z_stats"], (NB + 1) * MC)
            for c in range(MC):
                ins = V.bn_aggr(bmv[:, c, :], bstats[:, c, :, :].rearrange("p b s -> p (b s)"))
            link(ins)
            V.tensor_scalar(baff[:, 1, :], bmv[:, :, 1], BN_EPS, None, ALU.add).then_inc(s["rsq_in"], 1)
            rsqrt(tiny[:, 0:MC], baff[:, 1, :], baff[:, 0, :], 3)
            link(V.tensor_tensor(baff[:, 0, :], tiny[:, 0:MC], mixvec[:, 0, :], ALU.mult))
            link(V.tensor_tensor(tiny[:, 0:MC], baff[:, 0, :], bmv[:, :, 0], ALU.mult))
            V.tensor_tensor(baff[:, 1, :], mixvec[:, 1, :], tiny[:, 0:MC], ALU.subtract).then_inc(s["baff_ready"], 1)

            dve.wait_ge(s["z_mm"], (NB + 1) * MC)
            link(V.memset(ACC[:, :, :], 0.0))

            A2 = ATANH_MAX ** 2

            def factors(t, slot):
                u = U[slot]
                dve.wait_ge(s["u_evac"], plus(t * 3, 3 + 3))
                s1, st, f1, c2, f2 = (tiny[:, i:i + 1] for i in range(5))
                V.tensor_reduce(st, sq6[slot][:, :, :], AX.XY, ALU.add)
                link(V.tensor_reduce(s1, sq6[slot][:, 0, :], AX.X, ALU.add))
                k3 = u[:, 1, :].rearrange("p (g d) -> p g d", d=32)
                q3 = u[:, 0, :].rearrange("p (g d) -> p g d", d=32)
                V.tensor_reduce(ksum[:, :], k3, AX.X, ALU.add)
                link(V.tensor_scalar(s1, s1, MIN_NORM ** 2, None, ALU.max))
                link(V.reciprocal(f1, s1))
                link(V.tensor_scalar(f1, f1, A2, 1.0, ALU.mult, ALU.min))
                link(V.tensor_scalar(c2, st, f1, MIN_NORM ** 2, ALU.mult, ALU.max))
                link(V.reciprocal(f2, c2))
                link(V.tensor_scalar(f2, f2, A2, 1.0, ALU.mult, ALU.min))
                V.tensor_tensor(nd["fsq"][:, cut(t, 1)], f1, f2, ALU.mult).then_inc(s["fsq_ready"], 1)
                link(V.tensor_tensor(q3, q3, ksum[:, :, None].broadcast_to([P, 16, 32]), ALU.mult))

            def outputs(t, slot):
                u = U[slot]
                dve.wait_ge(s["eps_ready"], plus(t, 1))
                link(V.tensor_scalar(u[:, 1, :], u[:, 2, :], epsr[slot][:, 1:2], None, ALU.add))
                link(V.reciprocal(u[:, 1, :], u[:, 1, :]))
                link(V.tensor_tensor(u[:, 1, :], u[:, 1, :], u[:, 2, :], ALU.mult))
                V.tensor_tensor(u[:, 0, :], u[:, 0, :], u[:, 1, :], ALU.mult).then_inc(s["o_ready"], 1)

            turns_a = dve.alloc_register("dve_extra_a")
            turns_b = dve.alloc_register("dve_extra_b")
            dve.reg_mov(turns_a, 0)
            dve.reg_mov(turns_b, 0)

            def first_tile(g):
                return dve.value_load(tab[0:1, cut(g, 1), 0], min_val=0, max_val=NT - 1)

            def later_windows(g):
                return dve.value_load(tab[0:1, cut(g, 1), 1], min_val=0, max_val=NPAD // P)

            def column(buf, g):
                return buf[:, cut(g, 1)]

            def drained(ins):
                dve.drain()

            def h_trg_of_window(g, par, tile, order):
                order(V.tensor_scalar(htmp[:, :], hst[:, bass.ds(tile + 1, 1), H:2 * H].rearrange("p a h -> p (a h)"), column(below, g), None, ALU.mult))
                return V.scalar_tensor_tensor(out=hsel[par][:, :], in0=hst[:, bass.ds(tile, 1), H:2 * H].rearrange("p a h -> p (a h)"),
                                              scalar=column(above, g), in1=htmp[:, :], op0=ALU.mult, op1=ALU.add)

            def window(g, par, uses, edges):
                tile = first_tile(g)
                dve.wait_ge(dstl[par], uses)
                if not (isinstance(g, int) and g == 0):
                    dve.wait_ge(s["ohT_ready"], g)
                V.tensor_scalar(htmp[:, :], hst[:, bass.ds(tile + 1, 1), H:2 * H].rearrange("p a h -> p (a h)"), column(below, g), None,
                                ALU.mult).then_inc(s["hsel_tmp"], 1)
                V.tensor_scalar(ohT[par][:, 0:edges], dstb[par][:, 0:edges], column(target, g), None, ALU.is_equal)
                dve.wait_ge(s["hsel_tmp"], plus(g, 1))
                V.scalar_tensor_tensor(out=hsel[par][:, :], in0=hst[:, bass.ds(tile, 1), H:2 * H].rearrange("p a h -> p (a h)"),
                                       scalar=column(above, g), in1=htmp[:, :], op0=ALU.mult, op1=ALU.add).then_inc(s["ohT_ready"], 1)

            def scores(g, slot, par, uses):
                z = zed[par][:, :, :]
                dve.wait_ge(gath[slot], uses)
                dve.wait_ge(s["hte_ready"], plus(g, 1))
                V.tensor_tensor(z, G[slot][:, :, F:F + H], b_hte[:, 0:EC * H].rearrange("p (c h) -> p c h", c=EC), ALU.add).then_inc(s["z_done"], 1)
                more = later_windows(g)
                with dve.If(more > 0):
                    V.memset(dcur[:, 0:1], 0.0)
                    with dve.Fori(1, more + 1) as w:
                        done = dve.snap(turns_a)
                        tile = nc.s_assert_within(dve.snap(first_tile(g) + w), 0, NT - 1,
                                                  skip_runtime_bounds_check_because="a group's last window starts at or before its last target")
                        dve.drain()
                        V.tensor_scalar(dcur[:, 0:1], dcur[:, 0:1], float(P), None, ALU.add)
                        dve.drain()
                        V.tensor_tensor(dcur[:, 1:2], column(target, g), dcur[:, 0:1], ALU.add)
                        dve.drain()
                        V.tensor_scalar(ohT[par][:, :], dstb[par][:, :], dcur[:, 1:2], None, ALU.is_equal)
                        h_trg_of_window(g, par, tile, drained).then_inc(s["xoT"], 1)
                        dve.wait_ge(s["xhte"], done + 1)
                        V.tensor_tensor(z, z, b_hte[:, 256:256 + EC * H].rearrange("p (c h) -> p c h", c=EC), ALU.add)
                        dve.drain()
                        dve.reg_add(turns_a, turns_a, 1)
                dve.wait_ge(s["z_done"], plus(g, 1))
                V.scalar_tensor_tensor(out=z, in0=z, scalar=SLOPE, in1=z, op0=ALU.mult, op1=ALU.max).then_inc(s["zl_ready"], 1)
                V.sem_inc(s["dstb_free"], 1)

            def onehot(out_, keys):
                return V.tensor_tensor(out_, keys[:, :, None].broadcast_to([P, EC, P]), row_f[:, None, :].broadcast_to([P, EC, P]), ALU.is_equal)

            def of_group(buf, g):
                return buf[:, cut(g, 1), :].rearrange("p a c -> p (a c)")

            def messages(g, slot, par, parts):
                onehot(oh[par][:, :, :], of_group(key, g))
                dve.wait_ge(s["exp_done"], plus(g, 1))
                for rows, cs in parts:
                    V.tensor_tensor(mxe[0:rows, cs, :], mxe[0:rows, cs, :], G[slot][0:rows, cs, F:F + H], ALU.max)
                m3 = G[slot][:, :, 0:F].rearrange("p c (h d) -> p c h d", h=H)
                V.tensor_tensor(m3, m3, G[slot][:, :, F:F + H][:, :, :, None].broadcast_to([P, EC, H, DH]), ALU.mult).then_inc(s["msg_ready"], 1)

            def accumulate(g, par, tile):
                for part, mask in ((tile, above), (tile + 1, below)):
                    rows = ACC[:, bass.ds(part, 1), :].rearrange("p a f -> p (a f)")
                    ins = V.scalar_tensor_tensor(out=rows, in0=b_seg[par][:, 0:ACOLS], scalar=column(mask, g), in1=rows, op0=ALU.mult, op1=ALU.add)
                return ins

            def collect(g, slot, par):
                tile, more = first_tile(g), later_windows(g)
                dve.wait_ge(s["acc_done"], plus(g, CREDIT))
                dve.wait_ge(s["seg_ready"], plus(g, 2))
                accumulate(g, par, tile).then_inc(s["acc_done"], 1)
                with dve.If(more > 0):
                    V.memset(dcur[:, 0:1], 0.0)
                    with dve.Fori(1, more + 1) as w:
                        done = dve.snap(turns_b)
                        later = nc.s_assert_within(dve.snap(tile + w), 0, NT - 1,
                                                   skip_runtime_bounds_check_because="a group's last window starts at or before its last target")
                        dve.drain()
                        V.tensor_scalar(dcur[:, 0:1], dcur[:, 0:1], float(P), None, ALU.add)
                        dve.drain()
                        V.tensor_scalar(xtmp[:, :], of_group(dst_f, g), dcur[:, 0:1], None, ALU.subtract)
                        dve.drain()
                        window_key(xkey[:, :], xtmp[:, :], of_group(mod_f, g), drained)
                        onehot(oh[par][:, :, :], xkey).then_inc(s["xoh"], 1)
                        dve.wait_ge(s["xseg"], done + 1)
                        accumulate(g, par, later)
                        dve.drain()
                        dve.reg_add(turns_b, turns_b, 1)
                V.tensor_copy(tiny[:, 11:12], ones[:, 0:1]).then_inc(s["g_free"], 1)

            rest, part = divmod(LASTE, P)

            def step(g, i, k, first=False, left=3):
                par = k % 2
                if left >= 2:
                    window(plus(g, 2), par, plus(i * 32, (k + 2) // 2 * 16 + 16), EG if left > 2 else LASTE)
                if left >= 1:
                    scores(plus(g, 1), (k + 1) % SLOTS, 1 - par, plus(i * (16 * EC), (k + 1) // SLOTS * (16 * EC) + 16 * EC))
                messages(g, k % SLOTS, par, [(P, slice(0, EC))] if left else [(P, slice(0, rest)), (part, slice(rest, rest + 1))])
                if not first:
                    collect(plus(g, -1), (k - 1) % SLOTS, 1 - par)

            def unit(i, v, before=2, lefts=(3, 3)):
                t = plus(i * UNITS, v)
                g = plus(i * SLOTS, GPT * v)
                first = isinstance(t, int) and t == 0
                step(g, i, GPT * v, first=first, left=lefts[0])
                if before >= 1:
                    outputs(plus(t, -1), 1 - v)
                if len(lefts) > 1:
                    step(plus(g, 1), i, GPT * v + 1, left=lefts[1])
                factors(t, v)

            window(0, 0, 16, EG)
            window(1, 1, 16, EG)
            scores(0, 0, 0, 16 * EC)
            for v in range(UNITS):
                unit(0, v, before=v)
            ch.enter()
            with dve.Fori(1, PASSES - 1) as i:
                ch.turn(i, 11 * UNITS, 1)
                for v in range(UNITS):
                    unit(i, v)
            ch.leave(PASSES - 2)
            for v in range(UNITS):
                unit(PASSES - 1, v, lefts=(3, 3) if v + 1 < UNITS else (2, 1))
            unit(PASSES, 0, lefts=(0,))
            collect(NG - 1, (NG - 1) % SLOTS, 0)
            outputs(NT - 1, 0)

            def tile2(buf, t):
                return buf[:, cut(t, 1)].rearrange("p a c n -> p (a c) n")

            dve.wait_ge(s["no2_ready"], CREDIT + NT)
            V.tensor_scalar(nd["t0"], nd["no2"], MIN_NORM ** 2, None, ALU.max).then_inc(s["rsq_in"], 1)
            rsqrt(nd["rs"], nd["t0"], nd["t1"], 4)
            link(V.tensor_scalar(nd["rs"], nd["rs"], ATANH_MAX, None, ALU.mult))
            link(V.tensor_tensor(nd["rs"], nd["rs"], nd["fsq"], ALU.min))
            dve.wait_ge(s["mixed_ready"], 1 + NT)
            with dve.Fori(0, NT) as t:
                m = tile2(mixed, t)
                V.scalar_tensor_tensor(out=m, in0=m, scalar=nd["rs"][:, cut(t, 1)], in1=bres[:, :].rearrange("p (c n) -> p c n", c=KC),
                                       op0=ALU.mult, op1=ALU.add).then_inc(s["ft_ready"], 1)
            dve.wait_ge(s["nf2_ready"], 1 + NT)
            V.tensor_scalar(nd["t0"], nd["nf2"], MIN_NORM ** 2, None, ALU.max).then_inc(s["th_in"], 1)
            dve.wait_ge(s["th_out"], 1)
            link(V.reciprocal(nd["ff"], nd["n"]))
            link(V.tensor_scalar(nd["t1"], nd["t1"], MAXNORM, None, ALU.min))
            link(V.tensor_tensor(nd["ff"], nd["ff"], nd["t1"], ALU.mult))

            dve.wait_ge(s["exs_out"], 1)
            dve.drain()
            V.tensor_reduce(tiny[:, 0:1], mxe[:, :, :], AX.XY, ALU.max)
            V.tensor_reduce(tiny[:, 1:2], exs[:, 0:NT - 1, :], AX.XY, ALU.max)
            link(V.memset(tiny[:, 2:3], 0.0))
            link(V.tensor_reduce(tiny[0:LASTN, 2:3], exs[0:LASTN, NT - 1, :], AX.X, ALU.max))
            V.tensor_reduce(mx2[:, 0:1], tiny[:, 0:3], AX.X, ALU.max).then_inc(s["mx_in"], 1)
            dve.wait_ge(s["mx_all"], 1)
            link(V.tensor_scalar(guard[:, :], mx2[:, 1:2], GAT_EPS, 1e-37, ALU.mult, ALU.max))

            def assemble(t, slot, rows, use):
                y = xs[slot][:, :].rearrange("p (h d) -> p h d", h=H)
                e = exs[:, cut(t, 1), :].rearrange("p a h -> p (a h)")
                acc = ACC[:, cut(t, 1), :].rearrange("p a f -> p (a f)")
                dve.wait_ge(back_in[slot], plus(use * 32, 32))
                link(V.tensor_tensor(y, hp[slot][:, 0:F].rearrange("p (h d) -> p h d", h=H), e[:, :, None].broadcast_to([P, H, DH]), ALU.mult))
                link(V.scalar_tensor_tensor(out=tiny[:, 0:H], in0=acc[:, F:ACOLS], scalar=guard[:, 0:1], in1=e, op0=ALU.add, op1=ALU.add))
                link(V.reciprocal(tiny[:, 0:H], tiny[:, 0:H]))
                link(V.tensor_tensor(y, y, acc[:, 0:F].rearrange("p (h d) -> p h d", h=H), ALU.add))
                link(V.tensor_tensor(y, y, tiny[:, 0:H, None].broadcast_to([P, H, DH]), ALU.mult))
                m = tile2(mixed, t)
                link(V.scalar_tensor_tensor(out=m, in0=m, scalar=nd["ff"][:, cut(t, 1)], in1=xs[slot][:, :].rearrange("p (c n) -> p c n", c=KC),
                                            op0=ALU.mult, op1=ALU.add))
                m = m[0:rows]
                V.tensor_tensor(m, m, xr[slot][0:rows, :].rearrange("p (c n) -> p c n", c=KC), ALU.add).then_inc(s["asm_done"], 1)
            ch.enter()
            with dve.Fori(0, NT // 2) as i:
                ch.turn(i, 12)
                for j in range(2):
                    assemble(i * 2 + j, j, P, i)
            ch.leave(NT // 2)
            assemble(NT - 1, 0, LASTN, NT // 2)

            def residual(t):
                V.bn_stats(stats[:, cut(t, 1), :].rearrange("p a s -> p (a s)"), tile2(mixed, t)).then_inc(s["x2_ready"], 1)
            dve.wait_ge(s["asm_done"], CREDIT + NT)
            with dve.Fori(0, NT) as t:
                residual(t)
            dve.wait_ge(s["x2_ready"], NT)
            for t in range(NT):
                V.bn_aggr(mv[:, t, :], stats[:, t, :]).then_inc(s["x2_ready"], 1)
            dve.wait_ge(s["x2_ready"], 2 * NT)
            V.tensor_scalar(nd["t1"], mv[:, :, 1], LN_EPS, None, ALU.add).then_inc(s["rsq_in"], 1)
            rsqrt(nd["rstd"], nd["t1"], nd["t0"], 5)
            dve.wait_ge(s["ffn_v"], 64)
            v_ = fvec[:, 4:10:5, :]
            V.tensor_scalar(ftmp[:, :, :], v_, FBN_EPS, None, ALU.add).then_inc(s["faff_in"], 1)
            link(V.tensor_scalar(fvec[:, 4:10:5, :], v_, FBN_EPS, None, ALU.add))
            dve.wait_ge(s["faff_out"], 1)
            scale_, bias_ = faff[:, 0:4:2, :], faff[:, 1:4:2, :]
            link(V.reciprocal(scale_, ftmp[:, :, :]))
            newton(scale_, v_, ftmp[:, :, :])
            link(V.tensor_tensor(scale_, scale_, fvec[:, 1:10:5, :], ALU.mult))
            link(V.tensor_tensor(bias_, fvec[:, 0:10:5, :], fvec[:, 3:10:5, :], ALU.subtract))
            link(V.tensor_tensor(bias_, bias_, scale_, ALU.mult))
            V.tensor_tensor(bias_, bias_, fvec[:, 2:10:5, :], ALU.add).then_inc(s["faff_out"], 1)

            def norm2(t, slot):
                dve.wait_ge(s["tr2_done"], plus(t, 1))
                V.tensor_scalar(xs[slot][:, :].rearrange("p (c n) -> p c n", c=KC), tile2(mixed, t), mv[:, cut(t, 1), 0],
                                nd["rstd"][:, cut(t, 1)], ALU.subtract, ALU.mult).then_inc(s["xs2_ready"], 1)

            def gate_rows(t, slot):
                dve.wait_ge(s["lg_mm"], plus(t, 1 + CREDIT))
                V.tensor_tensor(gate[:, cut(t, 1), :].rearrange("p a e -> p (a e)"), bank[2 + slot][:, 0:NX], brb[:, :], ALU.add).then_inc(s["lg_done"], 1)
            with dve.Fori(0, NT // 2) as i:
                for j in range(2):
                    norm2(i * 2 + j, j)
                for j in range(2):
                    gate_rows(i * 2 + j, j)
            norm2(NT - 1, 0)
            gate_rows(NT - 1, 0)
            dve.wait_ge(s["lg_done"], CREDIT + NT)
            g3 = gred[:, :, None].broadcast_to([P, NT, NX])
            link(V.tensor_reduce(gred[:, :], gate[:, :, :], AX.X, ALU.max))
            V.tensor_tensor(gate[:, :, :], gate[:, :, :], g3, ALU.subtract).then_inc(s["sm_in"], 1)
            dve.wait_ge(s["sm_out"], 1)
            link(V.tensor_reduce(gred[:, :], gate[:, :, :], AX.X, ALU.add))
            link(V.reciprocal(gred[:, :], gred[:, :]))
            V.tensor_tensor(gate[:, :, :], gate[:, :, :], g3, ALU.mult).then_inc(s["gates"], 1)

            def bias_rows(t, slot):
                dve.wait_ge(s["bo_mm"], plus(t, 1 + CREDIT))
                m = tile2(mixed, t)
                V.tensor_tensor(m, m, bank[2 + slot][:, 0:F].rearrange("p (c n) -> p c n", c=KC), ALU.add).then_inc(s["x2b"], 1)
            with dve.Fori(0, NT // 2) as i:
                for j in range(2):
                    bias_rows(i * 2 + j, j)
            bias_rows(NT - 1, 0)
            dve.wait_ge(s["x2b"], CREDIT + NT)
            dve.wait_ge(s["gates"], 1)

            def experts(b, tiles):
                for e in range(NX):
                    dve.wait_ge(s["y_mm"], plus(b * NX, e + 1 + CREDIT))
                    for j in range(tiles):
                        t = plus(b * TPB, j)
                        if e:
                            dve.wait_ge(s["y_add"], plus(b * (NX * TPB), (e - 1) * tiles + j + 2))
                        m = tile2(mixed, t)
                        y = bank[4 + 2 * (e % 2) + j // 2][:, (j % 2) * F:(j % 2 + 1) * F].rearrange("p (c n) -> p c n", c=KC)
                        V.scalar_tensor_tensor(out=m, in0=y, scalar=gate[:, cut(t, 1), e], in1=m, op0=ALU.mult, op1=ALU.add).then_inc(s["y_add"], 1)
            with dve.Fori(0, NB) as b:
                experts(b, TPB)
            experts(NB, 1)


def _layout(i):
    def g(name):
        return np.asarray(i[name])

    def cols(v):
        return v.reshape(NX, KC, P).transpose(2, 0, 1).reshape(P, NX * KC)

    def chunked(v):
        return v.reshape((2, 4, 3, 32) + v.shape[1:]).swapaxes(1, 2).swapaxes(0, 1)

    def per_partition(v):
        return chunked(v).reshape(MC, P).T

    whole = (NG - 1) * EG
    tail = {k + "_t": g(k)[whole:whole + LASTE // P * P].reshape(LASTE // P, P).T for k in ("src", "dst")}
    arrays = {
        **tail,
        "x": g("x"), "src": g("src"), "dst": g("dst"),
        "src_l": g("src")[:whole].reshape(NG - 1, EC, P).transpose(2, 0, 1),
        "dst_l": g("dst")[:whole].reshape(NG - 1, EC, P).transpose(2, 0, 1),
        "W": g("L0_gnn_W"), "WT": g("L0_gnn_W").T, "b": g("L0_gnn_b"), "bcol": g("L0_gnn_b").reshape(KC, P).T,
        "acol": np.concatenate([g("L0_gnn_a_src").reshape(KC, P).T, g("L0_gnn_a_trg").reshape(KC, P).T], axis=1),
        "wqkv": chunked(g("L0_mix_w_qkv")[:, :, 2]).reshape(C2, F).T,
        "wpw": g("L0_mix_w_pw")[:, :, 0].reshape(2, 4, 3, 32, 32).transpose(1, 4, 2, 0, 3).reshape(P, MC, 32),
        "mixvec": np.stack([per_partition(g("L0_mix_bn_gamma")), per_partition(g("L0_mix_bn_beta")),
                            per_partition(g("L0_mix_w_dw")[:, 0, 2])], axis=1),
        "wres": g("L0_mix_w_res")[:, :, 0].T, "b_res": g("L0_mix_b_res"),
        "fvec": np.stack([cols(g("L0_ffn_" + n)) for n in ("b1", "g1", "be1", "m1", "v1", "b2", "g2", "be2", "m2", "v2")], axis=1),
        "W1": g("L0_ffn_W1"), "W2": g("L0_ffn_W2"), "Wo": g("L0_ffn_Wo"),
        "Wr": g("L0_ffn_Wr"), "br": g("L0_ffn_br"), "bo": g("L0_ffn_bo"),
    }
    return {k: np.ascontiguousarray(v) for k, v in arrays.items()}


def kernel(**inputs):
    import concourse.bacc as bacc
    from concourse.bass_utils import run_bass_kernel_spmd

    nc = bacc.Bacc("TRN2", target_bir_lowering=False, num_devices=1)
    arrays = _layout(inputs)
    args = {k: nc.dram_tensor(f"in_{k}", v.shape, mybir.dt.from_np(v.dtype), kind="ExternalInput").ap() for k, v in arrays.items()}
    out = nc.dram_tensor("out", (N, F), F32, kind="ExternalOutput").ap()
    program(nc, args, out)
    r = run_bass_kernel_spmd(nc, [{f"in_{k}": v for k, v in arrays.items()}], core_ids=[0])
    return r.results[0]["out"]
```

```python
import math
from contextlib import ExitStack

import numpy as np

import concourse.bass as bass
from concourse import mybir

F32 = mybir.dt.float32
F32R = mybir.dt.float32r
I32 = mybir.dt.int32
ALU = mybir.AluOpType
ACT = mybir.ActivationFunctionType
AX = mybir.AxisListType

P = 128
N = 3125
E = 50000
F = 256
KC = F // P
H = 8
DH = F // H
NT = -(-N // P)
LASTN = N - (NT - 1) * P
NPAD = NT * P
BLK = 512
NB = N // BLK
TPB = BLK // P
LASTB = N - NB * BLK
STEPS = NB + 1
STEP_TILES = [NT // STEPS + (i < NT % STEPS) for i in range(STEPS)]
HW = F + 2 * H
C2 = 768
MC = C2 // P
OC = 512
NX = 8
LN_EPS, BN_EPS, FBN_EPS, ATT_EPS, GAT_EPS = 1e-5, 1e-5, 1e-3, 1e-15, 1e-10
MIN_NORM = 1e-15
MAXNORM = float(np.float32(1.0 - 1e-5))
ATANH_MAX = math.atanh(MAXNORM)
SLOPE = 0.2

EC = 8
EG = EC * P
NG = -(-E // EG)
LASTE = E - (NG - 1) * EG
ACOLS = F + H
TSHIFT = P.bit_length() - 1
PAD_DST = -1000000
SLOTS = 4
GPT = 2
UNITS = 2
PASSES = (NT - 1) // UNITS
AHEAD = SLOTS - 1
XT = 8
PAIRS = [(t, min(2, NT - t)) for t in range(0, NT, 2)]
assert GPT * (NT - 1) == NG - 1 and PASSES * UNITS == NT - 1 and SLOTS == GPT * UNITS

CREDIT = 2
MM_CREDIT = 3
SPLIT = 2


def plus(a, b):
    if isinstance(b, int) and b == 0:
        return a
    if isinstance(a, int) and a == 0:
        return b
    return a + b


def cut(start, size):
    return slice(start, start + size) if isinstance(start, int) else bass.ds(start, size)


class Chain:

    def __init__(self, eng, sem):
        self.eng, self.sem, self.base, self.n = eng, sem, 0, 0

    def link(self, ins):
        ins.then_inc(self.sem, 1)
        self.n += 1
        self.eng.wait_ge(self.sem, plus(self.base, self.n))

    def enter(self):
        self.first = plus(self.base, self.n)
        return self.first

    def turn(self, i, per, start=0):
        self.base, self.n, self.per = plus(i * per, self.first - start * per), 0, per

    def leave(self, passes):
        assert self.n == self.per, (self.n, self.per)
        self.base, self.n = self.first + passes * self.per, 0


def first_tile_of(step):
    return sum(STEP_TILES[:step % STEPS])


def columns(step):
    left = N - first_tile_of(step) * P
    return min(STEP_TILES[step % STEPS] * P, left + left % 2)


def program(nc, a, out):
    with ExitStack() as ctx:
        def sb(name, shape, dt=F32):
            return ctx.enter_context(nc.sbuf_tensor(name, shape, dt))

        def sem(name):
            return ctx.enter_context(nc.semaphore(name))

        table = nc.dram_tensor("projected_rows", [NPAD, HW], F32, kind="Internal").ap()
        ranges = nc.dram_tensor("group_ranges", [2 * NG], I32, kind="Internal").ap()
        firsts = nc.dram_tensor("group_firsts", [2 * NG], I32, kind="Internal").ap()

        bank = [ctx.enter_context(nc.psum_tensor(f"bank{i}", [P, 512], F32)) for i in range(8)]
        b_q, b_k, b_v, b_o, b_r, b_hte = bank[:6]
        b_seg = bank[6:8]

        with ExitStack() as late:
            def late_sb(name, columns_, dt=F32R):
                return late.enter_context(nc.sbuf_tensor(name, [P, columns_], dt))
            late_sb("under_mixed", 2 * NPAD, F32)
            frh_all = late_sb("frh", KC * NPAD)
            frl_all = late_sb("frl", KC * NPAD)
            ew_all = late_sb("ew", (NT + 1) * ACOLS)
            g_late = [late_sb(f"g_late{i}", EC * HW) for i in range(SLOTS)]
        FRH, FRL = (b[:, :].rearrange("p (k n) -> p k n", k=KC) for b in (frh_all, frl_all))
        ew = ew_all[:, 0:4 * 3 * KC * F].rearrange("p (i h m k f) -> p i h m k f", i=2, h=2, m=3, k=KC)

        Z = sb("Z", [P, MC, NPAD])
        zflat = Z[:, :, :].rearrange("p c n -> p (c n)")
        x_in = zflat[:, 4 * NPAD:4 * NPAD + NT * F].rearrange("p (t f) -> p t f", f=F)
        mixed = Z[:, 0:2, :].rearrange("p c (t n) -> p t c n", n=P)
        frows = sb("frows", [P, (NT + 1) * ACOLS])
        FR = frows[:, 0:KC * NPAD].rearrange("p (k n) -> p k n", k=KC)
        ACC = frows[:, :].rearrange("p (t f) -> p t f", f=ACOLS)
        G = [sb(f"G{i}", [P, EC, HW]) for i in range(SLOTS)]
        hst = sb("hst", [P, NT + 1, 2 * H])
        tt_all = sb("TT", [P, 2 * MC * P])
        TT = [tt_all[:, i * MC * P:(i + 1) * MC * P].rearrange("p (c n) -> p c n", c=MC) for i in range(2)]
        wqkv = tt_all[:, :].rearrange("p (k n) -> p k n", k=KC)
        ip = sb("ip", [P, MC + 1, P])
        ident = ip[:, 0, :]
        wres = sb("wres", [P, OC // P, F])
        acol = sb("acol", [P, 4])
        bcol = sb("bcol", [P, KC])
        mixvec = sb("mixvec", [P, 3, MC])
        bres = sb("bres", [P, F])
        ones = sb("ones", [P, P])
        row_f = sb("row_f", [P, P])
        col_i = sb("col_i", [P, 1], I32)
        col_f = sb("col_f", [P, 1])
        early = [G[i][:, :, :].bitcast(I32).rearrange("p c n -> p (c n)") for i in range(SLOTS)]
        dst_rows = early[3][0:NG, 0:EG]
        dst_l = early[2][:, 0:NG * EC].rearrange("p (g c) -> p g c", c=EC)
        mod_l = early[2][:, NG * EC:2 * NG * EC].rearrange("p (g c) -> p g c", c=EC)
        src_l = sb("src_l", [P, NG, EC], I32)
        idx = [sb(f"idx{i}", [P, EC], I32) for i in range(SLOTS)]
        dst_f = sb("dst_f", [P, NG, EC])
        mod_f = sb("mod_f", [P, NG, EC])
        key = sb("key", [P, NG, EC])
        rng_i = sb("rng_i", [NG, 6], I32)
        tab = sb("tab", [1, NG, 2], I32)
        first_i = early[1][:, 0:NG]
        firstm_i = early[1][:, NG:2 * NG]
        row_i = early[1][:, 128:256]
        first_f = sb("first_f", [P, NG])
        firstm = sb("firstm", [P, NG])
        below = sb("below", [P, NG])
        above = sb("above", [P, NG])
        target = sb("target", [P, NG])
        dcur = sb("dcur", [P, 2])
        xkey = sb("xkey", [P, EC])
        xtmp = sb("xtmp", [P, EC])
        dstb_all = sb("dstb", [P, 2 * EG], I32)
        dstb = [dstb_all[:, i * EG:(i + 1) * EG] for i in range(2)]
        hsel = [sb(f"hsel{i}", [P, H]) for i in range(2)]
        negt = [sb(f"negt{i}", [P, 1]) for i in range(2)]
        htmp = sb("htmp", [P, H])
        ohT = [sb(f"ohT{i}", [P, EG]) for i in range(2)]
        oh = [sb(f"oh{i}", [P, EC, P]) for i in range(2)]
        hp = [oh[i][:, :, :].rearrange("p c w -> p (c w)")[:, F:F + HW] for i in range(2)]
        wx = ohT[0][:, 0:KC * HW].rearrange("p (k n) -> p k n", k=KC)
        hbias = ohT[0][:, KC * HW:(KC + 1) * HW]
        fs = [ohT[1][:, i * F:(i + 1) * F].rearrange("p (k n) -> p k n", k=KC) for i in range(2)]
        xs = [ohT[1][:, (2 + i) * F:(3 + i) * F] for i in range(2)]
        zed = [sb(f"zed{i}", [P, EC, H]) for i in range(2)]
        mxe = sb("mxe", [P, EC, H])
        exs = sb("exs", [P, NT, H])
        mx2 = sb("mx2", [P, 4])
        mxr = sb("mxr", [2, 1])
        negc = sb("negc", [P, 1])
        guard = sb("guard", [P, 1])
        stats = sb("stats", [P, NT, 6])
        mv = sb("mv", [P, NT, 2])
        bmv = sb("bmv", [P, MC, 2])
        baff = sb("baff", [P, 2, MC])
        nodes = sb("nodes", [P, 16, NT])
        U = [sb(f"U{i}", [P, 3, 512]) for i in range(2)]
        bstats = U[0][:, 0, 0:MC * (NB + 1) * 6].rearrange("p (c b s) -> p c b s", c=MC, s=6)
        oT = sb("oT", [P, 512])
        junk = sb("junk", [P, 512])
        fvec = U[0][:, 0, 0:10 * KC * NX].rearrange("p (v e) -> p v e", v=10)
        ftmp = U[0][:, 0, 160:160 + 2 * KC * NX].rearrange("p (v e) -> p v e", v=2)
        faff = U[0][:, 0, 192:192 + 4 * KC * NX].rearrange("p (v e) -> p v e", v=4)
        gate = U[0][:, 1, 0:NT * NX].rearrange("p (t e) -> p t e", e=NX)
        spill = [junk[:, :].bitcast(mybir.dt.bfloat16)[:, i * 512:(i + 1) * 512] for i in range(2)]
        wT = junk[:, :].rearrange("p (c n) -> p c n", c=KC)
        bcolb = oT[:, 0:256].rearrange("p (c m) -> p c m", c=KC)
        wpw = oT[:, 256:256 + MC * 32].rearrange("p (c o) -> p c o", c=MC)
        ablk = sb("ablk", [P, KC, 2 * H])
        sq3 = [sb(f"sq3{i}", [P, 3]) for i in range(2)]
        tiny = sb("tiny", [P, 12])
        epsr = [sb(f"epsr{i}", [P, 2]) for i in range(2)]
        lneps = sb("lneps", [P, 1])
        ksum = sb("ksum", [P, 16])
        aff = [sb(f"aff{i}", [P, 4, KC]) for i in range(2)]
        wr = sb("wr", [P, KC, NX])
        brb = sb("brb", [P, NX])
        gred = sb("gred", [P, NT])
        gflat = [G[i][:, :, :].rearrange("p c n -> p (c n)") for i in range(SLOTS)]
        xr = [gflat[i][:, 0:F] for i in range(SLOTS)]
        hr = [gflat[i][:, F:2 * F] for i in range(SLOTS)]
        yr = [gflat[i][:, 2 * F:3 * F] for i in range(SLOTS)]
        xs2 = [gflat[i][:, 3 * F:4 * F] for i in range(SLOTS)]
        fs2 = [gflat[i][:, 4 * F:5 * F].rearrange("p (k n) -> p k n", k=KC) for i in range(SLOTS)]
        HB = KC * BLK
        hid = [oh[i][:, :, :].rearrange("p c w -> p (c w)").rearrange("p (k n) -> p k n", k=KC) for i in range(2)]
        hidh, hidl = ([[g_late[2 * m + i][:, j * HB:(j + 1) * HB].rearrange("p (k n) -> p k n", k=KC) for i in range(2)]
                       for m in range(2)] for j in range(2))
        raw = [b[:, 0:3 * KC * F].rearrange("p (m k f) -> p m k f", m=3, k=KC) for b in (tt_all, dstb_all.bitcast(F32))]
        bo4 = ohT[0][:, 0:TPB * F]
        gT = junk[:, 0:2 * P]

        names = ("rstd f0 inv_f0 n2 n t0 t1 t2 fsq no2 rs nf2 ff scale").split()
        nd = {k: nodes[:, i, :] for i, k in enumerate(names)}

        s = {}
        for names_ in (
            "x_pad x_in weights edge_fill edges",
            "idn consts",
            "vchain achain gchain diff",
            "rsq_in rsq_out ln_in ln_out",
            "wa_ready wa_mm wx_ready",
            "rng_ready rng_out rng_in",
            "xs_ready tr_done fs_ready fr_copied proj_mm hp_ready",
            "cm_in cm_tr cm_red cm_mm exs_in exs_out",
            "z_mm z_copied z_stats baff_ready",
            "tt_ready u_mm u_evac fsq_ready qk_ready eps_ready",
            "o_ready o_tr oT_ready r_mm mixed_ready no2_ready",
            "dstb_free hsel_tmp win_ready ohT_ready hte_ready",
            "z_done zl_ready exp_done msg_ready",
            "seg_ready acc_done g_free idx_ready",
            "xoT xhte xoh xseg",
            "mx_in mx_all",
            "ft_ready nf2_ready th_in th_out",
            "self_done weighed with_mix asm_done x2_ready",
            "xs2_ready tr2_done fs2_ready frh_ready frl_ready",
            "lg_mm lg_done sm_in sm_out gates gt_tr gt_ready",
            "bo_clear bo_in bo_mm x2b",
            "ffn_v faff_in faff_out w_hi w_lo",
            "h1_mm h1_r h1_hi h1_lo h2_mm h2_r h2_hi h2_lo",
            "y_mm y_add out_done",
        ):
            s.update({k: sem(k) for k in names_.split()})
        x_part = [sem(f"x_part{i}") for i in range((NT - 1) // XT)]
        gath = [sem(f"gath{i}") for i in range(SLOTS)]
        tout = [sem(f"tout{i}") for i in range(2)]
        h_back = [sem(f"h_back{i}") for i in range(SLOTS)]
        x_back = [sem(f"x_back{i}") for i in range(SLOTS)]
        w_raw = [sem(f"w_raw{i}") for i in range(2)]
        dstl = [sem(f"dstl{i}") for i in range(2)]

        def outputs_of(step):
            for j in range(-(-columns(step) // P)):
                size = min(P, columns(step) - j * P)
                yield j, slice(j * P, j * P + size), bank[4 + 2 * (step % 2) + j // 2][0:size, (j % 2) * F:(j % 2 + 1) * F]

        block = ctx.enter_context(nc.Block())

        @block.sync
        def _(sp):
            nc.sync.sem_inc(tout[0], 16)
            nc.sync.sem_inc(tout[1], 16)
            sp.wait_ge(s["x_pad"], 1)
            full = (NT - 1) * P
            for part, t in zip(x_part, range(0, NT - 1, XT)):
                sp.dma_start(x_in[:, t:t + XT, :], a["x"][t * P:(t + XT) * P, :].rearrange("(t p) f -> p t f", p=P)).then_inc(part, 16)
            sp.dma_start(x_in[0:LASTN, NT - 1, :], a["x"][full:N, :]).then_inc(s["x_in"], 16)
            for dst, src in (
                (wx[:, :, 0:F], a["W"].rearrange("(k p) n -> p k n", p=P)),
                (wT, a["WT"].rearrange("(c p) i -> p c i", p=P)),
                (acol[:, :], a["acol"]), (bcol[:, :], a["bcol"]),
                (hbias[:, 0:F], a["b"][None, :].broadcast_to([P, F])),
                (wqkv, a["wqkv"].rearrange("(k p) n -> p k n", p=P)),
                (wpw, a["wpw"]), (mixvec[:, :, :], a["mixvec"]),
                (wres[:, :, :], a["wres"].rearrange("(c p) n -> p c n", p=P)),
                (bres[:, :], a["b_res"][None, :].broadcast_to([P, F])),
            ):
                sp.dma_start(dst, src).then_inc(s["weights"], 16)
            sp.wait_ge(s["edge_fill"], 2)
            whole = (NG - 1) * EG
            sp.dma_start(dst_rows[0:NG - 1, :], a["dst"][0:whole].rearrange("(g e) -> g e", e=EG)).then_inc(s["edges"], 16)
            sp.dma_start(dst_rows[NG - 1:NG, 0:LASTE], a["dst"][whole:E][None, :]).then_inc(s["edges"], 16)
            sp.dma_start(dst_rows[NG - 1:NG, LASTE:EG], a["dst"][whole:whole + EG - LASTE][None, :]).then_inc(s["edges"], 16)
            rest, part = divmod(LASTE, P)
            for buf, lay, flat in ((src_l, "src_l", "src"), (dst_l, "dst_l", "dst")):
                sp.dma_start(buf[:, 0:NG - 1, :], a[lay]).then_inc(s["edges"], 16)
                sp.dma_start(buf[:, NG - 1, 0:rest], a[flat + "_t"]).then_inc(s["edges"], 16)
                sp.dma_start(buf[0:part, NG - 1, rest:rest + 1], a[flat][whole + rest * P:E][:, None]).then_inc(s["edges"], 16)
            sp.wait_ge(s["rng_ready"], 1)
            sp.dma_start(ranges.rearrange("(g c) -> g c", c=2), rng_i[:, 0:2]).then_inc(s["rng_out"], 16)
            for c in range(2):
                sp.dma_start(firsts[c * NG:(c + 1) * NG][:, None], rng_i[:, 2 + c:3 + c]).then_inc(s["rng_out"], 16)
            sp.wait_ge(s["rng_out"], 48)
            sp.dma_start(tab[:, :, :], ranges.rearrange("(a g c) -> a g c", a=1, c=2)).then_inc(s["rng_in"], 16)
            sp.dma_start(first_i, firsts[None, 0:NG].broadcast_to([P, NG])).then_inc(s["rng_in"], 16)
            sp.dma_start(firstm_i, firsts[None, NG:2 * NG].broadcast_to([P, NG])).then_inc(s["rng_in"], 16)
            def table_rows(t, slot):
                sp.wait_ge(s["hp_ready"], plus(t, 1 + CREDIT))
                sp.dma_start(table[cut(t * P, P), :], hp[slot][:, :]).then_inc(tout[slot], 16)
            with sp.Fori(0, NT // 2) as i:
                for j in range(2):
                    table_rows(plus(i * 2, j), j)
            table_rows(NT - 1, 0)

            def targets(g, slot, edges):
                sp.wait_ge(s["dstb_free"], plus(g, 1))
                sp.dma_start(dstb[slot][:, 0:edges], a["dst"][cut(g * EG, edges)][None, :].broadcast_to([P, edges])).then_inc(dstl[slot], 16)
            with sp.Fori(0, (NG - 1) // 2) as i:
                for j in range(2):
                    targets(i * 2 + j, j, EG)
            targets(NG - 1, 0, LASTE)

            sp.wait_ge(s["no2_ready"], CREDIT + NT)
            sp.wait_ge(s["o_tr"], CREDIT + NT)
            for dst, src in ((fvec[:, :, :], a["fvec"]), (wr[:, :, :], a["Wr"].rearrange("(k p) e -> p k e", p=P)),
                             (brb[:, :], a["br"][None, :].broadcast_to([P, NX]))):
                sp.dma_start(dst, src).then_inc(s["ffn_v"], 16)

            def rows_again(t, slot, rows):
                sp.wait_ge(s["self_done"], plus(t, 1))
                sp.dma_start(hr[slot], table[cut(t * P, P), 0:F]).then_inc(h_back[slot], 16)

            def x_again(t, slot, rows):
                sp.wait_ge(s["asm_done"], plus(t, 1))
                sp.dma_start(xr[slot][0:rows, :], a["x"][cut(t * P, rows), :]).then_inc(x_back[slot], 16)
            sp.wait_ge(s["g_free"], SLOTS + NG)
            for again in (rows_again, x_again):
                with sp.Fori(0, NT // SLOTS) as i:
                    for j in range(SLOTS):
                        again(plus(i * SLOTS, j), j, P)
                again(NT - 1, 0, LASTN)

            def weights(e, slot):
                for m, w in enumerate(("W1", "W2", "Wo")):
                    src = a[w][cut(e, 1)].rearrange("e (k p) f -> p (e k) f", p=P)
                    sp.dma_start(raw[slot][:, m], src).then_inc(w_raw[slot], 16)
            sp.wait_ge(s["u_mm"], 1 + 3 * NT)
            weights(0, 0)
            weights(1, 1)
            sp.wait_ge(s["bo_clear"], 1)
            for q in range(P // (TPB * NX)):
                for j in range(TPB):
                    row = (q * TPB + j) * NX
                    sp.dma_start(bo4[row:row + NX, j * F:(j + 1) * F], a["bo"]).then_inc(s["bo_in"], 16)
            with sp.Fori(0, NX // 2 - 1) as i:
                for j in range(2):
                    sp.wait_ge(s["w_hi"], plus(i * 2, j + 1))
                    sp.wait_ge(s["w_lo"], plus(i * 2, j + 1))
                    weights(plus(i * 2, j + 2), j)

            full = (NX - 1) * STEPS
            for b in range(STEPS):
                sp.wait_ge(s["y_add"], full + b + 1 + CREDIT)
                for t in range(first_tile_of(b), first_tile_of(b) + STEP_TILES[b]):
                    rows = min(P, N - t * P)
                    sp.dma_start(out[t * P:t * P + rows, :].rearrange("n (c f) -> n c f", c=KC), mixed[0:rows, t]).then_inc(s["out_done"], 16)
            sp.wait_ge(s["out_done"], 16 * NT)

        @block.gpsimd
        def _(pool):
            g = nc.gpsimd
            chain = Chain(pool, s["gchain"])
            g.memset(x_in[:, NT - 1, :], 0.0).then_inc(s["x_pad"], 1)
            g.memset(src_l[:, NG - 1, :], 0).then_inc(s["edge_fill"], 1)
            g.memset(dst_l[:, NG - 1, :], PAD_DST).then_inc(s["edge_fill"], 1)
            g.memset(ones[:, :], 1.0).then_inc(s["consts"], 1)
            g.memset(ablk[:, :, :], 0.0).then_inc(s["consts"], 1)
            g.memset(ip[:, 1:MC + 1, :], 0.0).then_inc(s["consts"], 1)
            chain.link(g.memset(ident[:, :], 0.0))
            g.iota(row_i, pattern=[[1, P]], base=0, channel_multiplier=0).then_inc(s["consts"], 1)
            g.iota(col_i[:, :], pattern=[[0, 1]], base=0, channel_multiplier=1).then_inc(s["consts"], 1)
            g.affine_select(out=ident[:, :], in_=ident[:, :], compare_op=ALU.not_equal, fill=1.0, base=0,
                            pattern=[[-1, P]], channel_multiplier=1).then_inc(s["idn"], 1)

            def keep(t, slot):
                pool.wait_ge(s["fs_ready"], plus(t, 1))
                g.tensor_copy(FR[:, :, cut(t * P, P)], fs[slot][:, :, :]).then_inc(s["fr_copied"], 1)
            g.sem_inc(s["fr_copied"], CREDIT)
            with pool.Fori(0, NT // 2) as i:
                for j in range(2):
                    keep(plus(i * 2, j), j)
            keep(NT - 1, 0)

            def sources(grp, slot, uses):
                if not isinstance(uses, int) or uses:
                    pool.wait_ge(gath[slot], uses)
                g.tensor_copy(idx[slot][:, :], src_l[:, cut(grp, 1), :].rearrange("p a c -> p (a c)")).then_inc(s["idx_ready"], 1)

            def gather(grp, slot, nxt):
                pool.wait_ge(s["idx_ready"], plus(grp, 1))
                pool.wait_ge(s["g_free"], plus(grp, 1))
                if nxt is not None:
                    sources(*nxt)
                for c in range(EC):
                    g.indirect_dma_start(
                        out=G[slot][:, c, :], out_offset=None, in_=table[:, :],
                        in_offset=bass.IndirectOffsetOnAxis(ap=idx[slot][:, c:c + 1], axis=0),
                    ).then_inc(gath[slot], 16)
            pool.wait_ge(s["edges"], 16 * 9)
            pool.wait_ge(tout[0], 16 * (1 + NT - NT // 2))
            pool.wait_ge(tout[1], 16 * (1 + NT // 2))
            pool.wait_ge(s["exs_in"], 1)
            sources(0, 0, 0)

            def with_next(grp, place, i, j):
                gather(grp, place % SLOTS, (plus(grp, 1), (place + 1) % SLOTS, plus(i * (16 * EC), (j + 1) // SLOTS * (16 * EC))))
            for g_ in range(SLOTS):
                with_next(g_, g_, 0, g_)
            with pool.Fori(1, PASSES - 1) as i:
                for j in range(SLOTS):
                    with_next(plus(i * SLOTS, j), j, i, j)
            for g_ in range((PASSES - 1) * SLOTS, NG - 1):
                with_next(g_, g_, g_ // SLOTS, g_ % SLOTS)
            gather(NG - 1, (NG - 1) % SLOTS, None)

            g.sem_inc(s["self_done"], SLOTS)
            pool.wait_ge(s["mx_in"], 1)
            g.partition_all_reduce(mx2[:, 1:2], mx2[:, 0:1], P, bass.bass_isa.ReduceOp.max).then_inc(s["mx_all"], 1)

            def self_loop(t, slot, uses):
                pool.wait_ge(h_back[slot], uses)
                e = exs[:, cut(t, 1), :].rearrange("p a h -> p (a h)")
                g.tensor_tensor(yr[slot].rearrange("p (h d) -> p h d", h=H), hr[slot].rearrange("p (h d) -> p h d", h=H),
                                e[:, :, None].broadcast_to([P, H, DH]), ALU.mult).then_inc(s["gchain"], 1)
                pool.wait_ge(s["gchain"], plus(t, 2))
                acc = ACC[:, cut(t, 1), 0:F].rearrange("p a f -> p (a f)")
                g.tensor_tensor(acc, acc, yr[slot], ALU.add).then_inc(s["self_done"], 1)
            with pool.Fori(0, NT // SLOTS) as i:
                for j in range(SLOTS):
                    self_loop(plus(i * SLOTS, j), j, plus(i * 16, 16))
            self_loop(NT - 1, 0, NT // SLOTS * 16 + 16)
            g.memset(bo4, 0.0).then_inc(s["bo_clear"], 1)

        @block.scalar
        def _(act):
            A = nc.scalar
            A.sem_inc(s["z_copied"], 3)
            A.sem_inc(s["oT_ready"], 1)
            A.sem_inc(s["mixed_ready"], 1)
            A.sem_inc(s["nf2_ready"], CREDIT)
            A.sem_inc(s["h1_hi"], 1)
            A.sem_inc(s["h2_hi"], 1)
            A.sem_inc(s["h1_r"], CREDIT)
            A.sem_inc(s["h2_r"], CREDIT)
            A.sem_inc(s["u_evac"], 3)
            A.sem_inc(s["no2_ready"], CREDIT)
            act.wait_ge(s["rsq_in"], 1)
            A.activation(nd["t0"], nd["t1"], ACT.Sqrt).then_inc(s["rsq_out"], 1)
            act.wait_ge(s["rsq_in"], 2)
            A.activation(nd["n"], nd["n2"], ACT.Sqrt).then_inc(s["rsq_out"], 1)
            act.wait_ge(s["ln_in"], 1)
            A.activation(nd["t1"], nd["t0"], ACT.Ln).then_inc(s["ln_out"], 1)

            act.wait_ge(s["wa_mm"], 1)
            A.copy(wx[:, :, F:HW], b_r[:, 0:KC * 2 * H].rearrange("p (k h) -> p k h", k=KC)).then_inc(s["wx_ready"], 1)
            A.copy(hbias[:, F:HW], b_r[:, 64:64 + 2 * H]).then_inc(s["wx_ready"], 1)

            def features(t, slot):
                act.wait_ge(s["tr_done"], plus(t, 1 + CREDIT))
                act.wait_ge(s["proj_mm"], plus(t, 1))
                act.wait_ge(s["fr_copied"], plus(t, 1))
                A.copy(fs[slot][:, :, :], bank[slot][:, 0:F].rearrange("p (k n) -> p k n", k=KC)).then_inc(s["fs_ready"], 1)
            with act.Fori(0, NT // 2) as i:
                for j in range(2):
                    features(plus(i * 2, j), j)
            features(NT - 1, 0)

            act.wait_ge(s["exs_in"], 1)
            A.activation(exs[:, :, :], exs[:, :, :], ACT.Exp, bias=negc[:, 0:1]).then_inc(s["exs_out"], 1)

            def z_copy(b, n):
                for c in range(MC):
                    act.wait_ge(s["z_mm"], plus(b * MC, c + 1))
                    A.copy(Z[:, c, cut(b * BLK, n)], bank[c % 3][:, 0:n]).then_inc(s["z_copied"], 1)
            with act.Fori(0, NB) as b:
                z_copy(b, BLK)
            z_copy(NB, P)
            act.wait_ge(s["rsq_in"], 3)
            A.activation(baff[:, 0, :], baff[:, 1, :], ACT.Sqrt).then_inc(s["rsq_out"], 1)

            act.wait_ge(s["baff_ready"], 1)

            def batch_norm(t, slot, free):
                if free is not None:
                    act.wait_ge(s["u_mm"], free)
                for c in range(MC):
                    ins = A.activation(TT[slot][:, c, :], Z[:, c, cut(t * P, P)], ACT.Relu,
                                       bias=baff[:, 1, c:c + 1], scale=baff[:, 0, c:c + 1])
                ins.then_inc(s["tt_ready"], 1)

            def squares(t, slot):
                act.wait_ge(s["o_tr"], plus(t, 1))
                act.wait_ge(s["no2_ready"], plus(t, 1))
                for m in range(3):
                    act.wait_ge(s["u_mm"], plus(t * 3, m + 2))
                    act.wait_ge(s["u_evac"], plus(t * 3, m + 2))
                    A.activation(U[slot][:, m, :], bank[m][:, :], ACT.Copy if m == 2 else ACT.Relu)
                    A.activation(spill[(slot * 3 + m) % 2], bank[m][:, :], ACT.Square, accum_out=sq3[slot][:, m:m + 1]).then_inc(s["u_evac"], 1)

            def epsilon(t, slot):
                act.wait_ge(s["fsq_ready"], plus(t, 1))
                A.activation(epsr[slot][:, 0:1], nd["fsq"][:, cut(t, 1)], ACT.Ln).then_inc(s["achain"], 1)
                act.wait_ge(s["achain"], plus(t * 2, 1))
                A.activation(epsr[slot][:, 1:2], epsr[slot][:, 0:1], ACT.Exp, scale=0.5, bias=lneps[:, 0:1]).then_inc(s["achain"], 1)
                act.wait_ge(s["achain"], plus(t * 2, 2))
                act.wait_ge(s["qk_ready"], plus(t, 1))
                A.activation(U[slot][:, 1, :], U[slot][:, 2, :], ACT.Identity, bias=epsr[slot][:, 1:2]).then_inc(s["eps_ready"], 1)

            def out_features(t, slot):
                act.wait_ge(s["o_ready"], plus(t, 1))
                A.activation(U[slot][:, 1, :], U[slot][:, 0, :], ACT.Square, accum_out=nd["no2"][:, cut(t, 1)]).then_inc(s["no2_ready"], 1)
                act.wait_ge(s["o_tr"], plus(t, 1 + CREDIT))
                act.wait_ge(s["r_mm"], plus(t, 1))
                A.copy(oT[:, :], b_o[:, :]).then_inc(s["oT_ready"], 1)

            def mixed_out(t):
                act.wait_ge(s["r_mm"], plus(t, 2))
                A.copy(mixed[:, cut(t, 1)].rearrange("p a c n -> p (a c) n"),
                       b_r[:, 0:F].rearrange("p (c n) -> p c n", c=KC)).then_inc(s["mixed_ready"], 1)

            def exponentials(g, slot, par):
                act.wait_ge(s["zl_ready"], plus(g, 1))
                A.activation(G[slot][:, :, F:F + H], zed[par][:, :, :], ACT.Exp, bias=negc[:, 0:1]).then_inc(s["exp_done"], 1)

            def targets(g, par, uses, edges):
                act.wait_ge(dstl[par], uses)
                act.wait_ge(s["win_ready"], plus(g, 1))
                A.activation(ohT[par][:, 0:edges], dstb[par][:, 0:edges], ACT.Abs, bias=negt[par][:, 0:1]).then_inc(s["diff"], 1)
                act.wait_ge(s["diff"], plus(g, 1))
                A.activation(ohT[par][:, 0:edges], ohT[par][:, 0:edges], ACT.Relu, scale=-1.0, bias=1.0).then_inc(s["ohT_ready"], 1)

            def unit(i, v, before=2, groups=GPT, last=False):
                t = plus(i * UNITS, v)
                g = t * GPT

                def next_targets(k):
                    final = isinstance(i, int) and i == PASSES - 1 and v == UNITS - 1
                    if final and k == 1:
                        return
                    targets(plus(g, k + 2), k, plus(i * 32, (GPT * v + k + 2) // 2 * 16 + 16), LASTE if final else EG)

                if groups:
                    if not last:
                        next_targets(0)
                        exponentials(plus(g, 1), (GPT * v + 1) % SLOTS, 1)
                if before >= 1:
                    epsilon(plus(t, -1), 1 - v)
                if groups:
                    squares(t, v)
                if groups and not last:
                    next_targets(1)
                    exponentials(plus(g, 2), (GPT * v + 2) % SLOTS, 0)
                    batch_norm(plus(t, 1), 1 - v, plus(t * 3, 1) if not isinstance(t, int) or t else None)
                if before >= 1:
                    out_features(plus(t, -1), 1 - v)
                if before >= 2:
                    mixed_out(plus(t, -2))

            act.preload_act_table_set("natural_log_exp_and_others")
            targets(0, 0, 16, EG)
            targets(1, 1, 16, EG)
            batch_norm(0, 0, None)
            exponentials(0, 0, 0)
            for v in range(UNITS):
                unit(0, v, before=v)
            with act.Fori(1, PASSES - 1) as i:
                for v in range(UNITS):
                    unit(i, v)
            for v in range(UNITS):
                unit(PASSES - 1, v)
            unit(PASSES, 0, last=True)
            unit(PASSES, 1, groups=0)
            mixed_out(NT - 1)

            act.wait_ge(s["rsq_in"], 4)
            A.activation(nd["t1"], nd["t0"], ACT.Sqrt).then_inc(s["rsq_out"], 1)

            def norms(t, j):
                act.wait_ge(s["ft_ready"], plus(t, 1))
                act.wait_ge(s["nf2_ready"], plus(t, 1))
                A.activation(junk[:, j * F:(j + 1) * F].rearrange("p (c n) -> p c n", c=KC), mixed[:, cut(t, 1)].rearrange("p a c n -> p (a c) n"),
                             ACT.Square, accum_out=nd["nf2"][:, cut(t, 1)]).then_inc(s["nf2_ready"], 1)
            with act.Fori(0, NT // TPB) as i:
                for j in range(TPB):
                    norms(plus(i * TPB, j), j % 2)
            norms(NT - 1, 0)
            act.wait_ge(s["th_in"], 1)
            A.activation(nd["n"], nd["t0"], ACT.Sqrt).then_inc(s["achain"], 1)
            act.wait_ge(s["achain"], 2 * NT + 1)
            A.activation(nd["t1"], nd["n"], ACT.Tanh).then_inc(s["th_out"], 1)
            act.wait_ge(s["faff_in"], 1)
            A.activation(ftmp[:, :, :], ftmp[:, :, :], ACT.Sqrt).then_inc(s["faff_out"], 1)
            act.wait_ge(s["rsq_in"], 5)
            A.activation(nd["t0"], nd["t1"], ACT.Sqrt).then_inc(s["rsq_out"], 1)

            def features2(t, slot):
                act.wait_ge(s["tr2_done"], plus(t, 1 + SLOTS))
                act.wait_ge(s["lg_mm"], plus(t, 1))
                act.wait_ge(s["frl_ready"], plus(t, 1))
                src = bank[slot][:, 0:F].rearrange("p (k n) -> p k n", k=KC)
                A.copy(fs2[slot][:, :, :], src).then_inc(s["fs2_ready"], 1)
                A.copy(FRH[:, :, cut(t * P, P)], src).then_inc(s["frh_ready"], 1)
            with act.Fori(0, NT // SLOTS) as i:
                for j in range(SLOTS):
                    features2(plus(i * SLOTS, j), j)
            features2(NT - 1, 0)
            act.wait_ge(s["sm_in"], 1)
            A.activation(gate[:, :, :], gate[:, :, :], ACT.Exp).then_inc(s["sm_out"], 1)
            act.wait_ge(s["gt_tr"], 1)
            A.copy(gT[:, 0:P], bank[4][:, 0:P])
            A.copy(gT[0:NT * NX - P, P:2 * P], bank[4][0:NT * NX - P, P:2 * P]).then_inc(s["gt_ready"], 1)

            def split_weights(e, slot, uses, free):
                act.wait_ge(w_raw[slot], uses)
                if free is not None:
                    act.wait_ge(s["y_mm"], free)
                A.copy(ew[:, slot, 0], raw[slot][:, :, :, :]).then_inc(s["w_hi"], 1)

            def hidden(n, s_, layer):
                cols, par = columns(s_), s_ % 2
                mm, done, hi, lo = (s[f"h{layer + 1}_{x}"] for x in ("mm", "r", "hi", "lo"))
                for m in range(KC):
                    act.wait_ge(mm, plus(n * KC, m + 1 + MM_CREDIT))
                    if m == 0:
                        act.wait_ge(lo, plus(n, 1))
                        act.wait_ge(hi, plus(n, 1))
                    norm = aff[s_ // STEPS % 2]
                    A.activation(hid[layer][:, m, 0:cols], bank[2 * layer + m][:, 0:cols], ACT.Relu, bias=norm[:, 2 * layer + 1, m:m + 1],
                                 scale=norm[:, 2 * layer, m:m + 1]).then_inc(done, 1)
                if layer == 0:
                    act.wait_ge(s["h2_mm"], plus(n * KC, 1 + MM_CREDIT - 2 * KC))
                else:
                    act.wait_ge(s["y_mm"], plus(n, 1))
                act.wait_ge(done, plus(n * KC, KC + CREDIT))
                A.copy(hidh[layer][par][:, :, 0:cols], hid[layer][:, :, 0:cols]).then_inc(hi, 1)

            def step(i, s_):
                if not (isinstance(i, int) and s_ >= 2 * STEPS - 1):
                    hidden(plus(i * (2 * STEPS), s_ + 1), s_ + 1, 0)
                hidden(plus(i * (2 * STEPS), s_), s_, 1)

            act.wait_ge(s["faff_out"], 2)
            act.wait_ge(s["asm_done"], SLOTS + NT)
            split_weights(0, 0, 48, None)
            hidden(0, 0, 0)
            step(0, 0)
            def steps(i, last):
                for s_ in range(1, 2 * STEPS + (not last)):
                    if s_ == SPLIT:
                        split_weights(plus(i * 2, 1), 1, plus(i * 48, 48), plus(i * (2 * STEPS), CREDIT))
                    if s_ == SPLIT + STEPS and not last:
                        split_weights(plus(i * 2, 2), 0, plus(i * 48, 96), plus(i * (2 * STEPS), STEPS + CREDIT))
                    step(i, s_)
            with act.Fori(0, NX // 2 - 1) as i:
                steps(i, False)
            steps(NX // 2 - 1, True)

        @block.tensor
        def _(pe):
            T = nc.tensor
            T.sem_inc(s["tr_done"], CREDIT)
            T.sem_inc(s["seg_ready"], 1)
            T.sem_inc(s["r_mm"], 1)
            T.sem_inc(s["u_mm"], 1)
            T.sem_inc(s["proj_mm"], CREDIT)
            T.sem_inc(s["o_tr"], CREDIT)
            T.sem_inc(s["tr2_done"], SLOTS)
            T.sem_inc(s["lg_mm"], SLOTS)
            T.sem_inc(s["y_mm"], CREDIT)
            T.sem_inc(s["h1_mm"], MM_CREDIT)
            T.sem_inc(s["h2_mm"], MM_CREDIT)

            pe.wait_ge(s["wa_ready"], 2)
            for k in range(KC):
                for c in range(KC):
                    T.matmul(b_r[:, k * 2 * H:(k + 1) * 2 * H], wT[:, c, k * P:(k + 1) * P], ablk[:, c, :], start=(c == 0), stop=(c == KC - 1))
            for c in range(KC):
                ins = T.matmul(b_r[:, 64:64 + 2 * H], bcolb[:, c, :], ablk[:, c, :], start=(c == 0), stop=(c == KC - 1))
            ins.then_inc(s["wa_mm"], 1)
            pe.wait_ge(s["idn"], 1)

            def turn(t, slot):
                pe.wait_ge(s["xs_ready"], plus(t, 1))
                if not (isinstance(t, int) and t < 2):
                    pe.wait_ge(s["fs_ready"], plus(t, -1))
                for c in range(KC):
                    ins = T.transpose(bank[slot][:, c * P:(c + 1) * P], xs[slot][:, c * P:(c + 1) * P], ident[:, :])
                ins.then_inc(s["tr_done"], 1)

            def project(t, slot):
                pe.wait_ge(s["fs_ready"], plus(t, 1))
                pe.wait_ge(s["hp_ready"], plus(t, 1))
                for c in range(KC):
                    ins = T.matmul(bank[2 + slot][:, 0:HW], fs[slot][:, c, :], wx[:, c, :], start=(c == 0), stop=(c == KC - 1))
                ins.then_inc(s["proj_mm"], 1)

            pe.wait_ge(s["wx_ready"], 2)
            turn(0, 0)
            turn(1, 1)
            with pe.Fori(0, NT // 2 - 1) as i:
                for j in range(2):
                    project(plus(i * 2, j), j)
                    turn(plus(i * 2, j + 2), j)
            for t in range(NT - 3, NT):
                project(t, t % 2)
                if t + 2 < NT:
                    turn(t + 2, t % 2)

            pe.wait_ge(s["cm_in"], 1)
            T.transpose(b_hte[0:2, 0:P], mx2[:, 0:2], ident[:, :]).then_inc(s["cm_tr"], 1)
            pe.wait_ge(s["cm_red"], 1)
            T.matmul(b_hte[:, 256:257], ones[0:2, :], mxr[:, :], start=True, stop=True).then_inc(s["cm_mm"], 1)

            pe.wait_ge(s["fr_copied"], NT + CREDIT)
            pe.wait_ge(s["hp_ready"], CREDIT + NT)

            def channels(b, n):
                for c in range(MC):
                    pe.wait_ge(s["z_copied"], plus(b * MC, c + 1))
                    for k in range(KC):
                        ins = T.matmul(bank[c % 3][:, 0:n], wqkv[:, k, c * P:(c + 1) * P], FR[:, k, cut(b * BLK, n)],
                                       start=(k == 0), stop=(k == KC - 1))
                    ins.then_inc(s["z_mm"], 1)
            with pe.Fori(0, NB) as b:
                channels(b, BLK)
            channels(NB, P)

            pe.wait_ge(s["z_copied"], 3 + (NB + 1) * MC)

            def u_rows(t, slot):
                pe.wait_ge(s["tt_ready"], plus(t, 1))
                for m in range(3):
                    pe.wait_ge(s["u_evac"], plus(t * 3, m + 1))
                    for h in range(2):
                        c = 2 * m + h
                        ins = T.matmul(bank[m][:, h * 256:(h + 1) * 256], TT[slot][:, c, :], ip[:, 0:c + 2:c + 1, :], start=True, stop=True)
                    ins.then_inc(s["u_mm"], 1)

            def out_features(t, slot):
                pe.wait_ge(s["o_ready"], plus(t, 1))
                pe.wait_ge(s["oT_ready"], plus(t, 1))
                for c in range(4):
                    ins = T.transpose(b_o[:, c * P:(c + 1) * P], U[slot][:, 0, c * P:(c + 1) * P], ident[:, :])
                ins.then_inc(s["o_tr"], 1)

            def mixed_out(t):
                pe.wait_ge(s["oT_ready"], plus(t, 2))
                pe.wait_ge(s["mixed_ready"], plus(t, 1))
                for c in range(4):
                    half, src = divmod(c, 2)
                    ins = T.matmul(b_r[:, 0:F], oT[:, c * P:(c + 1) * P], wres[:, 2 * src + half, :], start=(c == 0), stop=(c == 3))
                ins.then_inc(s["r_mm"], 1)

            turns_a = pe.alloc_register("pe_extra_a")
            turns_b = pe.alloc_register("pe_extra_b")
            pe.reg_mov(turns_a, 0)
            pe.reg_mov(turns_b, 0)

            def per_edge(par, first_col):
                for c in range(EC):
                    ins = T.matmul(b_hte[:, first_col + c * H:first_col + (c + 1) * H], ohT[par][:, c * P:(c + 1) * P], hsel[par][:, :],
                                   start=True, stop=True)
                return ins

            def targets(g, par):
                pe.wait_ge(s["ohT_ready"], plus(g, 1))
                if not (isinstance(g, int) and g == 0):
                    pe.wait_ge(s["zl_ready"], g)
                per_edge(par, 0).then_inc(s["hte_ready"], 1)

            def sums_of(slot, par):
                for c in range(EC):
                    ins = T.matmul(b_seg[par][:, 0:ACOLS], oh[par][:, c, :], G[slot][:, c, 0:ACOLS], start=(c == 0), stop=(c == EC - 1))
                return ins

            def more_targets(g, par):
                more = pe.value_load(tab[0:1, cut(g, 1), 1], min_val=0, max_val=NPAD // P)
                with pe.If(more > 0):
                    with pe.Fori(0, more) as w:
                        done = pe.snap(turns_a)
                        pe.wait_ge(s["xoT"], done + 1)
                        per_edge(par, 256).then_inc(s["xhte"], 1)
                        pe.reg_add(turns_a, turns_a, 1)

            def more_sums(g, slot, par):
                more = pe.value_load(tab[0:1, cut(g, 1), 1], min_val=0, max_val=NPAD // P)
                with pe.If(more > 0):
                    with pe.Fori(0, more) as w:
                        done = pe.snap(turns_b)
                        pe.wait_ge(s["xoh"], done + 1)
                        sums_of(slot, par).then_inc(s["xseg"], 1)
                        pe.reg_add(turns_b, turns_b, 1)

            def step(g, k, first=False, left=3):
                par = k % 2
                if left >= 1:
                    more_targets(plus(g, 1), 1 - par)
                if left >= 2:
                    targets(plus(g, 2), par)
                if not first:
                    more_sums(plus(g, -1), (k - 1) % SLOTS, 1 - par)
                pe.wait_ge(s["msg_ready"], plus(g, 1))
                pe.wait_ge(s["acc_done"], plus(g, 1))
                sums_of(k % SLOTS, par).then_inc(s["seg_ready"], 1)

            def unit(t, v, before=2, lefts=(3, 3)):
                g = t * GPT
                if before >= 2:
                    mixed_out(plus(t, -2))
                if lefts:
                    u_rows(t, v)
                    step(g, GPT * v, first=isinstance(t, int) and t == 0, left=lefts[0])
                if before >= 1:
                    out_features(plus(t, -1), 1 - v)
                if len(lefts) > 1:
                    step(plus(g, 1), GPT * v + 1, left=lefts[1])

            targets(0, 0)
            more_targets(0, 0)
            targets(1, 1)
            for v in range(UNITS):
                unit(v, v, before=v)
            with pe.Fori(1, PASSES - 1) as i:
                for v in range(UNITS):
                    unit(plus(i * UNITS, v), v)
            for t in range(NT - 1 - UNITS, NT - 1):
                unit(t, t % UNITS, lefts=(3, 3) if t < NT - 2 else (2, 1))
            unit(NT - 1, 0, lefts=(0,))
            more_sums(NG - 1, (NG - 1) % SLOTS, 0)
            unit(NT, 1, lefts=())
            mixed_out(NT - 1)

            def turn2(t, slot):
                pe.wait_ge(s["xs2_ready"], plus(t, 1))
                if not (isinstance(t, int) and t < SLOTS):
                    pe.wait_ge(s["frh_ready"], plus(t, 1 - SLOTS))
                for c in range(KC):
                    ins = T.transpose(bank[slot][:, c * P:(c + 1) * P], xs2[slot][:, c * P:(c + 1) * P], ident[:, :])
                ins.then_inc(s["tr2_done"], 1)

            def scores(t, slot):
                pe.wait_ge(s["fs2_ready"], plus(t, 1))
                pe.wait_ge(s["lg_done"], plus(t, 1))
                for c in range(KC):
                    ins = T.matmul(bank[SLOTS + slot][:, 0:NX], fs2[slot][:, c, :], wr[:, c, :], start=(c == 0), stop=(c == KC - 1))
                ins.then_inc(s["lg_mm"], 1)
            pe.wait_ge(s["ffn_v"], 48)
            for t in range(AHEAD):
                turn2(t, t)
            with pe.Fori(0, NT // SLOTS - 1) as i:
                for j in range(SLOTS):
                    scores(plus(i * SLOTS, j), j)
                    turn2(plus(i * SLOTS, j + AHEAD), (j + AHEAD) % SLOTS)
            for t in range((NT // SLOTS - 1) * SLOTS, NT):
                scores(t, t % SLOTS)
                if t + AHEAD < NT:
                    turn2(t + AHEAD, (t + AHEAD) % SLOTS)

            pe.wait_ge(s["gates"], 1)
            flat = gate[:, :, :].rearrange("p t e -> p (t e)")
            T.transpose(bank[4][:, 0:P], flat[:, 0:P], ident[:, :])
            T.transpose(bank[4][0:NT * NX - P, P:2 * P], flat[:, P:NT * NX], ident[:, :]).then_inc(s["gt_tr"], 1)
            pe.wait_ge(s["gt_ready"], 1)
            pe.wait_ge(s["bo_in"], 16 * (P // NX))
            for n, (t, tiles) in enumerate(PAIRS):
                row = t * NX % P // 32 * 32
                rows = min(32, NT * NX - t // TPB * 32)
                if n >= 4:
                    pe.wait_ge(s["x2b"], n - 3)
                c = t % TPB * F
                T.matmul(bank[4 + n % 4][:, 0:tiles * F], gT[row:row + rows, t * NX // P * P:(t * NX // P + 1) * P],
                         bo4[row:row + rows, c:c + tiles * F], start=True, stop=True).then_inc(s["bo_mm"], 1)

            def split_product(out_, lh, ll, rh, rl, k):
                T.matmul(out_, lh, rh, start=(k == 0), stop=False)
                T.matmul(out_, lh, rl, start=False, stop=False)
                return T.matmul(out_, ll, rh, start=False, stop=(k == KC - 1))

            def first(n, s_, e):
                b, cols, par = s_ % STEPS, columns(s_), s_ // STEPS % 2
                if b == 0:
                    pe.wait_ge(s["w_hi"], plus(e, 1))
                    pe.wait_ge(s["w_lo"], plus(e, 1))
                nodes_ = slice(first_tile_of(b) * P, first_tile_of(b) * P + cols)
                for m in range(KC):
                    pe.wait_ge(s["h1_r"], plus(n * KC, m + 1))
                    w = slice(m * P, (m + 1) * P)
                    for k in range(KC):
                        ins = split_product(bank[m][:, 0:cols], ew[:, par, 0, 0, k, w], ew[:, par, 1, 0, k, w],
                                            FRH[:, k, nodes_], FRL[:, k, nodes_], k)
                    ins.then_inc(s["h1_mm"], 1)

            def second(n, s_):
                cols, par, w_par = columns(s_), s_ % 2, s_ // STEPS % 2
                pe.wait_ge(s["h1_hi"], plus(n, 2))
                pe.wait_ge(s["h1_lo"], plus(n, 2))
                for m in range(KC):
                    pe.wait_ge(s["h2_r"], plus(n * KC, m + 1))
                    w = slice(m * P, (m + 1) * P)
                    for k in range(KC):
                        ins = split_product(bank[2 + m][:, 0:cols], ew[:, w_par, 0, 1, k, w], ew[:, w_par, 1, 1, k, w],
                                            hidh[0][par][:, k, 0:cols], hidl[0][par][:, k, 0:cols], k)
                    ins.then_inc(s["h2_mm"], 1)

            def third(n, s_):
                par, w_par = s_ % 2, s_ // STEPS % 2
                pe.wait_ge(s["h2_hi"], plus(n, 2))
                pe.wait_ge(s["h2_lo"], plus(n, 2))
                pe.wait_ge(s["y_add"], plus(n, 1))
                for j, nodes_, y in outputs_of(s_):
                    for k in range(KC):
                        ins = split_product(y, hidh[1][par][:, k, nodes_], hidl[1][par][:, k, nodes_], ew[:, w_par, 0, 2, k, :], ew[:, w_par, 1, 2, k, :], k)
                ins.then_inc(s["y_mm"], 1)

            pe.wait_ge(s["frh_ready"], NT)
            pe.wait_ge(s["frl_ready"], SLOTS + NT)
            pe.wait_ge(s["lg_done"], SLOTS + NT)
            first(0, 0, 0)
            first(1, 1, 0)
            second(0, 0)
            pe.wait_ge(s["x2b"], len(PAIRS))
            def steps(i, last):
                for s_ in range(1, 2 * STEPS + 1):
                    n = plus(i * (2 * STEPS), s_)
                    if not last or s_ + 1 < 2 * STEPS:
                        first(plus(n, 1), s_ + 1, plus(i * 2, (s_ + 1) // STEPS))
                    if not last or s_ < 2 * STEPS:
                        second(n, s_)
                    third(plus(n, -1), s_ - 1)
            with pe.Fori(0, NX // 2 - 1) as i:
                steps(i, False)
            steps(NX // 2 - 1, True)

        @block.vector
        def _(dve):
            V = nc.vector
            ch = Chain(dve, s["vchain"])
            link = ch.link
            V.sem_inc(s["g_free"], SLOTS)
            V.sem_inc(s["hp_ready"], CREDIT)
            V.sem_inc(s["y_add"], CREDIT)
            V.sem_inc(s["h1_lo"], 1)
            V.sem_inc(s["h2_lo"], 1)
            V.sem_inc(s["frl_ready"], SLOTS)
            V.sem_inc(s["dstb_free"], 2)
            V.sem_inc(s["acc_done"], CREDIT)
            V.sem_inc(s["asm_done"], SLOTS)
            V.sem_inc(s["lg_done"], SLOTS)

            def rsqrt(y, v, root, count):
                dve.wait_ge(s["rsq_out"], count)
                link(V.reciprocal(y, root))
                newton(y, v, root)

            def newton(y, v, tmp):
                link(V.tensor_tensor(tmp, y, y, ALU.mult))
                link(V.tensor_tensor(tmp, tmp, v, ALU.mult))
                link(V.tensor_scalar(tmp, tmp, -0.5, 1.5, ALU.mult, ALU.add))
                link(V.tensor_tensor(y, y, tmp, ALU.mult))

            def mean_and_variance():
                mean, var, d = mv[:, :, 0], mv[:, :, 1], nd["t2"]
                V.tensor_tensor(d, stats[:, :, 1], stats[:, :, 4], ALU.subtract)
                V.tensor_tensor(mean, stats[:, :, 1], stats[:, :, 4], ALU.add)
                link(V.tensor_tensor(var, stats[:, :, 2], stats[:, :, 5], ALU.add))
                V.tensor_tensor(d, d, d, ALU.mult)
                V.tensor_scalar(mean, mean, 0.5, None, ALU.mult)
                link(V.tensor_scalar(var, var, 1.0 / F, None, ALU.mult))
                link(V.scalar_tensor_tensor(out=var, in0=d, scalar=0.25, in1=var, op0=ALU.mult, op1=ALU.add))

            def row_stats(t):
                V.bn_stats(stats[:, cut(t, 1), :].rearrange("p a s -> p (a s)"), x_in[:, cut(t, 1), :].rearrange("p a f -> p (a f)")).then_inc(s["vchain"], 1)
            for n, part in enumerate(x_part):
                dve.wait_ge(part, 16)
                with dve.Fori(0, XT // 4) as i:
                    for j in range(4):
                        row_stats(plus(i * 4, n * XT + j))
            dve.wait_ge(s["x_in"], 16)
            row_stats(NT - 1)
            ch.n += NT
            dve.wait_ge(s["vchain"], NT)
            mean_and_variance()
            var = mv[:, :, 1]
            V.tensor_scalar(nd["t1"], var, LN_EPS, None, ALU.add).then_inc(s["rsq_in"], 1)
            rsqrt(nd["rstd"], nd["t1"], nd["t0"], 1)
            link(V.tensor_tensor(nd["t0"], nd["rstd"], nd["rstd"], ALU.mult))
            link(V.tensor_tensor(nd["t0"], nd["t0"], var, ALU.mult))
            link(V.tensor_scalar(nd["n2"], nd["t0"], float(F), MIN_NORM ** 2, ALU.mult, ALU.max))
            V.tensor_copy(nd["t2"], nd["n2"]).then_inc(s["rsq_in"], 1)
            dve.wait_ge(s["rsq_out"], 2)
            link(V.tensor_scalar(nd["t0"], nd["n"], MAXNORM, None, ALU.min))
            link(V.tensor_scalar(nd["t1"], nd["t0"], -1.0, 1.0, ALU.mult, ALU.add))
            link(V.tensor_scalar(nd["t0"], nd["t0"], 1.0, None, ALU.add))
            link(V.reciprocal(nd["scale"], nd["t1"]))
            V.tensor_tensor(nd["t0"], nd["t0"], nd["scale"], ALU.mult).then_inc(s["ln_in"], 1)
            dve.wait_ge(s["ln_out"], 1)
            link(V.reciprocal(nd["scale"], nd["n"]))
            link(V.tensor_scalar(nd["t1"], nd["t1"], 0.5, None, ALU.mult))
            link(V.tensor_tensor(nd["f0"], nd["t1"], nd["scale"], ALU.mult))
            link(V.tensor_scalar(nd["t2"], nd["n2"], 0.01, None, ALU.min))
            link(V.tensor_scalar(nd["t1"], nd["t2"], 1.0 / 9, 1.0 / 7, ALU.mult, ALU.add))
            for c in (1.0 / 5, 1.0 / 3, 1.0):
                link(V.tensor_tensor(nd["t1"], nd["t1"], nd["t2"], ALU.mult))
                link(V.tensor_scalar(nd["t1"], nd["t1"], c, None, ALU.add))
            link(V.tensor_scalar(nd["t0"], nd["n2"], 0.01, None, ALU.is_lt))
            link(V.tensor_tensor(nd["t1"], nd["t1"], nd["f0"], ALU.subtract))
            link(V.tensor_tensor(nd["t1"], nd["t1"], nd["t0"], ALU.mult))
            link(V.tensor_tensor(nd["f0"], nd["f0"], nd["t1"], ALU.add))
            link(V.reciprocal(nd["inv_f0"], nd["f0"]))
            link(V.tensor_tensor(nd["scale"], nd["rstd"], nd["f0"], ALU.mult))

            dve.wait_ge(s["weights"], 160)
            dve.wait_ge(s["consts"], 5)
            per_chunk = P // DH
            for c in range(KC):
                for q in range(per_chunk):
                    h = c * per_chunk + q
                    rows = slice(q * DH, (q + 1) * DH)
                    ins = V.tensor_copy(ablk[rows, c, h:h + H + 1:H], acol[rows, c:c + 3:2])
            link(ins)
            for c in range(KC):
                ins = V.tensor_scalar(bcolb[:, c, :], ones[:, :], bcol[:, c:c + 1], None, ALU.mult)
            ins.then_inc(s["wa_ready"], 2)
            for q in range(P // 32):
                rows = slice(q * 32, (q + 1) * 32)
                V.tensor_tensor(ip[rows, 1:MC + 1, q * 32:(q + 1) * 32], wpw[rows],
                                mixvec[rows, 2, :][:, :, None].broadcast_to([32, MC, 32]), ALU.mult)
            dve.wait_ge(s["idn"], 1)
            V.tensor_copy(row_f[:, :], row_i)
            link(V.tensor_copy(col_f[:, :], col_i[:, :]))
            V.memset(lneps[:, :], math.log(ATT_EPS / ATANH_MAX))

            dve.wait_ge(s["edges"], 16 * 9)
            V.tensor_copy(dst_f[:, :, :], dst_l[:, :, :])
            V.tensor_scalar(mod_l, dst_l, P - 1, None, ALU.bitwise_and)
            link(V.tensor_reduce(rng_i[:, 4:5], dst_rows, AX.X, ALU.max))
            link(V.tensor_reduce(rng_i[:, 2:3], dst_rows, AX.X, ALU.min))
            V.tensor_copy(mod_f[:, :, :], mod_l)
            V.tensor_scalar(rng_i[:, 3:4], rng_i[:, 2:3], P - 1, None, ALU.bitwise_and)
            V.tensor_scalar(rng_i[:, 0:1], rng_i[:, 2:3], TSHIFT, None, ALU.arith_shift_right)
            link(V.tensor_tensor(rng_i[:, 5:6], rng_i[:, 4:5], rng_i[:, 2:3], ALU.subtract))
            V.tensor_scalar(rng_i[:, 1:2], rng_i[:, 5:6], TSHIFT, None, ALU.arith_shift_right).then_inc(s["rng_ready"], 1)

            def window_key(out_, offset, column, order):
                order(V.scalar_tensor_tensor(out=out_, in0=offset, scalar=0.0, in1=column, op0=ALU.is_ge, op1=ALU.mult))
                order(V.scalar_tensor_tensor(out=out_, in0=offset, scalar=float(P), in1=out_, op0=ALU.is_lt, op1=ALU.mult))
                order(V.tensor_scalar(out_, out_, -1.0, None, ALU.add))

            def norm1(t, slot):
                dve.wait_ge(s["tr_done"], plus(t, 1))
                V.tensor_scalar(xs[slot], x_in[:, cut(t, 1), :].rearrange("p a f -> p (a f)"), mv[:, cut(t, 1), 0],
                                nd["scale"][:, cut(t, 1)], ALU.subtract, ALU.mult).then_inc(s["xs_ready"], 1)

            def project(t, slot, use):
                dve.wait_ge(s["proj_mm"], plus(t, 1 + CREDIT))
                dve.wait_ge(tout[slot], plus(use * 16, 16))
                V.scalar_tensor_tensor(out=hst[:, cut(t, 1), :].rearrange("p a f -> p (a f)"), in0=bank[2 + slot][:, F:HW],
                                       scalar=nd["inv_f0"][:, cut(t, 1)], in1=hbias[:, F:HW], op0=ALU.mult, op1=ALU.add)
                V.scalar_tensor_tensor(out=hp[slot][:, :], in0=bank[2 + slot][:, 0:HW],
                                       scalar=nd["inv_f0"][:, cut(t, 1)], in1=hbias[:, :], op0=ALU.mult, op1=ALU.add).then_inc(s["hp_ready"], 1)
            dve.wait_ge(s["wx_ready"], 2)
            norm1(0, 0)
            norm1(1, 1)
            with dve.Fori(0, NT // 2 - 1) as i:
                for j in range(2):
                    norm1(plus(i * 2, j + 2), j)
                    project(plus(i * 2, j), j, i)
            for t in range(NT - 3, NT):
                if t + 2 < NT:
                    norm1(t + 2, t % 2)
                project(t, t % 2, t // 2)
            dve.wait_ge(s["hp_ready"], CREDIT + NT)

            V.tensor_reduce(mx2[:, 0:1], hst[:, 0:NT, 0:H], AX.XY, ALU.max)
            link(V.tensor_reduce(mx2[:, 2:3], hst[:, 0:NT, H:2 * H], AX.XY, ALU.max))
            V.tensor_scalar(mx2[:, 1:2], mx2[:, 2:3], 0.0, None, ALU.max).then_inc(s["cm_in"], 1)
            dve.wait_ge(s["cm_tr"], 1)
            V.tensor_reduce(mxr[:, :], b_hte[0:2, 0:P], AX.X, ALU.max).then_inc(s["cm_red"], 1)
            dve.wait_ge(s["cm_mm"], 1)
            link(V.tensor_scalar(tiny[:, 0:1], b_hte[:, 256:257], SLOPE, None, ALU.mult))
            link(V.tensor_tensor(tiny[:, 1:2], tiny[:, 0:1], b_hte[:, 256:257], ALU.max))
            link(V.tensor_scalar(negc[:, :], tiny[:, 1:2], -1.0, None, ALU.mult))
            dve.wait_ge(s["rng_in"], 48)
            V.tensor_copy(firstm[:, :], firstm_i)
            link(V.tensor_copy(first_f[:, :], first_i))
            link(V.tensor_scalar(below[:, :], firstm[:, :], col_f[:, 0:1], None, ALU.is_gt))
            V.tensor_scalar(above[:, :], below[:, :], -1.0, 1.0, ALU.mult, ALU.add)
            link(V.tensor_tensor(target[:, :], first_f[:, :], firstm[:, :], ALU.subtract))
            link(V.tensor_scalar(target[:, :], target[:, :], col_f[:, 0:1], None, ALU.add))
            link(V.scalar_tensor_tensor(out=target[:, :], in0=below[:, :], scalar=float(P), in1=target[:, :], op0=ALU.mult, op1=ALU.add))
            link(V.tensor_tensor(dst_f[:, :, :], dst_f[:, :, :], first_f[:, :, None].broadcast_to([P, NG, EC]), ALU.subtract))
            link(V.tensor_scalar(mod_f[:, :, :], mod_f[:, :, :], 1.0, None, ALU.add))
            window_key(key[:, :, :], dst_f[:, :, :], mod_f[:, :, :], link)
            link(V.tensor_tensor(exs[:, :, :], hst[:, 0:NT, 0:H], hst[:, 0:NT, H:2 * H], ALU.add))
            V.scalar_tensor_tensor(out=exs[:, :, :], in0=exs[:, :, :], scalar=SLOPE, in1=exs[:, :, :], op0=ALU.mult, op1=ALU.max).then_inc(s["exs_in"], 1)
            link(V.memset(mxe[:, :, :], 0.0))
            link(V.memset(hst[:, NT, :], 0.0))

            def z_stats(b, n):
                for c in range(MC):
                    dve.wait_ge(s["z_copied"], plus(b * MC, c + 1 + 3))
                    V.bn_stats(bstats[:, c, cut(b, 1), :].rearrange("p a s -> p (a s)"), Z[:, c, cut(b * BLK, n)]).then_inc(s["z_stats"], 1)
            with dve.Fori(0, NB) as b:
                z_stats(b, BLK)
            z_stats(NB, LASTB)
            dve.wait_ge(s["z_stats"], (NB + 1) * MC)
            for c in range(MC):
                ins = V.bn_aggr(bmv[:, c, :], bstats[:, c, :, :].rearrange("p b s -> p (b s)"))
            link(ins)
            V.tensor_scalar(baff[:, 1, :], bmv[:, :, 1], BN_EPS, None, ALU.add).then_inc(s["rsq_in"], 1)
            rsqrt(tiny[:, 0:MC], baff[:, 1, :], baff[:, 0, :], 3)
            link(V.tensor_tensor(baff[:, 0, :], tiny[:, 0:MC], mixvec[:, 0, :], ALU.mult))
            link(V.tensor_tensor(tiny[:, 0:MC], baff[:, 0, :], bmv[:, :, 0], ALU.mult))
            V.tensor_tensor(baff[:, 1, :], mixvec[:, 1, :], tiny[:, 0:MC], ALU.subtract).then_inc(s["baff_ready"], 1)


            A2 = ATANH_MAX ** 2

            def factors(t, slot):
                u = U[slot]
                dve.wait_ge(s["u_evac"], plus(t * 3, 3 + 3))
                link(V.tensor_reduce(tiny[:, 0:1], sq3[slot][:, :], AX.X, ALU.add))
                V.tensor_scalar(nd["fsq"][:, cut(t, 1)], tiny[:, 0:1], A2, None, ALU.max).then_inc(s["fsq_ready"], 1)
                k3 = u[:, 1, :].rearrange("p (g d) -> p g d", d=32)
                q3 = u[:, 0, :].rearrange("p (g d) -> p g d", d=32)
                link(V.tensor_reduce(ksum[:, :], k3, AX.X, ALU.add))
                V.tensor_tensor(q3, q3, ksum[:, :, None].broadcast_to([P, 16, 32]), ALU.mult).then_inc(s["qk_ready"], 1)

            def outputs(t, slot):
                u = U[slot]
                dve.wait_ge(s["eps_ready"], plus(t, 1))
                link(V.reciprocal(u[:, 1, :], u[:, 1, :]))
                link(V.tensor_tensor(u[:, 1, :], u[:, 1, :], u[:, 2, :], ALU.mult))
                V.tensor_tensor(u[:, 0, :], u[:, 0, :], u[:, 1, :], ALU.mult).then_inc(s["o_ready"], 1)

            turns_a = dve.alloc_register("dve_extra_a")
            turns_b = dve.alloc_register("dve_extra_b")
            dve.reg_mov(turns_a, 0)
            dve.reg_mov(turns_b, 0)

            def first_tile(g):
                return dve.value_load(tab[0:1, cut(g, 1), 0], min_val=0, max_val=NT - 1)

            def later_windows(g):
                return dve.value_load(tab[0:1, cut(g, 1), 1], min_val=0, max_val=NPAD // P)

            def column(buf, g):
                return buf[:, cut(g, 1)]

            def drained(ins):
                dve.drain()

            def h_trg_of_window(g, par, tile, order):
                order(V.tensor_scalar(htmp[:, :], hst[:, bass.ds(tile + 1, 1), H:2 * H].rearrange("p a h -> p (a h)"), column(below, g), None, ALU.mult))
                return V.scalar_tensor_tensor(out=hsel[par][:, :], in0=hst[:, bass.ds(tile, 1), H:2 * H].rearrange("p a h -> p (a h)"),
                                              scalar=column(above, g), in1=htmp[:, :], op0=ALU.mult, op1=ALU.add)

            def window(g, par):
                tile = first_tile(g)
                if not (isinstance(g, int) and g == 0):
                    dve.wait_ge(s["win_ready"], g)
                V.tensor_scalar(htmp[:, :], hst[:, bass.ds(tile + 1, 1), H:2 * H].rearrange("p a h -> p (a h)"), column(below, g), None,
                                ALU.mult).then_inc(s["hsel_tmp"], 1)
                V.tensor_scalar(negt[par][:, :], column(target, g), -1.0, None, ALU.mult)
                dve.wait_ge(s["hsel_tmp"], plus(g, 1))
                V.scalar_tensor_tensor(out=hsel[par][:, :], in0=hst[:, bass.ds(tile, 1), H:2 * H].rearrange("p a h -> p (a h)"),
                                       scalar=column(above, g), in1=htmp[:, :], op0=ALU.mult, op1=ALU.add).then_inc(s["win_ready"], 1)

            def scores(g, slot, par, uses, here=None):
                z = zed[par][:, :, :]
                dve.wait_ge(gath[slot], uses)
                dve.wait_ge(s["hte_ready"], plus(g, 1))
                V.tensor_tensor(z, G[slot][:, :, F:F + H], b_hte[:, 0:EC * H].rearrange("p (c h) -> p c h", c=EC), ALU.add).then_inc(s["z_done"], 1)
                if here is not None:
                    onehot(oh[1 - par][:, :, :], of_group(key, here))
                more = later_windows(g)
                with dve.If(more > 0):
                    V.memset(dcur[:, 0:1], 0.0)
                    with dve.Fori(1, more + 1) as w:
                        done = dve.snap(turns_a)
                        tile = nc.s_assert_within(dve.snap(first_tile(g) + w), 0, NT - 1,
                                                  skip_runtime_bounds_check_because="a group's last window starts at or before its last target")
                        dve.drain()
                        V.tensor_scalar(dcur[:, 0:1], dcur[:, 0:1], float(P), None, ALU.add)
                        dve.drain()
                        V.tensor_tensor(dcur[:, 1:2], column(target, g), dcur[:, 0:1], ALU.add)
                        dve.drain()
                        V.tensor_scalar(ohT[par][:, :], dstb[par][:, :], dcur[:, 1:2], None, ALU.is_equal)
                        h_trg_of_window(g, par, tile, drained).then_inc(s["xoT"], 1)
                        dve.wait_ge(s["xhte"], done + 1)
                        V.tensor_tensor(z, z, b_hte[:, 256:256 + EC * H].rearrange("p (c h) -> p c h", c=EC), ALU.add)
                        dve.drain()
                        dve.reg_add(turns_a, turns_a, 1)
                dve.wait_ge(s["z_done"], plus(g, 1))
                V.scalar_tensor_tensor(out=z, in0=z, scalar=SLOPE, in1=z, op0=ALU.mult, op1=ALU.max).then_inc(s["zl_ready"], 1)
                V.sem_inc(s["dstb_free"], 1)

            def onehot(out_, keys):
                return V.tensor_tensor(out_, keys[:, :, None].broadcast_to([P, EC, P]), row_f[:, None, :].broadcast_to([P, EC, P]), ALU.is_equal)

            def of_group(buf, g):
                return buf[:, cut(g, 1), :].rearrange("p a c -> p (a c)")

            def messages(g, slot, par, parts):
                dve.wait_ge(s["exp_done"], plus(g, 1))
                for rows, cs in parts:
                    V.tensor_tensor(mxe[0:rows, cs, :], mxe[0:rows, cs, :], G[slot][0:rows, cs, F:F + H], ALU.max)
                m3 = G[slot][:, :, 0:F].rearrange("p c (h d) -> p c h d", h=H)
                V.tensor_tensor(m3, m3, G[slot][:, :, F:F + H][:, :, :, None].broadcast_to([P, EC, H, DH]), ALU.mult).then_inc(s["msg_ready"], 1)

            def accumulate(g, par, tile):
                for part, mask in ((tile, above), (tile + 1, below)):
                    rows = ACC[:, bass.ds(part, 1), :].rearrange("p a f -> p (a f)")
                    ins = V.scalar_tensor_tensor(out=rows, in0=b_seg[par][:, 0:ACOLS], scalar=column(mask, g), in1=rows, op0=ALU.mult, op1=ALU.add)
                return ins

            def collect(g, slot, par):
                tile, more = first_tile(g), later_windows(g)
                dve.wait_ge(s["acc_done"], plus(g, CREDIT))
                dve.wait_ge(s["seg_ready"], plus(g, 2))
                accumulate(g, par, tile).then_inc(s["acc_done"], 1)
                with dve.If(more > 0):
                    V.memset(dcur[:, 0:1], 0.0)
                    with dve.Fori(1, more + 1) as w:
                        done = dve.snap(turns_b)
                        later = nc.s_assert_within(dve.snap(tile + w), 0, NT - 1,
                                                   skip_runtime_bounds_check_because="a group's last window starts at or before its last target")
                        dve.drain()
                        V.tensor_scalar(dcur[:, 0:1], dcur[:, 0:1], float(P), None, ALU.add)
                        dve.drain()
                        V.tensor_scalar(xtmp[:, :], of_group(dst_f, g), dcur[:, 0:1], None, ALU.subtract)
                        dve.drain()
                        window_key(xkey[:, :], xtmp[:, :], of_group(mod_f, g), drained)
                        onehot(oh[par][:, :, :], xkey).then_inc(s["xoh"], 1)
                        dve.wait_ge(s["xseg"], done + 1)
                        accumulate(g, par, later)
                        dve.drain()
                        dve.reg_add(turns_b, turns_b, 1)
                V.sem_inc(s["g_free"], 1)

            rest, part = divmod(LASTE, P)

            def step(g, i, k, first=False, left=3):
                par = k % 2
                if left >= 2:
                    window(plus(g, 2), par)
                if left >= 1:
                    scores(plus(g, 1), (k + 1) % SLOTS, 1 - par, plus(i * (16 * EC), (k + 1) // SLOTS * (16 * EC) + 16 * EC), here=g)
                else:
                    onehot(oh[par][:, :, :], of_group(key, g))
                messages(g, k % SLOTS, par, [(P, slice(0, EC))] if left else [(P, slice(0, rest)), (part, slice(rest, rest + 1))])
                if not first:
                    collect(plus(g, -1), (k - 1) % SLOTS, 1 - par)

            def unit(i, v, before=2, lefts=(3, 3)):
                t = plus(i * UNITS, v)
                g = plus(i * SLOTS, GPT * v)
                first = isinstance(t, int) and t == 0
                step(g, i, GPT * v, first=first, left=lefts[0])
                if before >= 1:
                    outputs(plus(t, -1), 1 - v)
                if len(lefts) > 1:
                    step(plus(g, 1), i, GPT * v + 1, left=lefts[1])
                factors(t, v)

            window(0, 0)
            window(1, 1)
            scores(0, 0, 0, 16 * EC)
            dve.wait_ge(s["z_mm"], (NB + 1) * MC)
            link(V.memset(ACC[:, :, :], 0.0))
            for v in range(UNITS):
                unit(0, v, before=v)
            ch.enter()
            with dve.Fori(1, PASSES - 1) as i:
                ch.turn(i, 4 * UNITS, 1)
                for v in range(UNITS):
                    unit(i, v)
            ch.leave(PASSES - 2)
            for v in range(UNITS):
                unit(PASSES - 1, v, lefts=(3, 3) if v + 1 < UNITS else (2, 1))
            unit(PASSES, 0, lefts=(0,))
            collect(NG - 1, (NG - 1) % SLOTS, 0)
            outputs(NT - 1, 0)

            dve.wait_ge(s["exs_out"], 1)
            dve.drain()
            V.tensor_reduce(tiny[:, 0:1], mxe[:, :, :], AX.XY, ALU.max)
            V.tensor_reduce(tiny[:, 1:2], exs[:, 0:NT - 1, :], AX.XY, ALU.max)
            link(V.memset(tiny[:, 2:3], 0.0))
            link(V.tensor_reduce(tiny[0:LASTN, 2:3], exs[0:LASTN, NT - 1, :], AX.X, ALU.max))
            V.tensor_reduce(mx2[:, 0:1], tiny[:, 0:3], AX.X, ALU.max).then_inc(s["mx_in"], 1)

            def tile2(buf, t):
                return buf[:, cut(t, 1)].rearrange("p a c n -> p (a c) n")

            dve.wait_ge(s["no2_ready"], CREDIT + NT)
            V.tensor_scalar(nd["t0"], nd["no2"], MIN_NORM ** 2, None, ALU.max).then_inc(s["rsq_in"], 1)
            rsqrt(nd["rs"], nd["t0"], nd["t1"], 4)
            link(V.tensor_scalar(nd["rs"], nd["rs"], ATANH_MAX, None, ALU.mult))
            link(V.reciprocal(nd["fsq"], nd["fsq"]))
            link(V.tensor_scalar(nd["fsq"], nd["fsq"], A2, None, ALU.mult))
            link(V.tensor_tensor(nd["rs"], nd["rs"], nd["fsq"], ALU.min))
            dve.wait_ge(s["mixed_ready"], 1 + NT)

            def with_bias(t):
                m = tile2(mixed, t)
                V.scalar_tensor_tensor(out=m, in0=m, scalar=nd["rs"][:, cut(t, 1)], in1=bres[:, :].rearrange("p (c n) -> p c n", c=KC),
                                       op0=ALU.mult, op1=ALU.add).then_inc(s["ft_ready"], 1)
            with dve.Fori(0, NT // TPB) as i:
                for j in range(TPB):
                    with_bias(plus(i * TPB, j))
            with_bias(NT - 1)
            dve.wait_ge(s["nf2_ready"], CREDIT + NT)
            V.tensor_scalar(nd["t0"], nd["nf2"], MIN_NORM ** 2, None, ALU.max).then_inc(s["th_in"], 1)
            dve.wait_ge(s["th_out"], 1)
            link(V.reciprocal(nd["ff"], nd["n"]))
            link(V.tensor_scalar(nd["t1"], nd["t1"], MAXNORM, None, ALU.min))
            link(V.tensor_tensor(nd["ff"], nd["ff"], nd["t1"], ALU.mult))

            dve.wait_ge(s["ffn_v"], 48)
            v_ = fvec[:, 4:10:5, :]
            V.tensor_scalar(ftmp[:, :, :], v_, FBN_EPS, None, ALU.add).then_inc(s["faff_in"], 1)
            link(V.tensor_scalar(fvec[:, 4:10:5, :], v_, FBN_EPS, None, ALU.add))
            dve.wait_ge(s["faff_out"], 1)
            scale_, bias_ = faff[:, 0:4:2, :], faff[:, 1:4:2, :]
            link(V.reciprocal(scale_, ftmp[:, :, :]))
            newton(scale_, v_, ftmp[:, :, :])
            link(V.tensor_tensor(scale_, scale_, fvec[:, 1:10:5, :], ALU.mult))
            link(V.tensor_tensor(bias_, fvec[:, 0:10:5, :], fvec[:, 3:10:5, :], ALU.subtract))
            link(V.tensor_tensor(bias_, bias_, scale_, ALU.mult))
            V.tensor_tensor(bias_, bias_, fvec[:, 2:10:5, :], ALU.add).then_inc(s["faff_out"], 1)

            dve.wait_ge(s["mx_all"], 1)
            link(V.tensor_scalar(guard[:, :], mx2[:, 1:2], GAT_EPS, 1e-37, ALU.mult, ALU.max))
            winv = gate
            link(V.tensor_tensor(winv[:, :, :], ACC[:, 0:NT, F:ACOLS], exs[:, :, :], ALU.add))
            link(V.tensor_scalar(winv[:, :, :], winv[:, :, :], guard[:, 0:1], None, ALU.add))
            link(V.reciprocal(winv[:, :, :], winv[:, :, :]))

            def attention(t):
                dve.wait_ge(s["self_done"], plus(t, 1 + SLOTS))
                y = ACC[:, cut(t, 1), 0:F].rearrange("p a (h d) -> p (a h) d", h=H)
                w = winv[:, cut(t, 1), :].rearrange("p a h -> p (a h)")
                V.tensor_tensor(y, y, w[:, :, None].broadcast_to([P, H, DH]), ALU.mult).then_inc(s["weighed"], 1)

            def with_mixing(t):
                dve.wait_ge(s["weighed"], plus(t, 1))
                m = tile2(mixed, t)
                V.scalar_tensor_tensor(out=m, in0=m, scalar=nd["ff"][:, cut(t, 1)], in1=ACC[:, cut(t, 1), 0:F].rearrange("p a (c n) -> p (a c) n", c=KC),
                                       op0=ALU.mult, op1=ALU.add).then_inc(s["with_mix"], 1)

            def residual(t, slot, uses):
                dve.wait_ge(s["with_mix"], plus(t, 1))
                dve.wait_ge(x_back[slot], uses)
                m = tile2(mixed, t)
                V.tensor_tensor(m, m, xr[slot].rearrange("p (c n) -> p c n", c=KC), ALU.add).then_inc(s["asm_done"], 1)

            def statistics(t):
                dve.wait_ge(s["asm_done"], plus(t, 1 + SLOTS))
                V.bn_stats(stats[:, cut(t, 1), :].rearrange("p a s -> p (a s)"), tile2(mixed, t)).then_inc(s["x2_ready"], 1)

            def assemble(i, j):
                t = plus(i * SLOTS, j)
                known = isinstance(t, int)
                if not known or t < NT:
                    attention(t)
                if not known or 1 <= t < NT + 1:
                    with_mixing(plus(t, -1))
                if not known or 2 <= t < NT + 2:
                    residual(plus(t, -2), (j - 2) % SLOTS, plus(i * 16, 16 if j >= 2 else 0))
                if not known or t >= 3:
                    statistics(plus(t, -3))
            for j in range(SLOTS):
                assemble(0, j)
            with dve.Fori(1, NT // SLOTS) as i:
                for j in range(SLOTS):
                    assemble(i, j)
            for j in range(SLOTS):
                assemble(NT // SLOTS, j)
            dve.wait_ge(s["x2_ready"], NT)
            mean_and_variance()
            V.tensor_scalar(nd["t1"], mv[:, :, 1], LN_EPS, None, ALU.add).then_inc(s["rsq_in"], 1)
            rsqrt(nd["rstd"], nd["t1"], nd["t0"], 5)

            def norm2(t, slot):
                dve.wait_ge(s["tr2_done"], plus(t, 1))
                V.tensor_scalar(xs2[slot].rearrange("p (c n) -> p c n", c=KC), tile2(mixed, t), mv[:, cut(t, 1), 0],
                                nd["rstd"][:, cut(t, 1)], ALU.subtract, ALU.mult).then_inc(s["xs2_ready"], 1)

            def rest_rows(t, slot):
                dve.wait_ge(s["frh_ready"], plus(t, 1))
                rows = cut(t * P, P)
                V.tensor_tensor(FRL[:, :, rows], fs2[slot][:, :, :], FRH[:, :, rows].bitcast(F32), ALU.subtract).then_inc(s["frl_ready"], 1)

            def gate_rows(t, slot):
                dve.wait_ge(s["lg_mm"], plus(t, 1 + SLOTS))
                V.tensor_tensor(gate[:, cut(t, 1), :].rearrange("p a e -> p (a e)"), bank[SLOTS + slot][:, 0:NX], brb[:, :], ALU.add).then_inc(s["lg_done"], 1)
            for t in range(AHEAD):
                norm2(t, t)
            with dve.Fori(0, NT // SLOTS - 1) as i:
                for j in range(SLOTS):
                    norm2(plus(i * SLOTS, j + AHEAD), (j + AHEAD) % SLOTS)
                    rest_rows(plus(i * SLOTS, j), j)
                    gate_rows(plus(i * SLOTS, j), j)
            for t in range((NT // SLOTS - 1) * SLOTS, NT):
                if t + AHEAD < NT:
                    norm2(t + AHEAD, (t + AHEAD) % SLOTS)
                rest_rows(t, t % SLOTS)
                gate_rows(t, t % SLOTS)
            dve.wait_ge(s["lg_done"], SLOTS + NT)
            g3 = gred[:, :, None].broadcast_to([P, NT, NX])
            link(V.tensor_reduce(gred[:, :], gate[:, :, :], AX.X, ALU.max))
            V.tensor_tensor(gate[:, :, :], gate[:, :, :], g3, ALU.subtract).then_inc(s["sm_in"], 1)
            dve.wait_ge(s["sm_out"], 1)
            link(V.tensor_reduce(gred[:, :], gate[:, :, :], AX.X, ALU.add))
            link(V.reciprocal(gred[:, :], gred[:, :]))
            V.tensor_tensor(gate[:, :, :], gate[:, :, :], g3, ALU.mult).then_inc(s["gates"], 1)

            for n, (t, tiles) in enumerate(PAIRS):
                dve.wait_ge(s["bo_mm"], n + 1)
                m = mixed[:, t:t + tiles]
                V.tensor_tensor(m, m, bank[4 + n % 4][:, 0:tiles * F].rearrange("p (t c n) -> p t c n", t=tiles, c=KC), ALU.add).then_inc(s["x2b"], 1)

            def split_weights(e, slot):
                dve.wait_ge(s["w_hi"], plus(e, 1))
                V.tensor_copy(aff[slot][:, :, :], faff[:, :, cut(e * KC, KC)])
                V.tensor_tensor(ew[:, slot, 1], raw[slot][:, :, :, :], ew[:, slot, 0].bitcast(F32), ALU.subtract).then_inc(s["w_lo"], 1)

            def rest_of(n, s_, layer):
                cols, par = columns(s_), s_ % 2
                dve.wait_ge(s[f"h{layer + 1}_hi"], plus(n, 2))
                V.tensor_tensor(hidl[layer][par][:, :, 0:cols], hid[layer][:, :, 0:cols], hidh[layer][par][:, :, 0:cols].bitcast(F32),
                                ALU.subtract).then_inc(s[f"h{layer + 1}_lo"], 1)

            def add_outputs(n, s_, e):
                dve.wait_ge(s["y_mm"], plus(n, 1 + CREDIT))
                dve.wait_ge(s["y_add"], plus(n, CREDIT))
                for j, nodes_, y in outputs_of(s_):
                    t = first_tile_of(s_) + j
                    rows = nodes_.stop - nodes_.start
                    m = mixed[0:rows, t]
                    ins = V.scalar_tensor_tensor(out=m, in0=y.rearrange("p (c n) -> p c n", c=KC), scalar=gate[0:rows, t, cut(e, 1)], in1=m,
                                                 op0=ALU.mult, op1=ALU.add)
                ins.then_inc(s["y_add"], 1)

            split_weights(0, 0)
            rest_of(0, 0, 0)
            rest_of(1, 1, 0)
            rest_of(0, 0, 1)
            dve.wait_ge(s["x2b"], len(PAIRS))
            def steps(i, last):
                for s_ in range(1, 2 * STEPS + 1):
                    n = plus(i * (2 * STEPS), s_)
                    if s_ == SPLIT:
                        split_weights(plus(i * 2, 1), 1)
                    if s_ == SPLIT + STEPS and not last:
                        split_weights(plus(i * 2, 2), 0)
                    if not last or s_ + 1 < 2 * STEPS:
                        rest_of(plus(n, 1), s_ + 1, 0)
                    if not last or s_ < 2 * STEPS:
                        rest_of(n, s_, 1)
                    add_outputs(plus(n, -1), s_ - 1, plus(i * 2, (s_ - 1) // STEPS))
            with dve.Fori(0, NX // 2 - 1) as i:
                steps(i, False)
            steps(NX // 2 - 1, True)


def _layout(i):
    def g(name):
        return np.asarray(i[name])

    def cols(v):
        return v.reshape(NX, KC, P).transpose(2, 0, 1).reshape(P, NX * KC)

    def chunked(v):
        return v.reshape((2, 4, 3, 32) + v.shape[1:]).swapaxes(1, 2).swapaxes(0, 1)

    def per_partition(v):
        return chunked(v).reshape(MC, P).T

    whole = (NG - 1) * EG
    tail = {k + "_t": g(k)[whole:whole + LASTE // P * P].reshape(LASTE // P, P).T for k in ("src", "dst")}
    arrays = {
        **tail,
        "x": g("x"), "src": g("src"), "dst": g("dst"),
        "src_l": g("src")[:whole].reshape(NG - 1, EC, P).transpose(2, 0, 1),
        "dst_l": g("dst")[:whole].reshape(NG - 1, EC, P).transpose(2, 0, 1),
        "W": g("L0_gnn_W"), "WT": g("L0_gnn_W").T, "b": g("L0_gnn_b"), "bcol": g("L0_gnn_b").reshape(KC, P).T,
        "acol": np.concatenate([g("L0_gnn_a_src").reshape(KC, P).T, g("L0_gnn_a_trg").reshape(KC, P).T], axis=1),
        "wqkv": chunked(g("L0_mix_w_qkv")[:, :, 2]).reshape(C2, F).T,
        "wpw": g("L0_mix_w_pw")[:, :, 0].reshape(2, 4, 3, 32, 32).transpose(1, 4, 2, 0, 3).reshape(P, MC, 32),
        "mixvec": np.stack([per_partition(g("L0_mix_bn_gamma")), per_partition(g("L0_mix_bn_beta")),
                            per_partition(g("L0_mix_w_dw")[:, 0, 2])], axis=1),
        "wres": g("L0_mix_w_res")[:, :, 0].T, "b_res": g("L0_mix_b_res"),
        "fvec": np.stack([cols(g("L0_ffn_" + n)) for n in ("b1", "g1", "be1", "m1", "v1", "b2", "g2", "be2", "m2", "v2")], axis=1),
        "W1": g("L0_ffn_W1"), "W2": g("L0_ffn_W2"), "Wo": g("L0_ffn_Wo"),
        "Wr": g("L0_ffn_Wr"), "br": g("L0_ffn_br"), "bo": g("L0_ffn_bo"),
    }
    return {k: np.ascontiguousarray(v) for k, v in arrays.items()}


def kernel(**inputs):
    import concourse.bacc as bacc
    from concourse.bass_utils import run_bass_kernel_spmd

    nc = bacc.Bacc("TRN2", target_bir_lowering=False, num_devices=1)
    arrays = _layout(inputs)
    args = {k: nc.dram_tensor(f"in_{k}", v.shape, mybir.dt.from_np(v.dtype), kind="ExternalInput").ap() for k, v in arrays.items()}
    out = nc.dram_tensor("out", (N, F), F32, kind="ExternalOutput").ap()
    program(nc, args, out)
    r = run_bass_kernel_spmd(nc, [{f"in_{k}": v for k, v in arrays.items()}], core_ids=[0])
    return r.results[0]["out"]
```
